# Optimizing a Trainium2 kernel written in Bass

```python
import numpy as np
import jax
import jax.numpy as jnp

def _softmax(x, axis=-1):
    return jax.nn.softmax(x, axis=axis)

def _gelu(x):
    return jax.nn.gelu(x, approximate=True)

def _silu(x):
    return jax.nn.silu(x)

def _sigmoid(x):
    return jax.nn.sigmoid(x)

def _layernorm(x, axis=-1, eps=1e-05):
    m = jnp.mean(x, axis=axis, keepdims=True)
    v = jnp.var(x, axis=axis, keepdims=True)
    return (x - m) / jnp.sqrt(v + eps)

def _scatter_add(tgt, idx, src, axis=0):
    return tgt.at[idx].add(src)

def _segment_sum(src, seg, n):
    return jax.ops.segment_sum(src, seg, n)
kernel_name = 'mk_gnn_preln_d2_gnn_r32_3d8029'

def setup_inputs(seed: int=0):
    np.random.seed(seed)
    _w = jnp.asarray

    def _rec_inputs():
        import jax
        import jax.numpy as jnp
        _gk = jax.random.key(seed)
        x = -0.0003713 + 1 * jax.random.normal(jax.random.fold_in(_gk, 1), (50000, 256), jnp.float32)
        src = jax.random.randint(jax.random.fold_in(_gk, 2), (25000,), 0, 50000, jnp.int32)
        dst = jnp.minimum((50000 * jax.random.uniform(jax.random.fold_in(_gk, 3), (25000,)) ** 2.0).astype(jnp.int32), 49999)
        _o = jnp.argsort(dst, stable=True)
        src = src[_o]
        dst = dst[_o]
        return (x, src, dst)
    x, src, dst = _rec_inputs()

    def _L0_gnn_setup():
        import jax, jax.numpy as jnp
        import numpy as np
        HEAD = 8
        D = 128
        GIN = 256
        GOUT = 256
        N = 50000
        E = 25000

        def gt_layer(edge_index, embeds, qT, kT, vT, ln_s, ln_b):
            rows, cols = (edge_index[0], edge_index[1])
            n, d = embeds.shape
            hd = d // HEAD
            rowE = embeds[rows]
            colE = embeds[cols]
            q = (rowE @ qT).reshape(-1, HEAD, hd)
            k = (colE @ kT).reshape(-1, HEAD, hd)
            v = (colE @ vT).reshape(-1, HEAD, hd)
            att = jnp.clip(jnp.einsum('ehd,ehd->eh', q, k), -10.0, 10.0)
            expAtt = jnp.exp(att)
            attNorm = jax.ops.segment_sum(expAtt, rows, num_segments=n)[rows]
            att = expAtt / (attNorm + 1e-08)
            res = (att[..., None] * v).reshape(-1, d)
            agg = jax.ops.segment_sum(res, rows, num_segments=n)
            out = agg + embeds
            mu = jnp.mean(out, axis=-1, keepdims=True)
            var = jnp.mean((out - mu) ** 2, axis=-1, keepdims=True)
            return (out - mu) / jnp.sqrt(var + 1e-06) * ln_s + ln_b
        key = jax.random.key(seed)
        ks = jax.random.split(key, 16)

        def xavier(k, shape):
            lim = np.sqrt(6.0 / (shape[0] + shape[1]))
            return jax.random.uniform(k, shape, jnp.float32, -lim, lim)
        inp = {'x': jax.random.normal(ks[0], (N, GIN), jnp.float32), 'edge_index': jax.random.randint(ks[1], (2, E), 0, N, jnp.int64), 'W_P_w': xavier(ks[2], (GIN, D)), 'W_P_b': jnp.zeros((D,), jnp.float32), 'W_pos': jax.random.uniform(ks[3], (1, D), jnp.float32, -0.02, 0.02), 'q1': xavier(ks[4], (D, D)), 'k1': xavier(ks[5], (D, D)), 'v1': xavier(ks[6], (D, D)), 'ln1_s': jnp.ones((D,), jnp.float32), 'ln1_b': jnp.zeros((D,), jnp.float32), 'q2': xavier(ks[7], (D, D)), 'k2': xavier(ks[8], (D, D)), 'v2': xavier(ks[9], (D, D)), 'ln2_s': jnp.ones((D,), jnp.float32), 'ln2_b': jnp.zeros((D,), jnp.float32), 'inv_w': xavier(ks[10], (D, GOUT)), 'inv_b': jnp.zeros((GOUT,), jnp.float32)}
        return inp
    _L0_gnn_all = _L0_gnn_setup()
    _L0_gnn_in = {k: v for k, v in _L0_gnn_all.items() if k in ('W_P_w', 'W_P_b', 'W_pos', 'q1', 'k1', 'v1', 'ln1_s', 'ln1_b', 'q2', 'k2', 'v2', 'ln2_s', 'ln2_b', 'inv_w', 'inv_b')}
    del _L0_gnn_all

    def _L1_gnn_setup():
        import jax, jax.numpy as jnp
        import numpy as np
        EPS = 1e-12

        def l2_normalize_rows(x):
            nrm = jnp.sqrt(jnp.sum(x * x, axis=1, keepdims=True))
            return x / jnp.maximum(nrm, EPS)
        key = jax.random.key(seed)
        k1, k2, k3, k4 = jax.random.split(key, 4)
        n, din, dout, E = (3125, 256, 256, 50000)
        x = jax.random.normal(k1, (n, din), dtype=jnp.float32)
        edge_index = jax.random.randint(k2, (2, E), 0, n, dtype=jnp.int64)
        s = float(np.sqrt(6.0 / (din + dout)))
        W_gcn = jax.random.uniform(k3, (din, dout), jnp.float32, -s, s)
        b_gcn = jnp.zeros((dout,), jnp.float32)
        W_V = jax.random.uniform(k4, (din, dout), jnp.float32, -s, s)
        return {'x': x, 'edge_index': edge_index, 'W_gcn': W_gcn, 'b_gcn': b_gcn, 'W_V': W_V}
    _L1_gnn_all = _L1_gnn_setup()
    _L1_gnn_in = {k: v for k, v in _L1_gnn_all.items() if k in ('W_gcn', 'b_gcn', 'W_V')}
    del _L1_gnn_all
    return {'x': x, 'src': src, 'dst': dst, 'L0_gnn_W_P_w': _L0_gnn_in['W_P_w'], 'L0_gnn_W_P_b': _L0_gnn_in['W_P_b'], 'L0_gnn_W_pos': _L0_gnn_in['W_pos'], 'L0_gnn_q1': _L0_gnn_in['q1'], 'L0_gnn_k1': _L0_gnn_in['k1'], 'L0_gnn_v1': _L0_gnn_in['v1'], 'L0_gnn_ln1_s': _L0_gnn_in['ln1_s'], 'L0_gnn_ln1_b': _L0_gnn_in['ln1_b'], 'L0_gnn_q2': _L0_gnn_in['q2'], 'L0_gnn_k2': _L0_gnn_in['k2'], 'L0_gnn_v2': _L0_gnn_in['v2'], 'L0_gnn_ln2_s': _L0_gnn_in['ln2_s'], 'L0_gnn_ln2_b': _L0_gnn_in['ln2_b'], 'L0_gnn_inv_w': _L0_gnn_in['inv_w'], 'L0_gnn_inv_b': _L0_gnn_in['inv_b'], 'L1_gnn_W_gcn': _L1_gnn_in['W_gcn'], 'L1_gnn_b_gcn': _L1_gnn_in['b_gcn'], 'L1_gnn_W_V': _L1_gnn_in['W_V']}

def reference(x, src, dst, L0_gnn_W_P_w, L0_gnn_W_P_b, L0_gnn_W_pos, L0_gnn_q1, L0_gnn_k1, L0_gnn_v1, L0_gnn_ln1_s, L0_gnn_ln1_b, L0_gnn_q2, L0_gnn_k2, L0_gnn_v2, L0_gnn_ln2_s, L0_gnn_ln2_b, L0_gnn_inv_w, L0_gnn_inv_b, L1_gnn_W_gcn, L1_gnn_b_gcn, L1_gnn_W_V):
    import jax
    import jax.numpy as jnp

    def _L0_gnn_ref(x, edge_index, W_P_w, W_P_b, W_pos, q1, k1, v1, ln1_s, ln1_b, q2, k2, v2, ln2_s, ln2_b, inv_w, inv_b):
        import jax, jax.numpy as jnp
        import numpy as np
        HEAD = 8
        D = 128
        GIN = 256
        GOUT = 256
        N = 50000
        E = 25000

        def gt_layer(edge_index, embeds, qT, kT, vT, ln_s, ln_b):
            rows, cols = (edge_index[0], edge_index[1])
            n, d = embeds.shape
            hd = d // HEAD
            rowE = embeds[rows]
            colE = embeds[cols]
            q = (rowE @ qT).reshape(-1, HEAD, hd)
            k = (colE @ kT).reshape(-1, HEAD, hd)
            v = (colE @ vT).reshape(-1, HEAD, hd)
            att = jnp.clip(jnp.einsum('ehd,ehd->eh', q, k), -10.0, 10.0)
            expAtt = jnp.exp(att)
            attNorm = jax.ops.segment_sum(expAtt, rows, num_segments=n)[rows]
            att = expAtt / (attNorm + 1e-08)
            res = (att[..., None] * v).reshape(-1, d)
            agg = jax.ops.segment_sum(res, rows, num_segments=n)
            out = agg + embeds
            mu = jnp.mean(out, axis=-1, keepdims=True)
            var = jnp.mean((out - mu) ** 2, axis=-1, keepdims=True)
            return (out - mu) / jnp.sqrt(var + 1e-06) * ln_s + ln_b
        z = x @ W_P_w + W_P_b
        embeds = z + W_pos
        embeds = gt_layer(edge_index, embeds, q1, k1, v1, ln1_s, ln1_b)
        embeds = gt_layer(edge_index, embeds, q2, k2, v2, ln2_s, ln2_b)
        return embeds @ inv_w + inv_b

    def _L1_gnn_ref(x, edge_index, W_gcn, b_gcn, W_V):
        import jax, jax.numpy as jnp
        import numpy as np
        EPS = 1e-12

        def l2_normalize_rows(x):
            nrm = jnp.sqrt(jnp.sum(x * x, axis=1, keepdims=True))
            return x / jnp.maximum(nrm, EPS)
        n = x.shape[0]
        beta = 0.1
        H = l2_normalize_rows(x)
        XW = H @ W_gcn
        loop = jnp.arange(n, dtype=edge_index.dtype)
        src = jnp.concatenate([edge_index[0], loop])
        dst = jnp.concatenate([edge_index[1], loop])
        deg = jax.ops.segment_sum(jnp.ones_like(dst, dtype=XW.dtype), dst, num_segments=n)
        dinv = jax.lax.rsqrt(jnp.maximum(deg, 1e-30))
        norm = dinv[src] * dinv[dst]
        msg = XW[src] * norm[:, None]
        z_local = jax.ops.segment_sum(msg, dst, num_segments=n) + b_gcn
        HtH = H.T @ H
        z_global = beta / n * (H @ HtH @ W_V)
        out = jax.nn.relu(z_local + z_global)
        return l2_normalize_rows(out)
    edge_index = jnp.stack([src, dst])
    h = jnp.maximum(_layernorm(x, axis=-1), 0.0)
    x = x + _L0_gnn_ref(h, edge_index, L0_gnn_W_P_w, L0_gnn_W_P_b, L0_gnn_W_pos, L0_gnn_q1, L0_gnn_k1, L0_gnn_v1, L0_gnn_ln1_s, L0_gnn_ln1_b, L0_gnn_q2, L0_gnn_k2, L0_gnn_v2, L0_gnn_ln2_s, L0_gnn_ln2_b, L0_gnn_inv_w, L0_gnn_inv_b)
    h = jnp.maximum(_layernorm(x, axis=-1), 0.0)
    x = x + _L1_gnn_ref(h, edge_index, L1_gnn_W_gcn, L1_gnn_b_gcn, L1_gnn_W_V)
    return x

_drawn_inputs = setup_inputs


def setup_inputs(seed=0):
    import zlib

    import numpy as np

    out = dict(_drawn_inputs(seed))
    spreads = {'L0_gnn_W_P_b': (0.0, 0.1),
     'L0_gnn_ln1_s': (1.0, 0.2),
     'L0_gnn_ln1_b': (0.0, 0.1),
     'L0_gnn_ln2_s': (1.0, 0.2),
     'L0_gnn_ln2_b': (0.0, 0.1),
     'L0_gnn_inv_b': (0.0, 0.1),
     'L1_gnn_b_gcn': (0.0, 0.1)}
    factors = {'L0_gnn_W_pos': 5.813, 'L1_gnn_W_V': 8.0}
    for name, (base, spread) in spreads.items():
        noise = np.random.default_rng([zlib.crc32(name.encode()), seed]).standard_normal(out[name].shape)
        drawn = base * np.exp(spread * noise) if base else spread * noise
        out[name] = jnp.asarray(drawn.astype(out[name].dtype))
    for name, factor in factors.items():
        out[name] = (out[name] * factor).astype(out[name].dtype)
    return out
```

```python
from contextlib import ExitStack

import concourse.bass as bass
from concourse import mybir

ALU = mybir.AluOpType
ACT = mybir.ActivationFunctionType
AX_X = mybir.AxisListType.X
F32 = mybir.dt.float32
BF16 = mybir.dt.bfloat16
I32 = mybir.dt.int32

P = 128
QUAD = 96
N = 50000
E = 25000
W = 256
D = 128
HEADS = 8
HD = D // HEADS
NT = -(-E // P)
EP = NT * P
HT = NT // 2
ET = 4
EG = NT // ET
G = 3
NG = N // (G * P)
TAIL = N - NG * G * P
DIG = 256
KEYS = DIG * DIG
EW = D + 4
XW = W + 8
LIST = EP + P
SKIP = 100000.0
EPS_X = 1e-5
EPS_E = 1e-6
EPS_ATT = 1e-8
EPS_L2 = 1e-12
BETA = 0.1
assert TAIL <= P and NT % (2 * ET) == ET and N <= KEYS


def need(eng, sem, count):
    if isinstance(count, int) and count <= 0:
        return
    eng.wait_ge(sem, count)


def pace(eng, passed, sem, count):
    if isinstance(count, int) and count <= 0:
        return
    eng.wait_ge(sem, count)
    eng.sem_inc(passed, 1)


def dma_count(g, slot, slots, per=16):
    return (g - slot) * (per // slots) + per


def phase_sems(nc, ctx, suffix=""):
    held = []

    def close():
        nc.clear_and_free_semaphores(held)
        nc.all_engine_barrier()

    def sem(name):
        held.append(nc.alloc_semaphore(name + suffix))
        return held[-1]

    ctx.callback(close)
    return sem


def run_steps(eng, step, total, lo, hi, unroll):
    assert (hi - lo) % unroll == 0
    for s in range(lo):
        step(s, s % unroll)
    with eng.Fori(lo, hi - unroll + 1, unroll) as i:
        for u in range(unroll):
            step(i + u, (lo + u) % unroll)
    for s in range(hi, total):
        step(s, s % unroll)


def program(nc, x, src, dst, W_P_w, W_P_b, W_pos, q1, k1, v1, ln1_s, ln1_b, q2, k2, v2, ln2_s,
            ln2_b, inv_w, inv_b, W_gcn, b_gcn, W_V, out):
    def dram(name, shape, dt=F32):
        return nc.dram_tensor(name, shape, dt, kind="Internal").ap()

    t = {
        "E0": dram("embed0", [N, EW]), "E1": dram("embed1", [N, EW]), "X2": dram("x2_rows", [N, XW]),
        "SORTED": dram("sorted_pairs", [2 * LIST, 2], I32),
        "DIGROW": dram("key_rows", [2, 2, EP]), "KEYROW": dram("sorted_key_rows", [2, EP]),
        "AUX": dram("node_aux", [2, KEYS]),
        "x": x, "src": src, "dst": dst, "out": out,
    }
    with ExitStack() as ctx:
        def sb(name, shape, dt=F32):
            return ctx.enter_context(nc.sbuf_tensor(name, shape, dt))

        c = {}
        for name, shape in (("ident", [P, P]), ("ones", [P, P]), ("wP", [P, 2, D]), ("bias0", [P, D]),
                            ("qkv1", [P, 3, D]), ("qkv2", [P, 3, D]), ("ln1s", [P, D]), ("ln1b", [P, D]),
                            ("w2", [P, W]), ("bias2", [P, W]), ("wg", [P, 2, W]), ("bg", [P, W]),
                            ("wv", [P, 2, W]), ("hth", [P, 2, W]), ("eps", [P, 2]), ("e127", [P, 1])):
            c[name] = sb(name, shape)
        c["posI"] = sb("posI", [P, 2 * NT], I32)
        c["pairs"] = sb("pairs", [P, 2 * NT, 2], I32)
        c["ek"] = sb("ek", [P, 3, 2, NT])
        c["fin"] = sb("fin", [P, 2, NT])
        for name in ("keyI", "otherI", "finI"):
            c[name] = sb(name, [P, 2, NT], I32)
        weights(nc, c, W_P_w, W_P_b, W_pos, q1, k1, v1, ln1_s, ln1_b, q2, k2, v2, ln2_s, ln2_b,
                inv_w, inv_b, W_gcn, b_gcn, W_V)
        rank_edges(nc, c, t)
        dense_embed(nc, c, t)
        unpack_lists(nc, c, t)
        edge_attention(nc, c, t, 1)
        edge_attention(nc, c, t, 2)
        dense_gcn(nc, c, t)
        edge_gcn(nc, c, t)


def weights(nc, c, W_P_w, W_P_b, W_pos, q1, k1, v1, ln1_s, ln1_b, q2, k2, v2, ln2_s, ln2_b,
            inv_w, inv_b, W_gcn, b_gcn, W_V):
    with ExitStack() as ctx:
        def sb(name, shape, dt=F32):
            return ctx.enter_context(nc.sbuf_tensor(name, shape, dt))

        sem = phase_sems(nc, ctx)

        pos_b = sb("pos_b", [P, D])
        ln2s_col = sb("ln2s_col", [P, 1])
        ln2b_col = sb("ln2b_col", [P, 1])
        ln2b_all = sb("ln2b_all", [P, P])
        invb = sb("invb", [P, W])
        ps_bias = ctx.enter_context(nc.psum_tensor("ps_bias", [P, W], F32))
        loaded = sem("weights_loaded")
        ones_set = sem("ones_set")
        ident_set = sem("ident_set")
        col_spread = sem("ln2b_spread")
        bias_mm = sem("bias_mm")
        done = sem("weights_done")
        row = lambda a: a.partition_broadcast(P)
        loads = [
            (c["wP"][:, :, :], W_P_w.rearrange("(h p) n -> p h n", p=P)),
            (c["wg"][:, :, :], W_gcn.rearrange("(h p) n -> p h n", p=P)),
            (c["wv"][:, :, :], W_V.rearrange("(h p) n -> p h n", p=P)),
            (c["w2"][:, :], inv_w), (ln2s_col[:, :], ln2_s.rearrange("(p a) -> p a", a=1)),
            (ln2b_col[:, :], ln2_b.rearrange("(p a) -> p a", a=1)),
            (c["bias0"][:, :], row(W_P_b)), (pos_b[:, :], row(W_pos[0])),
            (c["ln1s"][:, :], row(ln1_s)), (c["ln1b"][:, :], row(ln1_b)),
            (invb[:, :], row(inv_b)), (c["bg"][:, :], row(b_gcn)),
        ]
        for name, ws in (("qkv1", (q1, k1, v1)), ("qkv2", (q2, k2, v2))):
            loads += [(c[name][:, i, :], w) for i, w in enumerate(ws)]
        block = ctx.enter_context(nc.Block())

        @block.sync
        def _(sp):
            for o, i in loads:
                sp.dma_start(o, i).then_inc(loaded, 16)

        @block.gpsimd
        def _(pool):
            pool.memset(c["ones"][:, :], 1.0).then_inc(ones_set, 1)
            pool.memset(c["eps"][:, 0:1], EPS_X)
            pool.memset(c["eps"][:, 1:2], EPS_E)
            pool.wait_ge(ones_set, 1)
            pool.affine_select(out=c["ident"][:, :], in_=c["ones"][:, :], compare_op=ALU.is_equal, fill=0.0,
                               base=0, pattern=[[1, P]], channel_multiplier=-1)
            pool.affine_select(out=c["e127"][:, :], in_=c["ones"][:, 0:1], compare_op=ALU.is_equal, fill=0.0,
                               base=1 - P, pattern=[[0, 1]], channel_multiplier=1).then_inc(ident_set, 1)

        @block.vector
        def _(dve):
            dve.wait_ge(loaded, 16 * len(loads))
            dve.wait_ge(ones_set, 1)
            dve.tensor_scalar(ln2b_all[:, :], c["ones"][:, :], ln2b_col[:, :], None, ALU.mult).then_inc(col_spread, 1)
            dve.tensor_tensor(c["bias0"][:, :], c["bias0"][:, :], pos_b[:, :], ALU.add)
            dve.wait_ge(bias_mm, 1)
            dve.tensor_tensor(c["bias2"][:, :], ps_bias[:, :], invb[:, :], ALU.add)
            dve.tensor_scalar(c["w2"][:, :], c["w2"][:, :], ln2s_col[:, :], None, ALU.mult).then_inc(done, 1)

        @block.tensor
        def _(pe):
            pe.wait_ge(col_spread, 1)
            pe.matmul(ps_bias[:, :], ln2b_all[:, :], c["w2"][:, :], start=True, stop=True).then_inc(bias_mm, 1)


def rank_edges(nc, c, t):
    with ExitStack() as ctx:
        def sb(name, shape, dt=F32):
            return ctx.enter_context(nc.sbuf_tensor(name, shape, dt))

        def ps(name, shape):
            return ctx.enter_context(nc.psum_tensor(name, shape, F32))

        sem = phase_sems(nc, ctx)

        keyT = sb("keyT", [HT, 2, 2, P], I32)
        digT = sb("digT", [HT, 2, 2, 2, P], I32)
        keyTF = sb("keyTF", [HT, 3, 2, 2, P])
        ke = sb("ke", [P, 3, 2, NT])
        iota = sb("iota_digit", [P, DIG], BF16)
        pcol = sb("pcol", [P, 2])
        below = sb("below", [P, P])
        earlier = sb("earlier", [P, ET * P])
        oh = sb("onehot", [P, 2 * ET, 2, DIG], BF16)
        cnt = sb("cnt", [P, 2, 2, DIG])
        inc = sb("inc", [P, 2, 2, DIG])
        onesw = sb("onesw", [P, DIG])
        aux = sb("aux_out", [P, 2, 2, DIG])
        base = sb("base", [P, 4])
        start = sb("start", [P, 2, 2, DIG])
        seen = sb("seen", [P, 2, 2, DIG])
        krow = sb("krow", [P, 2, ET * P])
        hrow = sb("hrow", [P, 2, ET * P])
        ohT = sb("onehotT", [P, 2, 2, ET * P])
        dupj = sb("dup_junk", [P, ET, ET * P])
        selj = sb("sel_junk", [P, ET, DIG])
        dup = sb("dup", [P, ET])
        sel = sb("sel", [P, ET])
        pos = sb("pos", [P, 2 * NT])
        sentinel = sb("sentinel", [2, 2], I32)
        hist = [ps(f"hist{i}", [P, 512]) for i in range(4)]
        rows = ps("rows", [P, ET, DIG])
        runs = [ps(f"runs{i}", [P, 512]) for i in range(2)]

        padded = sem("keys_padded")
        loaded = sem("keys_loaded")
        digits = sem("digits")
        floats = sem("floats")
        rows_stored = sem("key_rows_stored")
        consts = sem("rank_consts")
        turned = sem("keys_turned")
        ke_ready = sem("ke_ready")
        oh_ready = sem("onehot_ready")
        oh_used = sem("onehot_used")
        cnt_ready = sem("cnt_ready")
        aux_ready = sem("aux_ready")
        aux_root = sem("aux_root")
        aux_stored = sem("aux_stored")
        scanned = sem("scanned")
        base_mm = sem("base_mm")
        base_ready = sem("base_ready")
        start_ready = sem("start_ready")
        krow_loaded = [sem(f"krow_loaded{i}") for i in range(2)]
        sp_passed = sem("rank_sp_passed")
        ohT_ready = sem("onehotT_ready")
        dup_ready = sem("dup_ready")
        rows_ready = sem("rows_ready")
        sel_ready = sem("sel_ready")
        oh2_ready = sem("onehot2_ready")
        run_ready = sem("run_ready")
        seen_ready = sem("seen_ready")
        pos_ready = sem("pos_ready")
        block = ctx.enter_context(nc.Block())

        def rank_steps(eng, step, l):
            for b in range(l * EG, l * EG + 3):
                step(b, b, l)
            with eng.Fori(l * EG + 3, (l + 1) * EG - 1, 2) as i:
                for u in range(2):
                    step(i + u, l * EG + 3 + u, l)

        @block.sync
        def _(sp):
            sp.wait_ge(padded, 1)
            full = (NT - 1) * P
            for l, a in enumerate((t["src"], t["dst"])):
                sp.dma_start(keyT[:, l, 0, :], a[0:HT * P].rearrange("(r c) -> r c", c=P)).then_inc(loaded, 16)
                sp.dma_start(keyT[0:HT - 1, l, 1, :], a[HT * P:full].rearrange("(r c) -> r c", c=P)).then_inc(loaded, 16)
                sp.dma_start(keyT[HT - 1:HT, l, 1, 0:E - full], a[full:E].rearrange("(r c) -> r c", r=1)).then_inc(loaded, 16)
            sp.wait_ge(floats, 2)
            for kind in range(2):
                for l in range(2):
                    sp.dma_start(t["DIGROW"][kind, l].rearrange("(a r c) -> r a c", a=2, c=P),
                                 keyTF[:, kind, l, :, :]).then_inc(rows_stored, 16)
            for l in range(2):
                sp.dma_start(t["SORTED"][l * LIST + EP:l * LIST + EP + 2, :], sentinel[:, :]).then_inc(rows_stored, 16)
            sp.wait_ge(rows_stored, 96)

            def step(b, m, l):
                pace(sp, sp_passed, dup_ready, b - 1)
                off = (b - l * EG) * (ET * P)
                for tile, kind in ((krow, 0), (hrow, 1)):
                    sp.dma_start(tile[:, m % 2, :], t["DIGROW"][kind, l, bass.ds(off, ET * P)].partition_broadcast(P)
                                 ).then_inc(krow_loaded[m % 2], 16)

            step(0, 0, 0)
            step(1, 1, 0)
            for l in range(2):
                if l == 1:
                    step(EG, EG, 1)
                    step(EG + 1, EG + 1, 1)
                lo = l * EG + 2
                with sp.Fori(lo, (l + 1) * EG - 2, 2) as i:
                    for u in range(2):
                        step(i + u, lo + u, l)
                step((l + 1) * EG - 1, (l + 1) * EG - 1, l)
            sp.wait_ge(aux_ready, 2)
            for k in range(2):
                sp.dma_start(t["AUX"][k].rearrange("(h p l) -> p h l", h=2, l=DIG), aux[:, k, :, :]).then_inc(aux_stored, 16)
            sp.wait_ge(aux_stored, 32)

        @block.gpsimd
        def _(pool):
            pool.iota(iota[:, :], [[1, DIG]], base=0, channel_multiplier=0, allow_small_or_imprecise_dtypes=True)
            for h in range(2):
                pool.iota(pcol[:, h:h + 1], [[0, 1]], base=h * P, channel_multiplier=1,
                          allow_small_or_imprecise_dtypes=True)
            pool.memset(onesw[:, :], 1.0)
            pool.memset(earlier[:, 0:(ET - 1) * P], 1.0)
            pool.affine_select(out=below[:, :], in_=c["ones"][:, :], compare_op=ALU.is_gt, fill=0.0,
                               base=0, pattern=[[1, P]], channel_multiplier=-1)
            pool.affine_select(out=earlier[:, (ET - 1) * P:], in_=c["ones"][:, :], compare_op=ALU.is_gt, fill=0.0,
                               base=0, pattern=[[-1, P]], channel_multiplier=1).then_inc(consts, 1)

        @block.vector
        def _(dve):
            dve.memset(sentinel[:, :], 2 * N)
            dve.memset(keyT[:, :, :, :], N).then_inc(padded, 1)
            dve.wait_ge(loaded, 96)
            dve.tensor_scalar(digT[:, 0, :, :, :], keyT[:, :, :, :], 8, None, ALU.logical_shift_right)
            dve.tensor_scalar(digT[:, 1, :, :, :], keyT[:, :, :, :], 255, None, ALU.bitwise_and).then_inc(digits, 1)
            dve.tensor_copy(keyTF[:, 0, :, :, :], keyT[:, :, :, :]).then_inc(floats, 1)
            dve.wait_ge(digits, 1)
            dve.tensor_copy(keyTF[:, 1, :, :, :], digT[:, 0, :, :, :]).then_inc(floats, 1)
            dve.tensor_copy(keyTF[:, 2, :, :, :], digT[:, 1, :, :, :]).then_inc(floats, 1)
            dve.wait_ge(ke_ready, 3)
            for copy in range(2):
                for l in range(2):
                    dve.tensor_copy(c["pairs"][:, copy * NT:(copy + 1) * NT, l], ke[:, 0, l, :])
            dve.wait_ge(consts, 1)

            def onehots(tile, j, l, ready):
                for d in range(2):
                    o = dve.tensor_scalar(oh[:, j, d, :], iota[:, :], ke[:, 1 + d, l, bass.ds(tile, 1)], None, ALU.is_equal)
                o.then_inc(ready, 1)

            def count_tiles(base_tile, l, first):
                for j in range(ET):
                    n = base_tile + j + l * NT
                    if not first:
                        need(dve, oh_used, n + 1 - ET)
                    onehots(base_tile + j, j, l, oh_ready)

            for l in range(2):
                count_tiles(0, l, l == 0)
                with dve.Fori(ET, NT - 2 * ET + 1, ET) as i:
                    count_tiles(i, l, False)
                count_tiles(NT - ET, l, False)

            dve.wait_ge(oh_used, 2 * NT)
            for l in range(2):
                for h in range(2):
                    o = dve.tensor_copy(cnt[:, l, h, :], hist[2 * l + h][:, 0:DIG])
            o.then_inc(cnt_ready, 1)
            dve.wait_ge(cnt_ready, 1)
            dve.tensor_scalar(aux[:, 0, :, :], cnt[:, 0, :, :], 0.0, None, ALU.is_equal).then_inc(aux_ready, 1)
            dve.tensor_scalar(aux[:, 1, :, :], cnt[:, 1, :, :], 1.0, 1e-30, ALU.add, ALU.max).then_inc(aux_root, 1)
            for l in range(2):
                for h in range(2):
                    o = dve.tensor_tensor_scan(inc[:, l, h, :], onesw[:, :], cnt[:, l, h, :], 0.0, ALU.mult, ALU.add)
            o.then_inc(scanned, 1)
            dve.wait_ge(aux_root, 2)
            dve.reciprocal(aux[:, 1, :, :], aux[:, 1, :, :]).then_inc(aux_ready, 1)
            dve.wait_ge(base_mm, 1)
            dve.tensor_copy(base[:, :], rows[:, 0, 0:4]).then_inc(base_ready, 1)
            dve.wait_ge(base_ready, 1)
            dve.wait_ge(scanned, 1)
            for l in range(2):
                for h in range(2):
                    o = dve.scalar_tensor_tensor(out=start[:, l, h, :], in0=inc[:, l, h, :],
                                                 scalar=base[:, 2 * l + h:2 * l + h + 1], in1=cnt[:, l, h, :],
                                                 op0=ALU.add, op1=ALU.subtract)
            o.then_inc(start_ready, 1)

            def step(b, m, l):
                slot = m % 2
                tile = (b - l * EG) * ET
                dve.wait_ge(krow_loaded[slot], dma_count(b, slot, 2, 32))
                need(dve, rows_ready, b - 1)
                for h in range(2):
                    o = dve.tensor_scalar(ohT[:, slot, h, :], hrow[:, slot, :], pcol[:, h:h + 1], None, ALU.is_equal)
                o.then_inc(ohT_ready, 1)
                need(dve, run_ready, b - 1)
                for j in range(ET):
                    onehots(tile + j, slot * ET + j, l, oh2_ready)
                need(dve, pos_ready, b)
                for j in range(ET):
                    w = (j + 1) * P
                    o = dve.scalar_tensor_tensor(out=dupj[:, j, 0:w], in0=krow[:, slot, 0:w],
                                                 scalar=ke[:, 0, l, bass.ds(tile + j, 1)],
                                                 in1=earlier[:, (ET - 1 - j) * P:], op0=ALU.is_equal,
                                                 op1=ALU.mult, accum_out=dup[:, j:j + 1])
                o.then_inc(dup_ready, 1)
                need(dve, rows_ready, b + 1)
                need(dve, oh2_ready, (b + 1) * ET)
                for j in range(ET):
                    o = dve.tensor_tensor_reduce(out=selj[:, j, :], in0=rows[:, j, :], in1=oh[:, slot * ET + j, 1, :],
                                                 scale=1.0, scalar=0.0, op0=ALU.mult, op1=ALU.add,
                                                 accum_out=sel[:, j:j + 1])
                o.then_inc(sel_ready, 1)
                need(dve, sel_ready, b + 1)
                need(dve, dup_ready, b + 1)
                dve.tensor_tensor(pos[:, bass.ds(b * ET, ET)], sel[:, :], dup[:, :], ALU.add).then_inc(pos_ready, 1)

            dve.wait_ge(start_ready, 1)
            for l in range(2):
                rank_steps(dve, step, l)
            dve.wait_ge(pos_ready, 2 * EG)
            dve.tensor_copy(c["posI"][:, 0:NT], pos[:, 0:NT])
            dve.tensor_scalar(c["posI"][:, NT:], pos[:, NT:], float(LIST), None, ALU.add)

        @block.scalar
        def _(act):
            for kind in range(3):
                act.wait_ge(turned, kind + 1)
                nc.scalar.copy(ke[:, kind, :, :].rearrange("p l t -> p (l t)"), hist[kind][:, 0:2 * NT]).then_inc(ke_ready, 1)
            act.wait_ge(aux_root, 1)
            nc.scalar.activation(aux[:, 1, :, :], aux[:, 1, :, :], ACT.Sqrt).then_inc(aux_root, 1)

            def step(b, m, l):
                need(act, run_ready, b + 1)
                need(act, rows_ready, b)
                for h in range(2):
                    o = nc.scalar.copy(seen[:, (m + 1) % 2, h, :], runs[h][:, 0:DIG])
                o.then_inc(seen_ready, 1)

            for l in range(2):
                rank_steps(act, step, l)

        @block.tensor
        def _(pe):
            for kind in range(3):
                pe.wait_ge(floats, kind + 1)
                for l in range(2):
                    for a in range(2):
                        at = (l * 2 + a) * HT
                        o = pe.transpose(hist[kind][:, at:at + HT], keyTF[:, kind, l, a, :], c["ident"][0:HT, 0:HT])
                o.then_inc(turned, 1)
            pe.wait_ge(ke_ready, 3)

            def count(base_tile, l, first, last):
                for j in range(ET):
                    n = base_tile + j + l * NT
                    need(pe, oh_ready, n + 1)
                    for h in range(2):
                        o = pe.matmul(hist[2 * l + h][:, 0:DIG], oh[:, j, 0, h * P:(h + 1) * P], oh[:, j, 1, :],
                                      start=first and j == 0, stop=last and j == ET - 1)
                    o.then_inc(oh_used, 1)

            for l in range(2):
                count(0, l, True, False)
                with pe.Fori(ET, NT - 2 * ET + 1, ET) as i:
                    count(i, l, False, False)
                count(NT - ET, l, False, True)
            pe.wait_ge(scanned, 1)
            pe.wait_ge(consts, 1)
            for l in range(2):
                pe.matmul(rows[:, 0, 2 * l:2 * l + 1], below[:, :], inc[:, l, 0, DIG - 1:DIG], start=True, stop=True)
                pe.matmul(rows[:, 0, 2 * l + 1:2 * l + 2], below[:, :], inc[:, l, 1, DIG - 1:DIG], start=True, stop=False)
                o = pe.matmul(rows[:, 0, 2 * l + 1:2 * l + 2], c["ones"][:, :], inc[:, l, 0, DIG - 1:DIG],
                              start=False, stop=True)
            o.then_inc(base_mm, 1)
            pe.wait_ge(start_ready, 1)

            def step(b, m, l):
                slot = m % 2
                first = m == l * EG
                need(pe, ohT_ready, b + 1)
                need(pe, seen_ready, b)
                need(pe, sel_ready, b)
                table = start[:, l, :, :] if first else seen[:, slot, :, :]
                for j in range(ET):
                    for h in range(2):
                        o = pe.matmul(rows[:, j, :], ohT[:, slot, h, j * P:(j + 1) * P], table[:, h, :],
                                      start=(h == 0 and j % 2 == 0), stop=(h == 1), skip_group_check=True)
                o.then_inc(rows_ready, 1)
                need(pe, oh2_ready, (b + 1) * ET)
                for h in range(2):
                    if first:
                        pe.matmul(runs[h][:, 0:DIG], c["ident"][:, :], start[:, l, h, :], start=True, stop=False,
                                  skip_group_check=True)
                    for j in range(ET):
                        o = pe.matmul(runs[h][:, 0:DIG], oh[:, slot * ET + j, 0, h * P:(h + 1) * P],
                                      oh[:, slot * ET + j, 1, :], start=False, stop=j == ET - 1, skip_group_check=True)
                o.then_inc(run_ready, 1)

            for l in range(2):
                rank_steps(pe, step, l)


def spread(row, p, n, w):
    return row[0:p, :].unsqueeze(1).to_broadcast([p, n, w])


def dense_embed(nc, c, t):
    UN = 8
    LO, SCATTER_LO, SCATTER_HI, HI = 8, 4, 96, 128
    A, B, C, M, X, H, T = range(7)
    STEPS = NG + 1 + T
    with ExitStack() as ctx:
        def sb(name, shape, dt=F32):
            return ctx.enter_context(nc.sbuf_tensor(name, shape, dt))

        def ps(name, shape):
            return ctx.enter_context(nc.psum_tensor(name, shape, F32))

        sem = phase_sems(nc, ctx)

        xt = sb("xt", [P, UN, G, W])
        h0 = sb("h0", [P, 2, G, W])
        hT = sb("hT", [P, 2, G, 2, P])
        e0 = sb("e0", [P, 2, G, EW])
        e1 = sb("e1", [P, 2, G, EW])
        n1 = sb("n1", [P, 2, G, D])
        n2 = sb("n2", [P, 2, G, D])
        n2T = sb("n2T", [P, 2, G, P])
        x2 = sb("x2", [P, 4, G, XW])
        r = sb("r", [P, 2, G, W])
        rsq = sb("rsq", [P, G, W])
        rw = sb("rw", [P, 2, G, W])
        SX, SX2, SE0, SE1 = range(4)
        st = sb("st", [P, 4, G, 6])
        mv = sb("mv", [P, 2, 4, G, 2])
        std = sb("std", [P, 2, 4, G])
        rstd = sb("rstd", [P, 2, 4, G])
        nb = sb("nb", [P, 2, 4, G])
        ss = sb("ss", [P, 2, G])
        nrm = sb("nrm", [P, 2, G])
        inv = sb("inv", [P, 2, G])
        w1 = sb("w1", [P, 2, G])
        aux = sb("aux", [P, 2, (NG + 1) * G])
        idx = sb("scatter_idx", [P, 4, ET], I32)
        pay = sb("scatter_pairs", [P, 4, ET, 2], I32)
        ps_h = ps("ps_h", [P, 4, 2, P])
        ps_z = ps("ps_z", [P, 4, D])
        ps_n = ps("ps_n", [P, 4, D])
        ps_x = ps("ps_x", [P, 4, W])
        ps_hth = ps("ps_hth", [P, 2, W])

        x_loaded = [sem(f"x_loaded{i}") for i in range(UN)]
        aux_loaded = sem("aux_loaded")
        e0_stored = [sem(f"e0_stored{i}") for i in range(2)]
        e1_stored = [sem(f"e1_stored{i}") for i in range(2)]
        x2_stored = [sem(f"x2_stored{i}") for i in range(4)]
        pair_stored = [sem(f"pair_stored{i}") for i in range(4)]
        sp_passed = sem("embed_sp_passed")
        pool_passed = sem("embed_pool_passed")
        dve_passed = sem("embed_dve_passed")
        (cleared, x_stat, x2_stat, e0_stat, e1_stat, mv_ready, std_ready, rstd_ready, nb_ready, h0_ready,
         h0_turned, hT_ready, z_ready, e0_ready, e0_aux, n1_ready, e1_scaled, e1_ready, n2_ready, n2_turned,
         n2T_ready, x2_mm, xb_ready, x2_ready, r_ready, ss_ready, nrm_ready, nmax_ready, inv_ready, w1_ready,
         rw_ready, hth_mm, k_ready, row_ready, idx_ready) = (sem(s) for s in (
            "cleared", "x_stat", "x2_stat", "e0_stat", "e1_stat", "mv_ready", "std_ready", "rstd_ready",
            "nb_ready", "h0_ready", "h0_turned", "hT_ready", "z_ready", "e0_ready", "e0_aux", "n1_ready",
            "e1_scaled", "e1_ready", "n2_ready", "n2_turned", "n2T_ready", "x2_mm", "xb_ready", "x2_ready",
            "r_ready", "ss_ready", "nrm_ready", "nmax_ready", "inv_ready", "w1_ready", "rw_ready", "hth_mm",
            "k_ready", "row_ready", "idx_ready"))
        block = ctx.enter_context(nc.Block())

        def exists(g):
            return not isinstance(g, int) or 0 <= g <= NG

        def shape(g):
            return (TAIL, 1) if isinstance(g, int) and g == NG else (P, G)

        def nodes(ap, g):
            p, n = shape(g)
            return ap[bass.ds(g * (P * G), p * n), :].rearrange("(p k) c -> p k c", k=n)

        def stored(eng, sems, g, slots, m, passed=None):
            if not isinstance(g, int) or g >= slots:
                eng.wait_ge(sems[m % slots], dma_count(g - slots, m % slots, slots))
                if passed is not None:
                    eng.sem_inc(passed, 1)

        @block.sync
        def _(sp):
            for k in range(2):
                sp.dma_start(aux[:, k, 0:NG * G].rearrange("p (g k) -> p g k", k=G),
                             t["AUX"][k, 0:NG * P * G].rearrange("(g p k) -> p g k", p=P, k=G)).then_inc(aux_loaded, 16)
                sp.dma_start(aux[0:TAIL, k, NG * G:NG * G + 1],
                             t["AUX"][k, NG * P * G:N].rearrange("(p k) -> p k", k=1)).then_inc(aux_loaded, 16)

            def load(g, m):
                if exists(g):
                    p, n = shape(g)
                    pace(sp, sp_passed, x2_ready, g - UN + 1)
                    sp.dma_start(xt[0:p, m % UN, 0:n, :], nodes(t["x"], g)).then_inc(x_loaded[m % UN], 16)

            def step(s, m):
                load(s + 1, m + 1)
                g, mg = s - C - 1, m - C - 1
                if exists(g):
                    p, n = shape(g)
                    pace(sp, sp_passed, e0_ready, g + 1)
                    pace(sp, sp_passed, e0_aux, g + 1)
                    sp.dma_start(nodes(t["E0"], g), e0[0:p, mg % 2, 0:n, :]).then_inc(e0_stored[mg % 2], 16)
                    pace(sp, sp_passed, e1_ready, g + 1)
                    sp.dma_start(nodes(t["E1"], g), e1[0:p, mg % 2, 0:n, :]).then_inc(e1_stored[mg % 2], 16)
                g, mg = s - H - 1, m - H - 1
                if exists(g):
                    p, n = shape(g)
                    pace(sp, sp_passed, row_ready, g + 1)
                    sp.dma_start(nodes(t["X2"], g), x2[0:p, mg % 4, 0:n, :]).then_inc(x2_stored[mg % 4], 16)

            load(0, 0)
            run_steps(sp, step, STEPS, LO, HI, UN)
            for stores, slots in ((e0_stored, 2), (e1_stored, 2), (x2_stored, 4)):
                for k in range(slots):
                    sp.wait_ge(stores[k], 16 * len(range(k, NG + 1, slots)))

        @block.gpsimd
        def _(pool):
            pool.memset(e0[:, :, :, D:], 0.0)
            pool.memset(e1[:, :, :, D:], 0.0)
            pool.memset(x2[:, :, :, W:], 0.0)
            pool.memset(mv[:, :, :, :, :], 1.0).then_inc(cleared, 1)
            pool.wait_ge(cleared, 1)
            pool.wait_ge(aux_loaded, 64)

            def scatter(q, m):
                if not isinstance(q, int) or q >= 4:
                    pool.wait_ge(pair_stored[m % 4], dma_count(q - 4, m % 4, 4, 16 * ET))
                    pool.sem_inc(pool_passed, 1)
                pool.tensor_copy(idx[:, m % 4, :], c["posI"][:, bass.ds(q * ET, ET)])
                pool.tensor_copy(pay[:, m % 4, :, :], c["pairs"][:, bass.ds(q * ET, ET), :]).then_inc(idx_ready, 1)
                pace(pool, pool_passed, idx_ready, q + 1)
                for j in range(ET):
                    pool.indirect_dma_start(t["SORTED"][:, :], bass.IndirectOffsetOnAxis(idx[:, m % 4, j:j + 1], 0),
                                            pay[:, m % 4, j, :], None).then_inc(pair_stored[m % 4], 16)

            def step(s, m):
                g, mg = s - C, m - C
                if exists(g):
                    p, n = shape(g)
                    slot = mg % 2
                    dinv = aux[0:p, 1, bass.ds(g * G, n)]
                    xs = xt[0:p, mg % UN, 0:n, :]
                    pace(pool, pool_passed, h0_ready, g + 1)
                    pool.tensor_tensor(xs, xs, spread(c["bias2"], p, n, W), ALU.add).then_inc(xb_ready, 1)
                    stored(pool, e0_stored, g, 2, mg, pool_passed)
                    pool.tensor_copy(e0[0:p, slot, 0:n, D], dinv).then_inc(e0_aux, 1)
                    stored(pool, e1_stored, g, 2, mg, pool_passed)
                    pool.tensor_copy(e1[0:p, slot, 0:n, D], dinv)
                    pace(pool, pool_passed, e1_stat, g - 1)
                    pace(pool, pool_passed, n2_ready, g - 1)
                    pace(pool, pool_passed, n1_ready, g + 1)
                    es = e1[0:p, slot, 0:n, 0:D]
                    pool.tensor_tensor(es, n1[0:p, slot, 0:n, :], spread(c["ln1s"], p, n, D), ALU.mult).then_inc(e1_scaled, 1)
                    pace(pool, pool_passed, e1_scaled, g + 1)
                    pool.tensor_tensor(es, es, spread(c["ln1b"], p, n, D), ALU.add).then_inc(e1_ready, 1)
                g, mg = s - H, m - H
                if exists(g):
                    p, n = shape(g)
                    slot, at = mg % 2, (m - 1) % 2
                    row = x2[0:p, mg % 4, 0:n, :]
                    invs = inv[0:p, slot, 0:n]
                    pace(pool, pool_passed, inv_ready, g + 1)
                    pool.tensor_tensor(row[:, :, W], rstd[0:p, at, SX2, 0:n], invs, ALU.mult)
                    pool.tensor_copy(row[:, :, W + 4], aux[0:p, 1, bass.ds(g * G, n)])
                    pool.tensor_tensor(row[:, :, W + 1], nb[0:p, at, SX2, 0:n], invs, ALU.mult).then_inc(k_ready, 1)
                    pace(pool, pool_passed, k_ready, g + 1)
                    pool.tensor_tensor(row[:, :, W + 2], row[:, :, W], row[:, :, W + 4], ALU.mult)
                    pool.tensor_tensor(row[:, :, W + 3], row[:, :, W + 1], row[:, :, W + 4], ALU.mult).then_inc(row_ready, 1)

            for s in range(LO):
                if s >= SCATTER_LO:
                    scatter(s - SCATTER_LO, s - SCATTER_LO)
                step(s, s)
            with pool.Fori(LO, SCATTER_HI - UN + 1, UN) as i:
                for u in range(UN):
                    scatter(i + (u - SCATTER_LO), u)
                    step(i + u, u)
            with pool.Fori(SCATTER_HI, HI - UN + 1, UN) as i:
                for u in range(UN):
                    step(i + u, u)
            for s in range(HI, STEPS):
                q = SCATTER_HI - SCATTER_LO + s - HI
                if q < 2 * EG:
                    scatter(q, q)
                step(s, s)
            for k in range(4):
                pool.wait_ge(pair_stored[k], 16 * ET * len(range(k, 2 * EG, 4)))

        @block.vector
        def _(dve):
            def stats(tile, place, m, p, n, stat, g):
                for k in range(n):
                    o = dve.bn_stats(st[0:p, place, k, :], tile[:, k, :])
                o.then_inc(stat, 1)
                need(dve, stat, g + 1)
                dve.sem_inc(dve_passed, 1)
                for k in range(n):
                    o = dve.bn_aggr(mv[0:p, m % 2, place, k, :], st[0:p, place, k, :])
                return o

            def step(s, m):
                par = m % 2
                g, mg = s - X, m - X
                if exists(g):
                    p, n = shape(g)
                    need(dve, x2_mm, g + 1)
                    need(dve, xb_ready, g + 1)
                    need(dve, r_ready, g - 3)
                    stored(dve, x2_stored, g, 4, mg)
                    dve.tensor_tensor(x2[0:p, mg % 4, 0:n, 0:W], ps_x[0:p, 0:n, :], xt[0:p, mg % UN, 0:n, :],
                                      ALU.add).then_inc(x2_ready, 1)
                    need(dve, x2_ready, g + 1)
                    last = stats(x2[0:p, mg % 4, 0:n, 0:W], SX2, m, p, n, x2_stat, g)
                g, mg = s - C, m - C
                if exists(g):
                    p, n = shape(g)
                    need(dve, z_ready, g + 1)
                    need(dve, n1_ready, g - 1)
                    stored(dve, e0_stored, g, 2, mg)
                    dve.tensor_tensor(e0[0:p, mg % 2, 0:n, 0:D], ps_z[0:p, 0:n, :], spread(c["bias0"], p, n, D),
                                      ALU.add).then_inc(e0_ready, 1)
                    need(dve, e0_ready, g + 1)
                    last = stats(e0[0:p, mg % 2, 0:n, 0:D], SE0, m, p, n, e0_stat, g)
                g, mg = s - M, m - M
                if exists(g):
                    p, n = shape(g)
                    need(dve, e1_ready, g + 1)
                    last = stats(e1[0:p, mg % 2, 0:n, 0:D], SE1, m, p, n, e1_stat, g)
                if exists(s):
                    p, n = shape(s)
                    dve.wait_ge(x_loaded[m % UN], dma_count(s, m % UN, UN))
                    last = stats(xt[0:p, m % UN, 0:n, :], SX, m, p, n, x_stat, s)
                if s is not None and (not isinstance(s, int) or s <= NG + X):
                    last.then_inc(mv_ready, 1)
                    need(dve, h0_ready, s - 1 if not isinstance(s, int) else min(s - 1, NG + 1))
                    need(dve, r_ready, s - H)
                    need(dve, row_ready, s - H)
                    need(dve, std_ready, s + 1)
                    dve.reciprocal(rstd[:, par, :, :], std[:, par, :, :]).then_inc(rstd_ready, 1)
                    need(dve, rstd_ready, s + 1)
                    dve.scalar_tensor_tensor(out=nb[:, par, :, :], in0=mv[:, par, :, :, 0], scalar=-1.0,
                                             in1=rstd[:, par, :, :], op0=ALU.mult, op1=ALU.mult).then_inc(nb_ready, 1)
                g, mg = s - M, m - M
                if exists(g):
                    p, n = shape(g)
                    need(dve, n2_turned, g + 1)
                    need(dve, x2_mm, g - 1)
                    dve.tensor_copy(n2T[:, mg % 2, 0:n, 0:p], ps_n[:, 0:n, 0:p]).then_inc(n2T_ready, 1)
                g, mg = s - H, m - H
                if exists(g):
                    p, n = shape(g)
                    slot = mg % 2
                    need(dve, nrm_ready, g + 1)
                    dve.tensor_scalar(nrm[0:p, slot, 0:n], nrm[0:p, slot, 0:n], EPS_L2, None, ALU.max).then_inc(nmax_ready, 1)
                    need(dve, nmax_ready, g + 1)
                    need(dve, row_ready, g - 1)
                    dve.reciprocal(inv[0:p, slot, 0:n], nrm[0:p, slot, 0:n]).then_inc(inv_ready, 1)
                    need(dve, inv_ready, g + 1)
                    dve.tensor_tensor(w1[0:p, slot, 0:n], inv[0:p, slot, 0:n], aux[0:p, 0, bass.ds(g * G, n)],
                                      ALU.mult).then_inc(w1_ready, 1)
                    need(dve, w1_ready, g + 1)
                    need(dve, hth_mm, g - 1)
                    for k in range(n):
                        o = dve.tensor_scalar(rw[0:p, slot, k, :], r[0:p, slot, k, :], inv[0:p, slot, k:k + 1],
                                              w1[0:p, slot, k:k + 1], ALU.mult, ALU.mult)
                    o.then_inc(rw_ready, 1)

            dve.wait_ge(cleared, 1)
            dve.wait_ge(aux_loaded, 64)
            run_steps(dve, step, STEPS, LO, HI, UN)
            need(dve, hth_mm, NG + 1)
            dve.tensor_copy(c["hth"][:, :, :], ps_hth[:, :, :])

        @block.scalar
        def _(act):
            def step(s, m):
                par, before = m % 2, (m - 1) % 2
                g, mg = s - B, m - B
                if exists(g):
                    p, n = shape(g)
                    need(act, nb_ready, g + 1)
                    need(act, h0_turned, g - 1)
                    for k in range(n):
                        o = nc.scalar.activation(h0[0:p, mg % 2, k, :], xt[0:p, mg % UN, k, :], ACT.Relu,
                                                 bias=nb[0:p, before, SX, k:k + 1], scale=rstd[0:p, before, SX, k:k + 1])
                    o.then_inc(h0_ready, 1)
                g, mg = s - H, m - H
                if exists(g):
                    p, n = shape(g)
                    slot = mg % 2
                    need(act, nb_ready, g + X + 1)
                    need(act, hth_mm, g - 1)
                    need(act, rw_ready, g - 1)
                    for k in range(n):
                        o = nc.scalar.activation(r[0:p, slot, k, :], x2[0:p, mg % 4, k, 0:W], ACT.Relu,
                                                 bias=nb[0:p, before, SX2, k:k + 1], scale=rstd[0:p, before, SX2, k:k + 1])
                    o.then_inc(r_ready, 1)
                    need(act, r_ready, g + 1)
                    need(act, ss_ready, g)
                    for k in range(n):
                        o = nc.scalar.activation(rsq[0:p, k, :], r[0:p, slot, k, :], ACT.Square,
                                                 accum_out=ss[0:p, slot, k:k + 1])
                    o.then_inc(ss_ready, 1)
                    need(act, ss_ready, g + 1)
                    need(act, inv_ready, g - 1)
                    nc.scalar.activation(nrm[0:p, slot, 0:n], ss[0:p, slot, 0:n], ACT.Sqrt).then_inc(nrm_ready, 1)
                g, mg = s - B, m - B
                if exists(g):
                    p, n = shape(g)
                    need(act, h0_turned, g + 1)
                    need(act, z_ready, g - 1)
                    nc.scalar.copy(hT[:, mg % 2, 0:n, :, 0:p], ps_h[:, 0:n, :, 0:p]).then_inc(hT_ready, 1)
                if not isinstance(s, int) or s <= NG + X:
                    need(act, mv_ready, s + 1)
                    need(act, rstd_ready, s - 1)
                    nc.scalar.activation(std[:, par, 0:2, :], mv[:, par, 0:2, :, 1], ACT.Sqrt, bias=c["eps"][:, 0:1])
                    nc.scalar.activation(std[:, par, 2:4, :], mv[:, par, 2:4, :, 1], ACT.Sqrt,
                                         bias=c["eps"][:, 1:2]).then_inc(std_ready, 1)
                for skew, slot_of, src_, dst_, place, before_write, ready in (
                        (M, 2, e1, n2, SE1, n2_turned, n2_ready), (C, 2, e0, n1, SE0, e1_scaled, n1_ready)):
                    g, mg = s - skew, m - skew
                    if exists(g):
                        p, n = shape(g)
                        need(act, nb_ready, s + 1)
                        need(act, before_write, g - 1)
                        for k in range(n):
                            o = nc.scalar.activation(dst_[0:p, mg % 2, k, :], src_[0:p, mg % 2, k, 0:D], ACT.Identity,
                                                     bias=nb[0:p, par, place, k:k + 1], scale=rstd[0:p, par, place, k:k + 1])
                        o.then_inc(ready, 1)

            run_steps(act, step, STEPS, LO, HI, UN)

        @block.tensor
        def _(pe):
            def hth(g, mg, first=False):
                p, n = shape(g)
                need(pe, rw_ready, g + 1)
                for k in range(n):
                    for h in range(2):
                        o = pe.matmul(ps_hth[:, h, :], rw[0:p, mg % 2, k, h * P:(h + 1) * P], r[0:p, mg % 2, k, :],
                                      start=first and k == 0 and h == 0, stop=isinstance(g, int) and g == NG,
                                      skip_group_check=True)
                o.then_inc(hth_mm, 1)

            def step(s, m):
                g, mg = s - T, m - T
                if exists(g):
                    hth(g, mg, isinstance(g, int) and g == 0)
                g, mg = s - B, m - B
                if exists(g):
                    p, n = shape(g)
                    need(pe, h0_ready, g + 1)
                    need(pe, hT_ready, g)
                    for k in range(n):
                        for h in range(2):
                            o = pe.transpose(ps_h[:, k, h, 0:p], h0[0:p, mg % 2, k, h * P:(h + 1) * P], c["ident"][0:p, 0:p])
                    o.then_inc(h0_turned, 1)
                g, mg = s - B, m - B
                if exists(g):
                    p, n = shape(g)
                    need(pe, hT_ready, g + 1)
                    need(pe, e0_ready, g)
                    for k in range(n):
                        for h in range(2):
                            o = pe.matmul(ps_z[0:p, k, :], hT[:, mg % 2, k, h, 0:p], c["wP"][:, h, :],
                                          start=h == 0, stop=h == 1)
                    o.then_inc(z_ready, 1)
                g, mg = s - M, m - M
                if exists(g):
                    p, n = shape(g)
                    need(pe, n2_ready, g + 1)
                    need(pe, n2T_ready, g)
                    for k in range(n):
                        o = pe.transpose(ps_n[:, k, 0:p], n2[0:p, mg % 2, k, :], c["ident"][0:p, 0:p])
                    o.then_inc(n2_turned, 1)
                    need(pe, n2T_ready, g + 1)
                    need(pe, x2_ready, g)
                    for k in range(n):
                        o = pe.matmul(ps_x[0:p, k, :], n2T[:, mg % 2, k, 0:p], c["w2"][:, :], start=True, stop=True)
                    o.then_inc(x2_mm, 1)

            run_steps(pe, step, STEPS, LO, HI, UN)


def unpack_lists(nc, c, t):
    with ExitStack() as ctx:
        def sb(name, shape, dt=F32):
            return ctx.enter_context(nc.sbuf_tensor(name, shape, dt))

        sem = phase_sems(nc, ctx)

        pairT = sb("pairT", [HT, 2, 2, P, 2], I32)
        nextT = sb("nextT", [HT, 2, 2, P, 2], I32)
        listT = sb("listT", [HT, 3, 2, 2, P])
        ends = sb("ends", [P, 2, NT])
        skip = sb("skip", [P, 2, NT])
        turn = [ctx.enter_context(nc.psum_tensor(f"turn{i}", [P, 512], F32)) for i in range(3)]
        loaded = sem("lists_loaded")
        floats = sem("list_floats")
        stored = sem("list_rows_stored")
        turned = sem("list_turned")
        ready = sem("list_ready")
        ends_ready = sem("ends_ready")
        fin_ready = sem("fin_ready")
        skip_ready = sem("skip_ready")
        block = ctx.enter_context(nc.Block())

        @block.sync
        def _(sp):
            for l in range(2):
                for off, tile in ((0, pairT), (1, nextT)):
                    at = l * LIST + off
                    sp.dma_start(tile[:, l, :, :, :], t["SORTED"][at:at + EP, :].rearrange(
                        "(a r c) k -> r a (c k)", a=2, c=P).rearrange("r a (c k) -> r a c k", k=2)).then_inc(loaded, 16)
            sp.wait_ge(floats, 2)
            for l in range(2):
                sp.dma_start(t["KEYROW"][l].rearrange("(a r c) -> r a c", a=2, c=P), listT[:, 0, l, :, :]).then_inc(stored, 16)
            sp.wait_ge(stored, 32)

        @block.vector
        def _(dve):
            dve.wait_ge(loaded, 64)
            for kind, tile, who in ((0, pairT, (0, 1)), (1, pairT, (1, 0)), (2, nextT, (0, 1))):
                for l in range(2):
                    dve.tensor_copy(listT[:, kind, l, :, :], tile[:, l, :, :, who[l]]).then_inc(floats, 1)
            dve.wait_ge(ready, 3)
            ek = c["ek"]
            dve.tensor_tensor(ends[:, :, :], ek[:, 0, :, :], ek[:, 2, :, :], ALU.not_equal).then_inc(ends_ready, 1)
            dve.tensor_scalar(c["keyI"][:, :, :], ek[:, 0, :, :], float(N - 1), None, ALU.min)
            dve.tensor_scalar(c["otherI"][:, :, :], ek[:, 1, :, :], float(N - 1), None, ALU.min)
            dve.wait_ge(ends_ready, 1)
            dve.scalar_tensor_tensor(out=c["fin"][:, :, :], in0=ek[:, 0, :, :], scalar=float(N), in1=ends[:, :, :],
                                     op0=ALU.is_lt, op1=ALU.mult).then_inc(fin_ready, 1)
            dve.wait_ge(fin_ready, 1)
            dve.tensor_scalar(skip[:, :, :], c["fin"][:, :, :], -SKIP, SKIP, ALU.mult, ALU.add).then_inc(skip_ready, 1)
            dve.wait_ge(skip_ready, 1)
            dve.tensor_tensor(c["finI"][:, :, :], skip[:, :, :], ek[:, 0, :, :], ALU.add)

        @block.scalar
        def _(act):
            for kind in range(3):
                act.wait_ge(turned, kind + 1)
                nc.scalar.copy(c["ek"][:, kind, :, :].rearrange("p l t -> p (l t)"), turn[kind][:, 0:2 * NT]).then_inc(ready, 1)

        @block.tensor
        def _(pe):
            for kind in range(3):
                pe.wait_ge(floats, 2 * kind + 2)
                for l in range(2):
                    for a in range(2):
                        at = (l * 2 + a) * HT
                        o = pe.transpose(turn[kind][:, at:at + HT], listT[:, kind, l, a, :], c["ident"][0:HT, 0:HT])
                o.then_inc(turned, 1)


def edge_attention(nc, c, t, layer):
    last = layer == 2
    UN, LO, HI = 8, 9, 49
    B, C, M, X, H, T = 1, 2, 3, 4, 5, 6
    SC = 6 if last else 3
    STEPS = EG + SC
    VW = D + HEADS
    R4 = ET
    table = t["E1"] if last else t["E0"]
    wt = c["qkv2"] if last else c["qkv1"]
    L = f"_{layer}"
    with ExitStack() as ctx:
        def sb(name, shape, dt=F32):
            return ctx.enter_context(nc.sbuf_tensor(name + L, shape, dt))

        def ps(name, shape):
            return ctx.enter_context(nc.psum_tensor(name + L, shape, F32))

        sem = phase_sems(nc, ctx, L)

        idx = sb("gather_idx", [P, 4, 2, ET], I32)
        fidx = sb("final_idx", [P, 4, ET], I32)
        rrow = sb("src_rows", [P, 4, ET, EW])
        crow = sb("dst_rows", [P, 2, ET, EW])
        keys = sb("keys", [P, 2, ET * P])
        kc = sb("key_cols", [P, 2, ET + 1])
        dv = sb("dinv", [P, 8, ET])
        S = sb("same_src", [P, 2, ET, P])
        cm = sb("carry_to", [P, 2, ET, P])
        rT = sb("rT", [P, ET, P])
        cT = sb("cT", [P, ET, P])
        qs = sb("qs", [P, ET, D])
        qk = sb("qk", [P, ET, D])
        att = sb("att", [P, 2, ET * HEADS])
        vals = sb("vals", [P, 2, ET, VW])
        carry = sb("carry", [P, ET, VW])
        den = sb("den", [P, 2, ET, HEADS])
        emb = sb("emb", [P, 2, 2, ET, D])
        nrmd = sb("normalised", [P, 2, ET, D])
        st = sb("st", [P, 2, ET, 6])
        mv = sb("mv", [P, 2, 2, ET, 2])
        std = sb("std", [P, 2, 2, ET])
        rstd = sb("rstd", [P, 2, 2, ET])
        nb = sb("nb", [P, 2, 2, ET])
        ps_r = ps("ps_r", [P, ET, P])
        ps_c = ps("ps_c", [P, ET, P])
        ps_q = ps("ps_q", [P, ET, D])
        ps_kv = ps("ps_kv", [P, ET, 2, D])
        ps_a = ps("ps_a", [P, ET, 2 * D])
        if last:
            xr = sb("x_rows", [P, 4, ET, W])
            x2 = sb("x2_new", [P, 4, ET, XW])
            n2T = sb("n2T", [P, ET, P])
            r = sb("r", [P, 2, ET, W])
            rsq = sb("rsq", [P, ET, W])
            rw = sb("rw", [P, 2, ET, W])
            ss = sb("ss", [P, 2, ET])
            nrm = sb("nrm", [P, 2, ET])
            inv = sb("inv", [P, 2, ET])
            w1 = sb("w1", [P, 2, ET])
            ps_hth = ps("ps_hth", [P, 2, W])
        else:
            e1 = sb("e1_new", [P, 2, 2, ET, EW])

        r_loaded = [sem(f"r_loaded{i}") for i in range(4)]
        c_loaded = [sem(f"c_loaded{i}") for i in range(2)]
        x_loaded = [sem(f"xr_loaded{i}") for i in range(4)] if last else None
        keys_loaded = [sem(f"keys_loaded{i}") for i in range(2)]
        new_stored = [sem(f"new_stored{i}") for i in range(4)]
        names = ("sp_passed", "pool_passed", "dve_passed", "cleared", "idx_ready", "fidx_ready", "kc_ready",
                 "S_ready", "dv_ready", "r_turned", "c_turned", "rT_ready", "cT_ready", "q_mm", "kv_mm", "q_ready",
                 "qk_ready", "att_ready", "clip_ready", "exp_ready", "vals_ready", "agg_mm", "carry_ready",
                 "den_ready", "rec_ready", "avg_ready", "emb_ready", "stat", "mv_ready", "std_ready", "rstd_ready",
                 "nb_ready", "n_ready", "scaled", "new_ready")
        if last:
            names += ("n2_turned", "n2T_ready", "x2_mm", "x2_ready", "x2_stat", "r_ready", "ss_ready", "nrm_ready",
                      "nmax_ready", "inv_ready", "k_ready", "rw_ready", "hth_mm")
        sems = {name: sem(name) for name in names}
        (sp_passed, pool_passed, dve_passed, cleared, idx_ready, fidx_ready, kc_ready, S_ready, dv_ready, r_turned,
         c_turned, rT_ready, cT_ready, q_mm, kv_mm, q_ready, qk_ready, att_ready, clip_ready, exp_ready, vals_ready,
         agg_mm, carry_ready, den_ready, rec_ready, avg_ready, emb_ready, stat, mv_ready, std_ready, rstd_ready,
         nb_ready, n_ready, scaled, new_ready) = (sems[name] for name in names[:35])
        if last:
            (n2_turned, n2T_ready, x2_mm, x2_ready, x2_stat, r_ready, ss_ready, nrm_ready, nmax_ready, inv_ready,
             k_ready, rw_ready, hth_mm) = (sems[name] for name in names[35:])
        block = ctx.enter_context(nc.Block())

        def exists(g):
            return not isinstance(g, int) or 0 <= g < EG

        @block.sync
        def _(sp):
            def step(s, m):
                if exists(s):
                    pace(sp, sp_passed, S_ready, s - 1)
                    sp.dma_start(keys[:, m % 2, :], t["KEYROW"][0, bass.ds(s * (ET * P), ET * P)].partition_broadcast(P)
                                 ).then_inc(keys_loaded[m % 2], 16)

            run_steps(sp, step, EG, LO, HI, UN)

        @block.gpsimd
        def _(pool):
            bound = pool.to_reg(N - 1)

            def gather(tile, slot, source, kind, islot, loaded):
                for j in range(ET):
                    pool.indirect_dma_start(tile[:, slot, j, :], None, source[:, :],
                                            bass.IndirectOffsetOnAxis(idx[:, islot, kind, j:j + 1], 0)
                                            ).then_inc(loaded[slot], 16)

            def step(s, m):
                if exists(s):
                    if not isinstance(s, int) or s >= 4:
                        for loaded in ((r_loaded, x_loaded) if last else (r_loaded,)):
                            pool.wait_ge(loaded[m % 4], dma_count(s - 4, m % 4, 4, 16 * ET))
                            pool.sem_inc(pool_passed, 1)
                    if not isinstance(s, int) or s >= 2:
                        pool.wait_ge(c_loaded[m % 2], dma_count(s - 2, m % 2, 2, 16 * ET))
                        pool.sem_inc(pool_passed, 1)
                    pool.tensor_copy(idx[:, m % 4, 0, :], c["keyI"][:, 0, bass.ds(s * ET, ET)])
                    pool.tensor_copy(idx[:, m % 4, 1, :], c["otherI"][:, 0, bass.ds(s * ET, ET)]).then_inc(idx_ready, 1)
                    pace(pool, pool_passed, idx_ready, s + 1)
                    pace(pool, pool_passed, emb_ready, s - 3)
                    pace(pool, pool_passed, r_turned, s - 3)
                    pace(pool, pool_passed, dv_ready, s - 3)
                    gather(rrow, m % 4, table, 0, m % 4, r_loaded)
                    pace(pool, pool_passed, c_turned, s - 1)
                    gather(crow, m % 2, table, 1, m % 4, c_loaded)
                    if last:
                        pace(pool, pool_passed, x2_ready, s - 3)
                        gather(xr, m % 4, t["x"], 0, m % 4, x_loaded)
                g, mg = s - SC, m - SC
                if exists(g):
                    if not isinstance(g, int) or g >= 4:
                        pool.wait_ge(new_stored[mg % 4], dma_count(g - 4, mg % 4, 4, 16 * ET))
                        pool.sem_inc(pool_passed, 1)
                    pool.tensor_copy(fidx[:, mg % 4, :], c["finI"][:, 0, bass.ds(g * ET, ET)]).then_inc(fidx_ready, 1)
                    pace(pool, pool_passed, fidx_ready, g + 1)
                    pace(pool, pool_passed, new_ready, g + 1)
                    for j in range(ET):
                        new = x2[:, mg % 4, j, :] if last else e1[:, 1, mg % 2, j, :]
                        pool.indirect_dma_start(t["X2" if last else "E1"][:, :],
                                                bass.IndirectOffsetOnAxis(fidx[:, mg % 4, j:j + 1], 0), new, None,
                                                bounds_check=bound, oob_is_err=False).then_inc(new_stored[mg % 4], 16)

            run_steps(pool, step, STEPS, LO, HI, UN)
            for k in range(4):
                pool.wait_ge(new_stored[k], 16 * ET * len(range(k, EG, 4)))

        @block.vector
        def _(dve):
            def stats(tile, place, m, done, g):
                for j in range(ET):
                    o = dve.bn_stats(st[:, place, j, :], tile[:, j, :])
                o.then_inc(done, 1)
                need(dve, done, g + 1)
                dve.sem_inc(dve_passed, 1)
                for j in range(ET):
                    o = dve.bn_aggr(mv[:, m % 2, place, j, :], st[:, place, j, :])
                return o

            def step(s, m):
                par, before = m % 2, (m - 1) % 2
                if last:
                    g, mg = s - X, m - X
                    if exists(g):
                        need(dve, x2_mm, g + 1)
                        dve.wait_ge(x_loaded[mg % 4], dma_count(g, mg % 4, 4, 16 * ET))
                        need(dve, r_ready, g - 3)
                        if not isinstance(g, int) or g >= 4:
                            dve.wait_ge(new_stored[mg % 4], dma_count(g - 4, mg % 4, 4, 16 * ET))
                        dve.tensor_tensor(x2[:, mg % 4, :, 0:W], ps_kv[:, :, :, :].rearrange("p j k d -> p j (k d)"),
                                          xr[:, mg % 4, :, :], ALU.add).then_inc(x2_ready, 1)
                        need(dve, x2_ready, g + 1)
                        tail = stats(x2[:, mg % 4, :, 0:W], 1, m, x2_stat, g)
                    g, mg = s - M, m - M
                    if exists(g):
                        need(dve, n2_turned, g + 1)
                        need(dve, x2_mm, g)
                        dve.tensor_copy(n2T[:, :, :], ps_r[:, :, :]).then_inc(n2T_ready, 1)
                g, mg = s - B, m - B
                if exists(g):
                    p2 = mg % 2
                    lo = 1 if isinstance(g, int) and g == 0 else 0
                    if lo:
                        dve.memset(kc[:, p2, 0:1], -1.0)
                    dve.tensor_copy(kc[:, p2, lo:], c["ek"][:, 0, 0, bass.ds(g * ET - 1 + lo, ET + 1 - lo)]).then_inc(kc_ready, 1)
                    need(dve, kc_ready, g + 1)
                    dve.wait_ge(keys_loaded[p2], dma_count(g, p2, 2))
                    need(dve, agg_mm, (g - 1) * ET)
                    for j in range(ET):
                        kj = keys[:, p2, j * P:(j + 1) * P]
                        dve.tensor_scalar(S[:, p2, j, :], kj, kc[:, p2, j + 1:j + 2], None, ALU.is_equal)
                        o = dve.tensor_scalar(cm[QUAD:, p2, j, :], kj[QUAD:, :], kc[QUAD:, p2, j:j + 1],
                                              c["e127"][QUAD:, :], ALU.is_equal, ALU.mult)
                    o.then_inc(S_ready, 1)
                    dve.wait_ge(r_loaded[mg % 4], dma_count(g, mg % 4, 4, 16 * ET))
                    dve.tensor_copy(dv[:, mg % 8, :], rrow[:, mg % 4, :, D]).then_inc(dv_ready, 1)
                    need(dve, c_turned, g + 1)
                    need(dve, kv_mm, g)
                    dve.tensor_copy(cT[:, :, :], ps_c[:, :, :]).then_inc(cT_ready, 1)
                g, mg = s - C, m - C
                if exists(g):
                    p2 = mg % 2
                    need(dve, carry_ready, (g + 1) * ET)
                    dve.tensor_scalar(den[:, 0, :, :], ps_a[:, :, D:VW], EPS_ATT, None, ALU.add).then_inc(den_ready, 1)
                    need(dve, den_ready, g + 1)
                    dve.reciprocal(den[:, 1, :, :], den[:, 0, :, :]).then_inc(rec_ready, 1)
                    need(dve, rec_ready, g + 1)
                    need(dve, n_ready, g - 1)
                    dve.tensor_tensor(
                        emb[:, 0, p2, :, :].rearrange("p j (h d) -> p j h d", h=HEADS),
                        ps_a[:, :, 0:D].rearrange("p j (h d) -> p j h d", h=HEADS),
                        den[:, 1, :, :].unsqueeze(3).to_broadcast([P, ET, HEADS, HD]), ALU.mult).then_inc(avg_ready, 1)
                    need(dve, avg_ready, g + 1)
                    dve.tensor_tensor(emb[:, 1, p2, :, :], emb[:, 0, p2, :, :], rrow[:, mg % 4, :, 0:D],
                                      ALU.add).then_inc(emb_ready, 1)
                    need(dve, emb_ready, g + 1)
                    tail = stats(emb[:, 1, p2, :, :], 0, m, stat, g)
                if not isinstance(s, int) or C <= s < EG + (X if last else C):
                    tail.then_inc(mv_ready, 1)
                n = s - C
                g, mg = s - B, m - B
                if exists(g):
                    need(dve, q_ready, g + 1)
                    need(dve, kv_mm, g + 1)
                    dve.tensor_tensor(qk[:, :, :], qs[:, :, :], ps_kv[:, :, 0, :], ALU.mult).then_inc(qk_ready, 1)
                    need(dve, qk_ready, g + 1)
                    need(dve, exp_ready, g - 1)
                    dve.tensor_reduce(att[:, mg % 2, :], qk[:, :, :].rearrange("p j (h d) -> p (j h) d", h=HEADS),
                                      AX_X, ALU.add).then_inc(att_ready, 1)
                    need(dve, att_ready, g + 1)
                    dve.tensor_scalar(att[:, mg % 2, :], att[:, mg % 2, :], -10.0, 10.0, ALU.max, ALU.min).then_inc(clip_ready, 1)
                if not isinstance(s, int) or C <= s < EG + (X if last else C):
                    need(dve, n_ready, n - 1 if not isinstance(n, int) else min(n - 1, EG))
                    if last:
                        need(dve, r_ready, s - H)
                        need(dve, new_ready, s - H)
                    need(dve, std_ready, n + 1)
                    dve.reciprocal(rstd[:, par, :, :], std[:, par, :, :]).then_inc(rstd_ready, 1)
                    need(dve, rstd_ready, n + 1)
                    dve.scalar_tensor_tensor(out=nb[:, par, :, :], in0=mv[:, par, :, :, 0], scalar=-1.0,
                                             in1=rstd[:, par, :, :], op0=ALU.mult, op1=ALU.mult).then_inc(nb_ready, 1)
                g, mg = s - B, m - B
                if exists(g):
                    p2 = mg % 2
                    need(dve, exp_ready, g + 1)
                    dve.tensor_tensor(
                        vals[:, p2, :, 0:D].rearrange("p j (h d) -> p j h d", h=HEADS),
                        ps_kv[:, :, 1, :].rearrange("p j (h d) -> p j h d", h=HEADS),
                        vals[:, p2, :, D:VW].unsqueeze(3).to_broadcast([P, ET, HEADS, HD]), ALU.mult).then_inc(vals_ready, 1)
                if not last:
                    g, mg = s - C, m - C
                    if exists(g):
                        p2 = mg % 2
                        need(dve, n_ready, g + 1)
                        if not isinstance(g, int) or g >= 2:
                            dve.wait_ge(new_stored[(mg - 2) % 4], dma_count(g - 2, (mg - 2) % 4, 4, 16 * ET))
                        dve.tensor_tensor(e1[:, 0, p2, :, 0:D], nrmd[:, p2, :, :], spread(c["ln1s"], P, ET, D), ALU.mult)
                        dve.tensor_copy(e1[:, 1, p2, :, D], dv[:, mg % 8, :]).then_inc(scaled, 1)
                        need(dve, scaled, g + 1)
                        dve.tensor_tensor(e1[:, 1, p2, :, 0:D], e1[:, 0, p2, :, 0:D], spread(c["ln1b"], P, ET, D),
                                          ALU.add).then_inc(new_ready, 1)
                else:
                    g, mg = s - H, m - H
                    if exists(g):
                        p2 = mg % 2
                        row = x2[:, mg % 4, :, :]
                        need(dve, nrm_ready, g + 1)
                        dve.tensor_scalar(nrm[:, p2, :], nrm[:, p2, :], EPS_L2, None, ALU.max).then_inc(nmax_ready, 1)
                        need(dve, nmax_ready, g + 1)
                        dve.reciprocal(inv[:, p2, :], nrm[:, p2, :]).then_inc(inv_ready, 1)
                        need(dve, inv_ready, g + 1)
                        dve.tensor_tensor(w1[:, p2, :], inv[:, p2, :], c["fin"][:, 0, bass.ds(g * ET, ET)], ALU.mult)
                        dve.tensor_tensor(row[:, :, W], rstd[:, before, 1, :], inv[:, p2, :], ALU.mult)
                        dve.tensor_copy(row[:, :, W + 4], dv[:, mg % 8, :])
                        dve.tensor_tensor(row[:, :, W + 1], nb[:, before, 1, :], inv[:, p2, :], ALU.mult).then_inc(k_ready, 1)
                        need(dve, k_ready, g + 1)
                        dve.tensor_tensor(row[:, :, W + 2], row[:, :, W], row[:, :, W + 4], ALU.mult)
                        dve.tensor_tensor(row[:, :, W + 3], row[:, :, W + 1], row[:, :, W + 4], ALU.mult).then_inc(new_ready, 1)
                        need(dve, hth_mm, g - 1)
                        for j in range(ET):
                            o = dve.tensor_scalar(rw[:, p2, j, :], r[:, p2, j, :], inv[:, p2, j:j + 1],
                                                  w1[:, p2, j:j + 1], ALU.mult, ALU.mult)
                        o.then_inc(rw_ready, 1)

            dve.memset(mv[:, :, :, :, :], 1.0).then_inc(cleared, 1)
            if last:
                dve.memset(x2[:, :, :, W:], 0.0).then_inc(cleared, 1)
            else:
                dve.memset(e1[:, :, :, :, D:], 0.0).then_inc(cleared, 1)
            dve.wait_ge(cleared, 2)
            run_steps(dve, step, EG + (H if last else C) , LO, HI, UN)
            if last:
                need(dve, hth_mm, EG)
                dve.tensor_tensor(c["hth"][:, :, :], c["hth"][:, :, :], ps_hth[:, :, :], ALU.add)

        @block.scalar
        def _(act):
            def step(s, m):
                par, before = m % 2, (m - 1) % 2
                if last:
                    g, mg = s - H, m - H
                    if exists(g):
                        p2 = mg % 2
                        need(act, nb_ready, s - C)
                        need(act, hth_mm, g - 1)
                        need(act, rw_ready, g - 1)
                        for j in range(ET):
                            o = nc.scalar.activation(r[:, p2, j, :], x2[:, mg % 4, j, 0:W], ACT.Relu,
                                                     bias=nb[:, before, 1, j:j + 1], scale=rstd[:, before, 1, j:j + 1])
                        o.then_inc(r_ready, 1)
                        need(act, r_ready, g + 1)
                        need(act, ss_ready, g)
                        for j in range(ET):
                            o = nc.scalar.activation(rsq[:, j, :], r[:, p2, j, :], ACT.Square, accum_out=ss[:, p2, j:j + 1])
                        o.then_inc(ss_ready, 1)
                        need(act, ss_ready, g + 1)
                        need(act, inv_ready, g - 1)
                        nc.scalar.activation(nrm[:, p2, :], ss[:, p2, :], ACT.Sqrt).then_inc(nrm_ready, 1)
                g, mg = s - B, m - B
                if exists(g):
                    need(act, r_turned, g + 1)
                    need(act, q_mm, g)
                    nc.scalar.copy(rT[:, :, :], ps_r[:, :, :]).then_inc(rT_ready, 1)
                g, mg = s - C, m - C
                if exists(g):
                    for j in range(ET):
                        need(act, agg_mm, g * ET + j + 1)
                        nc.scalar.copy(carry[QUAD:, j, :], ps_a[QUAD:, j, 0:VW]).then_inc(carry_ready, 1)
                g, mg = s - B, m - B
                if exists(g):
                    need(act, q_mm, g + 1)
                    need(act, qk_ready, g)
                    nc.scalar.copy(qs[:, :, :], ps_q[:, :, :]).then_inc(q_ready, 1)
                n = s - C
                if not isinstance(s, int) or C <= s < EG + (X if last else C):
                    need(act, mv_ready, n + 1)
                    need(act, rstd_ready, n - 1)
                    nc.scalar.activation(std[:, par, 0, :], mv[:, par, 0, :, 1], ACT.Sqrt, bias=c["eps"][:, 1:2])
                    nc.scalar.activation(std[:, par, 1, :], mv[:, par, 1, :, 1], ACT.Sqrt,
                                         bias=c["eps"][:, 0:1]).then_inc(std_ready, 1)
                g, mg = s - B, m - B
                if exists(g):
                    p2 = mg % 2
                    need(act, clip_ready, g + 1)
                    need(act, agg_mm, (g - 1) * ET)
                    nc.scalar.activation(vals[:, p2, :, D:VW], att[:, p2, :].rearrange("p (j h) -> p j h", h=HEADS),
                                         ACT.Exp).then_inc(exp_ready, 1)
                g, mg = s - C, m - C
                if exists(g):
                    p2 = mg % 2
                    need(act, nb_ready, n + 1)
                    need(act, n2_turned if last else new_ready, g - 1)
                    for j in range(ET):
                        o = nc.scalar.activation(nrmd[:, p2, j, :], emb[:, 1, p2, j, :], ACT.Identity,
                                                 bias=nb[:, par, 0, j:j + 1], scale=rstd[:, par, 0, j:j + 1])
                    o.then_inc(n_ready, 1)

            run_steps(act, step, EG + (H if last else C), LO, HI, UN)

        @block.tensor
        def _(pe):
            def step(s, m):
                if last:
                    g, mg = s - T, m - T
                    if exists(g):
                        need(pe, rw_ready, g + 1)
                        for j in range(ET):
                            for h in range(2):
                                o = pe.matmul(ps_hth[:, h, :], rw[:, mg % 2, j, h * P:(h + 1) * P], r[:, mg % 2, j, :],
                                              start=isinstance(g, int) and g == 0 and j == 0 and h == 0,
                                              stop=isinstance(g, int) and g == EG - 1 and j == ET - 1,
                                              skip_group_check=True)
                        o.then_inc(hth_mm, 1)
                    g, mg = s - M, m - M
                    if exists(g):
                        need(pe, n_ready, g + 1)
                        need(pe, rT_ready, s - M + 2 if not isinstance(s, int) else min(g + 2, EG))
                        for j in range(ET):
                            o = pe.transpose(ps_r[:, j, :], nrmd[:, mg % 2, j, :], c["ident"][:, :])
                        o.then_inc(n2_turned, 1)
                g, mg = s - B, m - B
                if exists(g):
                    pe.wait_ge(r_loaded[mg % 4], dma_count(g, mg % 4, 4, 16 * ET))
                    need(pe, rT_ready, g)
                    if last:
                        need(pe, n2T_ready, g - M + B + 1)
                    for j in range(ET):
                        o = pe.transpose(ps_r[:, j, :], rrow[:, mg % 4, j, 0:D], c["ident"][:, :])
                    o.then_inc(r_turned, 1)
                    pe.wait_ge(c_loaded[mg % 2], dma_count(g, mg % 2, 2, 16 * ET))
                    need(pe, cT_ready, g)
                    for j in range(ET):
                        o = pe.transpose(ps_c[:, j, :], crow[:, mg % 2, j, 0:D], c["ident"][:, :])
                    o.then_inc(c_turned, 1)
                g, mg = s - C, m - C
                if exists(g):
                    p2 = mg % 2
                    need(pe, S_ready, g + 1)
                    need(pe, vals_ready, g + 1)
                    need(pe, avg_ready, g)
                    for j in range(ET):
                        first = isinstance(g, int) and g == 0 and j == 0
                        need(pe, carry_ready, g * ET + j)
                        o = pe.matmul(ps_a[:, j, 0:VW], S[:, p2, j, :], vals[:, p2, j, :], start=True, stop=first)
                        if not first:
                            o = pe.matmul(ps_a[:, j, 0:VW], cm[QUAD:, p2, j, :], carry[QUAD:, (j - 1) % ET, :],
                                          start=False, stop=True)
                        o.then_inc(agg_mm, 1)
                g, mg = s - B, m - B
                if exists(g):
                    need(pe, rT_ready, g + 1)
                    need(pe, q_ready, g)
                    for j in range(ET):
                        o = pe.matmul(ps_q[:, j, :], rT[:, j, :], wt[:, 0, :], start=True, stop=True)
                    o.then_inc(q_mm, 1)
                    need(pe, cT_ready, g + 1)
                    need(pe, vals_ready, g)
                    if last:
                        need(pe, x2_ready, g - X + B + 1)
                    for j in range(ET):
                        o = pe.matmul(ps_kv[:, j, :, :], cT[:, j, :], wt[:, 1:3, :], start=True, stop=True)
                    o.then_inc(kv_mm, 1)
                if last:
                    g, mg = s - M, m - M
                    if exists(g):
                        need(pe, n2T_ready, g + 1)
                        need(pe, vals_ready, s - B + 1 if not isinstance(s, int) else min(s - B + 1, EG))
                        need(pe, x2_ready, g)
                        for j in range(ET):
                            x2_out = ps_kv[:, j, :, :].rearrange("p k d -> p (k d)")
                            pe.matmul(x2_out, c["ones"][0:1, :], c["bias2"][0:1, :], start=True, stop=False)
                            o = pe.matmul(x2_out, n2T[:, j, :], c["w2"][:, :], start=False, stop=True)
                        o.then_inc(x2_mm, 1)

            run_steps(pe, step, EG + (T if last else C), LO, HI, UN)


def dense_gcn(nc, c, t):
    UN, LO, HI = 8, 8, 128
    B, C, O = 0, 1, 2
    STEPS = NG + 1 + O
    with ExitStack() as ctx:
        def sb(name, shape, dt=F32):
            return ctx.enter_context(nc.sbuf_tensor("n_" + name, shape, dt))

        def ps(name, shape):
            return ctx.enter_context(nc.psum_tensor("n_" + name, shape, F32))

        sem = phase_sems(nc, ctx)
        wsum = sb("wsum", [P, 2, W])
        x2 = sb("x2_in", [P, 8, G, XW])
        h = sb("h", [P, 2, G, W])
        hT = sb("hT", [P, 2, G, 2, P])
        zb = sb("zb", [P, 2, G, W])
        z = sb("z", [P, 2, G, W])
        zsq = sb("zsq", [P, G, W])
        ss = sb("ss", [P, 2, G])
        nrm = sb("nrm", [P, 2, G])
        inv = sb("inv", [P, 2, G])
        o_sb = sb("o_sb", [P, 4, G, W])
        ps_m = ps("ps_m", [P, 2, W])
        ps_h = ps("ps_h", [P, 4, 2, P])
        ps_z = ps("ps_z", [P, 2, 4, W])

        x_loaded = [sem(f"x2_loaded{i}") for i in range(8)]
        o_stored = [sem(f"out_stored{i}") for i in range(4)]
        (sp_passed, m_mm, wv_ready, wsum_ready, h_ready, h_turned, hT_ready, z_mm, zb_ready, z_ready, ss_ready,
         nrm_ready, nmax_ready, inv_ready, o_ready) = (sem("gcn_" + s) for s in (
            "sp_passed", "m_mm", "wv_ready", "wsum_ready", "h_ready", "h_turned", "hT_ready", "z_mm", "zb_ready",
            "z_ready", "ss_ready", "nrm_ready", "nmax_ready", "inv_ready", "o_ready"))
        block = ctx.enter_context(nc.Block())

        def exists(g):
            return not isinstance(g, int) or 0 <= g <= NG

        def shape(g):
            return (TAIL, 1) if isinstance(g, int) and g == NG else (P, G)

        def nodes(ap, g):
            p, n = shape(g)
            return ap[bass.ds(g * (P * G), p * n), :].rearrange("(p k) c -> p k c", k=n)

        @block.sync
        def _(sp):
            def load(g, m):
                if exists(g):
                    p, n = shape(g)
                    pace(sp, sp_passed, o_ready, g - 7)
                    sp.dma_start(x2[0:p, m % 8, 0:n, :], nodes(t["X2"], g)).then_inc(x_loaded[m % 8], 16)

            def step(s, m):
                load(s + 4, m + 4)
                g, mg = s - O, m - O
                if exists(g):
                    p, n = shape(g)
                    pace(sp, sp_passed, o_ready, g + 1)
                    sp.dma_start(nodes(t["out"], g), o_sb[0:p, mg % 4, 0:n, :]).then_inc(o_stored[mg % 4], 16)

            for g in range(4):
                load(g, g)
            run_steps(sp, step, STEPS, LO, HI - 8, UN)
            for k in range(4):
                sp.wait_ge(o_stored[k], 16 * len(range(k, NG + 1, 4)))

        @block.vector
        def _(dve):
            dve.wait_ge(m_mm, 1)
            dve.tensor_scalar(c["wv"][:, :, :], ps_m[:, :, :], BETA / N, None, ALU.mult).then_inc(wv_ready, 1)
            dve.wait_ge(wv_ready, 1)
            dve.tensor_tensor(wsum[:, :, :], c["wv"][:, :, :], c["wg"][:, :, :], ALU.add).then_inc(wsum_ready, 1)

            def step(s, m):
                g, mg = s - C, m - C
                if exists(g):
                    p, n = shape(g)
                    need(dve, z_mm, g + 1)
                    need(dve, z_ready, g - 1)
                    dve.tensor_tensor(zb[0:p, mg % 2, 0:n, :], ps_z[0:p, mg % 2, 0:n, :], spread(c["bg"], p, n, W),
                                      ALU.add).then_inc(zb_ready, 1)
                g, mg = s - B, m - B
                if exists(g):
                    p, n = shape(g)
                    need(dve, h_turned, g + 1)
                    need(dve, z_mm, g - 1)
                    dve.tensor_copy(hT[:, mg % 2, 0:n, :, 0:p], ps_h[:, 0:n, :, 0:p]).then_inc(hT_ready, 1)
                g, mg = s - O, m - O
                if exists(g):
                    p, n = shape(g)
                    p2 = mg % 2
                    need(dve, nrm_ready, g + 1)
                    dve.tensor_scalar(nrm[0:p, p2, 0:n], nrm[0:p, p2, 0:n], EPS_L2, None, ALU.max).then_inc(nmax_ready, 1)
                    need(dve, nmax_ready, g + 1)
                    dve.reciprocal(inv[0:p, p2, 0:n], nrm[0:p, p2, 0:n]).then_inc(inv_ready, 1)
                    need(dve, inv_ready, g + 1)
                    if not isinstance(g, int) or g >= 4:
                        dve.wait_ge(o_stored[mg % 4], dma_count(g - 4, mg % 4, 4))
                    for k in range(n):
                        o = dve.scalar_tensor_tensor(out=o_sb[0:p, mg % 4, k, :], in0=z[0:p, p2, k, :],
                                                     scalar=inv[0:p, p2, k:k + 1], in1=x2[0:p, mg % 8, k, 0:W],
                                                     op0=ALU.mult, op1=ALU.add)
                    o.then_inc(o_ready, 1)

            run_steps(dve, step, STEPS, LO, HI, UN)

        @block.scalar
        def _(act):
            def step(s, m):
                g, mg = s - B, m - B
                if exists(g):
                    p, n = shape(g)
                    act.wait_ge(x_loaded[mg % 8], dma_count(g, mg % 8, 8))
                    need(act, h_turned, g - 1)
                    for k in range(n):
                        row = x2[0:p, mg % 8, k, :]
                        o = nc.scalar.activation(h[0:p, mg % 2, k, :], row[:, 0:W], ACT.Relu,
                                                 bias=row[:, W + 1:W + 2], scale=row[:, W:W + 1])
                    o.then_inc(h_ready, 1)
                g, mg = s - C, m - C
                if exists(g):
                    p, n = shape(g)
                    p2 = mg % 2
                    need(act, zb_ready, g + 1)
                    need(act, o_ready, g - 1)
                    nc.scalar.activation(z[0:p, p2, 0:n, :], zb[0:p, p2, 0:n, :], ACT.Relu).then_inc(z_ready, 1)
                    need(act, z_ready, g + 1)
                    need(act, ss_ready, g)
                    for k in range(n):
                        o = nc.scalar.activation(zsq[0:p, k, :], z[0:p, p2, k, :], ACT.Square, accum_out=ss[0:p, p2, k:k + 1])
                    o.then_inc(ss_ready, 1)
                    need(act, ss_ready, g + 1)
                    need(act, inv_ready, g - 1)
                    nc.scalar.activation(nrm[0:p, p2, 0:n], ss[0:p, p2, 0:n], ACT.Sqrt).then_inc(nrm_ready, 1)

            run_steps(act, step, STEPS - 1, LO, HI, UN)

        @block.tensor
        def _(pe):
            for i in range(2):
                for k in range(2):
                    o = pe.matmul(ps_m[:, i, :], c["hth"][:, k, i * P:(i + 1) * P], c["wv"][:, k, :],
                                  start=i == 0 and k == 0, stop=i == 1 and k == 1, skip_group_check=True)
            o.then_inc(m_mm, 1)
            pe.wait_ge(wsum_ready, 1)

            def step(s, m):
                g, mg = s - B, m - B
                if exists(g):
                    p, n = shape(g)
                    need(pe, h_ready, g + 1)
                    need(pe, hT_ready, g)
                    for k in range(n):
                        for i in range(2):
                            o = pe.transpose(ps_h[:, k, i, 0:p], h[0:p, mg % 2, k, i * P:(i + 1) * P], c["ident"][0:p, 0:p])
                    o.then_inc(h_turned, 1)
                g, mg = s - C, m - C
                if exists(g):
                    product(g, mg)

            def product(g, mg):
                p, n = shape(g)
                need(pe, hT_ready, g + 1)
                need(pe, zb_ready, g - 1)
                for k in range(n):
                    for i in range(2):
                        o = pe.matmul(ps_z[0:p, mg % 2, k, :], hT[:, mg % 2, k, i, 0:p], wsum[:, i, :],
                                      start=i == 0, stop=i == 1)
                o.then_inc(z_mm, 1)

            run_steps(pe, step, STEPS - 1, LO, HI, UN)


def edge_gcn(nc, c, t):
    UN, LO, HI = 8, 9, 49
    B, C, Q, O, SC = 1, 2, 3, 4, 5
    STEPS = EG + SC
    with ExitStack() as ctx:
        def sb(name, shape, dt=F32):
            return ctx.enter_context(nc.sbuf_tensor("g_" + name, shape, dt))

        def ps(name, shape):
            return ctx.enter_context(nc.psum_tensor("g_" + name, shape, F32))

        sem = phase_sems(nc, ctx, "_g")
        idx = sb("gather_idx", [P, 4, 2, ET], I32)
        fidx = sb("final_idx", [P, 4, ET], I32)
        srow = sb("src_rows", [P, 2, ET, XW])
        drow = sb("dst_rows", [P, 4, ET, XW])
        keys = sb("keys", [P, 2, ET * P])
        kc = sb("key_cols", [P, 2, ET + 1])
        S = sb("same_dst", [P, 2, ET, P])
        cm = sb("carry_to", [P, 2, ET, P])
        hs = sb("hs", [P, 2, ET, W])
        carry = sb("carry", [P, ET, W])
        hd = sb("hd", [P, ET, W])
        sums = sb("sums", [P, ET, W])
        both = sb("both", [P, ET, 2, 2, P])
        zb = sb("zb", [P, ET, W])
        z = sb("z", [P, 2, ET, W])
        zsq = sb("zsq", [P, ET, W])
        ss = sb("ss", [P, 2, ET])
        nrm = sb("nrm", [P, 2, ET])
        inv = sb("inv", [P, 2, ET])
        o_sb = sb("o_sb", [P, 4, ET, W])
        ps_a = ps("ps_a", [P, ET, W])
        ps_t = ps("ps_t", [P, ET, 2, 2, P])
        ps_z = ps("ps_z", [P, ET, W])

        s_loaded = [sem(f"s_loaded{i}") for i in range(2)]
        d_loaded = [sem(f"d_loaded{i}") for i in range(4)]
        keys_loaded = [sem(f"keys_loaded{i}") for i in range(2)]
        new_stored = [sem(f"new_stored{i}") for i in range(4)]
        (sp_passed, pool_passed, idx_ready, fidx_ready, kc_ready, S_ready, hs_ready, agg_mm, carry_ready, hd_ready,
         sums_ready, own_ready, hd_turned, sums_turned, both_ready, z_mm, zb_ready, z_ready, ss_ready, nrm_ready,
         nmax_ready, inv_ready, o_ready) = (sem(s) for s in (
            "sp_passed", "pool_passed", "idx_ready", "fidx_ready", "kc_ready", "S_ready", "hs_ready", "agg_mm",
            "carry_ready", "hd_ready", "sums_ready", "own_ready", "hd_turned", "sums_turned", "both_ready", "z_mm",
            "zb_ready", "z_ready", "ss_ready", "nrm_ready", "nmax_ready", "inv_ready", "o_ready"))
        block = ctx.enter_context(nc.Block())

        def exists(g):
            return not isinstance(g, int) or 0 <= g < EG

        @block.sync
        def _(sp):
            def step(s, m):
                pace(sp, sp_passed, S_ready, s - 1)
                sp.dma_start(keys[:, m % 2, :], t["KEYROW"][1, bass.ds(s * (ET * P), ET * P)].partition_broadcast(P)
                             ).then_inc(keys_loaded[m % 2], 16)

            run_steps(sp, step, EG, LO, HI, UN)

        @block.gpsimd
        def _(pool):
            bound = pool.to_reg(N - 1)

            def gather(tile, slot, kind, islot, loaded):
                for j in range(ET):
                    pool.indirect_dma_start(tile[:, slot, j, :], None, t["X2"][:, :],
                                            bass.IndirectOffsetOnAxis(idx[:, islot, kind, j:j + 1], 0)
                                            ).then_inc(loaded[slot], 16)

            def step(s, m):
                if exists(s):
                    if not isinstance(s, int) or s >= 4:
                        pool.wait_ge(d_loaded[m % 4], dma_count(s - 4, m % 4, 4, 16 * ET))
                        pool.sem_inc(pool_passed, 1)
                    if not isinstance(s, int) or s >= 2:
                        pool.wait_ge(s_loaded[m % 2], dma_count(s - 2, m % 2, 2, 16 * ET))
                        pool.sem_inc(pool_passed, 1)
                    pool.tensor_copy(idx[:, m % 4, 0, :], c["keyI"][:, 1, bass.ds(s * ET, ET)])
                    pool.tensor_copy(idx[:, m % 4, 1, :], c["otherI"][:, 1, bass.ds(s * ET, ET)]).then_inc(idx_ready, 1)
                    pace(pool, pool_passed, idx_ready, s + 1)
                    pace(pool, pool_passed, hs_ready, s - 1)
                    gather(srow, m % 2, 1, m % 4, s_loaded)
                    pace(pool, pool_passed, o_ready, s - 3)
                    gather(drow, m % 4, 0, m % 4, d_loaded)
                g, mg = s - SC, m - SC
                if exists(g):
                    if not isinstance(g, int) or g >= 4:
                        pool.wait_ge(new_stored[mg % 4], dma_count(g - 4, mg % 4, 4, 16 * ET))
                        pool.sem_inc(pool_passed, 1)
                    pool.tensor_copy(fidx[:, mg % 4, :], c["finI"][:, 1, bass.ds(g * ET, ET)]).then_inc(fidx_ready, 1)
                    pace(pool, pool_passed, fidx_ready, g + 1)
                    pace(pool, pool_passed, o_ready, g + 1)
                    for j in range(ET):
                        pool.indirect_dma_start(t["out"][:, :], bass.IndirectOffsetOnAxis(fidx[:, mg % 4, j:j + 1], 0),
                                                o_sb[:, mg % 4, j, :], None,
                                                bounds_check=bound, oob_is_err=False).then_inc(new_stored[mg % 4], 16)

            run_steps(pool, step, STEPS, LO, HI, UN)
            for k in range(4):
                pool.wait_ge(new_stored[k], 16 * ET * len(range(k, EG, 4)))

        @block.vector
        def _(dve):
            def step(s, m):
                g, mg = s - O, m - O
                if exists(g):
                    p2 = mg % 2
                    need(dve, nrm_ready, g + 1)
                    dve.tensor_scalar(nrm[:, p2, :], nrm[:, p2, :], EPS_L2, None, ALU.max).then_inc(nmax_ready, 1)
                    need(dve, nmax_ready, g + 1)
                    dve.reciprocal(inv[:, p2, :], nrm[:, p2, :]).then_inc(inv_ready, 1)
                    need(dve, inv_ready, g + 1)
                    if not isinstance(g, int) or g >= 4:
                        dve.wait_ge(new_stored[mg % 4], dma_count(g - 4, mg % 4, 4, 16 * ET))
                    for j in range(ET):
                        o = dve.scalar_tensor_tensor(out=o_sb[:, mg % 4, j, :], in0=z[:, p2, j, :],
                                                     scalar=inv[:, p2, j:j + 1], in1=drow[:, mg % 4, j, 0:W],
                                                     op0=ALU.mult, op1=ALU.add)
                    o.then_inc(o_ready, 1)
                g, mg = s - B, m - B
                if exists(g):
                    p2 = mg % 2
                    lo = 1 if isinstance(g, int) and g == 0 else 0
                    if lo:
                        dve.memset(kc[:, p2, 0:1], -1.0)
                    dve.tensor_copy(kc[:, p2, lo:], c["ek"][:, 0, 1, bass.ds(g * ET - 1 + lo, ET + 1 - lo)]).then_inc(kc_ready, 1)
                    need(dve, kc_ready, g + 1)
                    dve.wait_ge(keys_loaded[p2], dma_count(g, p2, 2))
                    need(dve, agg_mm, (g - 1) * ET)
                    for j in range(ET):
                        kj = keys[:, p2, j * P:(j + 1) * P]
                        dve.tensor_scalar(S[:, p2, j, :], kj, kc[:, p2, j + 1:j + 2], None, ALU.is_equal)
                        o = dve.tensor_scalar(cm[QUAD:, p2, j, :], kj[QUAD:, :], kc[QUAD:, p2, j:j + 1],
                                              c["e127"][QUAD:, :], ALU.is_equal, ALU.mult)
                    o.then_inc(S_ready, 1)
                g, mg = s - C, m - C
                if exists(g):
                    need(dve, carry_ready, (g + 1) * ET)
                    need(dve, hd_ready, g + 1)
                    need(dve, sums_turned, g)
                    for j in range(ET):
                        dinv = drow[:, mg % 4, j, W + 4:W + 5]
                        o = dve.scalar_tensor_tensor(out=sums[:, j, :], in0=hd[:, j, :], scalar=dinv,
                                                     in1=ps_a[:, j, :], op0=ALU.mult, op1=ALU.add)
                    o.then_inc(sums_ready, 1)
                    need(dve, sums_ready, g + 1)
                    for j in range(ET):
                        dinv = drow[:, mg % 4, j, W + 4:W + 5]
                        o = dve.tensor_scalar(sums[:, j, :], sums[:, j, :], dinv, None, ALU.mult)
                    o.then_inc(own_ready, 1)
                    for kind, turned in ((1, hd_turned), (0, sums_turned)):
                        need(dve, turned, g + 1)
                        need(dve, z_mm, g)
                        for b in range(2):
                            o = dve.tensor_copy(both[:, 2 * b:2 * b + 2, kind, :, :], ps_t[:, 2 * b:2 * b + 2, kind, :, :])
                        o.then_inc(both_ready, 1)
                g, mg = s - Q, m - Q
                if exists(g):
                    need(dve, z_mm, g + 1)
                    need(dve, z_ready, g)
                    dve.tensor_tensor(zb[:, :, :], ps_z[:, :, :], spread(c["bg"], P, ET, W), ALU.add).then_inc(zb_ready, 1)

            run_steps(dve, step, EG + O, LO, HI, UN)

        @block.scalar
        def _(act):
            def step(s, m):
                g, mg = s - B, m - B
                if exists(g):
                    act.wait_ge(s_loaded[mg % 2], dma_count(g, mg % 2, 2, 16 * ET))
                    need(act, agg_mm, (g - 1) * ET)
                    for j in range(ET):
                        row = srow[:, mg % 2, j, :]
                        o = nc.scalar.activation(hs[:, mg % 2, j, :], row[:, 0:W], ACT.Relu,
                                                 bias=row[:, W + 3:W + 4], scale=row[:, W + 2:W + 3])
                    o.then_inc(hs_ready, 1)
                g, mg = s - C, m - C
                if exists(g):
                    act.wait_ge(d_loaded[mg % 4], dma_count(g, mg % 4, 4, 16 * ET))
                    need(act, hd_turned, g)
                    need(act, sums_ready, g)
                    for j in range(ET):
                        row = drow[:, mg % 4, j, :]
                        o = nc.scalar.activation(hd[:, j, :], row[:, 0:W], ACT.Relu,
                                                 bias=row[:, W + 1:W + 2], scale=row[:, W:W + 1])
                    o.then_inc(hd_ready, 1)
                    for j in range(ET):
                        need(act, agg_mm, g * ET + j + 1)
                        nc.scalar.copy(carry[QUAD:, j, :], ps_a[QUAD:, j, :]).then_inc(carry_ready, 1)
                g, mg = s - Q, m - Q
                if exists(g):
                    p2 = mg % 2
                    need(act, zb_ready, g + 1)
                    need(act, o_ready, g - 1)
                    nc.scalar.activation(z[:, p2, :, :], zb[:, :, :], ACT.Relu).then_inc(z_ready, 1)
                    need(act, z_ready, g + 1)
                    need(act, ss_ready, g)
                    for j in range(ET):
                        o = nc.scalar.activation(zsq[:, j, :], z[:, p2, j, :], ACT.Square, accum_out=ss[:, p2, j:j + 1])
                    o.then_inc(ss_ready, 1)
                    need(act, ss_ready, g + 1)
                    need(act, inv_ready, g - 1)
                    nc.scalar.activation(nrm[:, p2, :], ss[:, p2, :], ACT.Sqrt).then_inc(nrm_ready, 1)

            run_steps(act, step, EG + Q, LO, HI, UN)

        @block.tensor
        def _(pe):
            def step(s, m):
                g, mg = s - Q, m - Q
                if exists(g):
                    need(pe, both_ready, 2 * g + 2)
                    need(pe, zb_ready, g)
                    for j in range(ET):
                        for kind, w in ((0, c["wg"]), (1, c["wv"])):
                            for i in range(2):
                                o = pe.matmul(ps_z[:, j, :], both[:, j, kind, i, :], w[:, i, :],
                                              start=kind == 0 and i == 0, stop=kind == 1 and i == 1)
                    o.then_inc(z_mm, 1)
                g, mg = s - C, m - C
                if exists(g):
                    p2 = mg % 2
                    need(pe, S_ready, g + 1)
                    need(pe, hs_ready, g + 1)
                    need(pe, sums_ready, g)
                    for j in range(ET):
                        first = isinstance(g, int) and g == 0 and j == 0
                        need(pe, carry_ready, g * ET + j)
                        o = pe.matmul(ps_a[:, j, :], S[:, p2, j, :], hs[:, p2, j, :], start=True, stop=first)
                        if not first:
                            o = pe.matmul(ps_a[:, j, :], cm[QUAD:, p2, j, :], carry[QUAD:, (j - 1) % ET, :],
                                          start=False, stop=True)
                        o.then_inc(agg_mm, 1)
                    for kind, tile, ready, turned in ((1, hd, hd_ready, hd_turned), (0, sums, own_ready, sums_turned)):
                        need(pe, ready, g + 1)
                        need(pe, both_ready, 2 * g + (0 if kind else 1))
                        for j in range(ET):
                            for i in range(2):
                                o = pe.transpose(ps_t[:, j, kind, i, :], tile[:, j, i * P:(i + 1) * P], c["ident"][:, :])
                        o.then_inc(turned, 1)

            run_steps(pe, step, EG + Q, LO, HI, UN)


_INS = ['x', 'src', 'dst', 'L0_gnn_W_P_w', 'L0_gnn_W_P_b', 'L0_gnn_W_pos', 'L0_gnn_q1', 'L0_gnn_k1', 'L0_gnn_v1',
        'L0_gnn_ln1_s', 'L0_gnn_ln1_b', 'L0_gnn_q2', 'L0_gnn_k2', 'L0_gnn_v2', 'L0_gnn_ln2_s', 'L0_gnn_ln2_b',
        'L0_gnn_inv_w', 'L0_gnn_inv_b', 'L1_gnn_W_gcn', 'L1_gnn_b_gcn', 'L1_gnn_W_V']
_OUTS = [((50000, 256), 'float32')]


def kernel(**inputs):
    import numpy as _np
    import concourse.bacc as _bacc
    from concourse import mybir as _mybir
    from concourse.bass_utils import run_bass_kernel_spmd as _run

    nc = _bacc.Bacc("TRN2", target_bir_lowering=False, num_devices=1)
    arrays, args = {}, []
    for name in _INS:
        a = _np.ascontiguousarray(inputs[name])
        arrays[f"in_{name}_dram"] = a
        args.append(nc.dram_tensor(f"in_{name}_dram", a.shape, _mybir.dt.from_np(a.dtype), kind="ExternalInput").ap())
    for i, (shape, dtype) in enumerate(_OUTS):
        dt = _mybir.dt.from_np(_np.dtype(dtype))
        args.append(nc.dram_tensor(f"out_{i}_dram", shape, dt, kind="ExternalOutput").ap())
    program(nc, *args)
    r = _run(nc, [arrays], core_ids=[0])
    got = tuple(r.results[0][f"out_{i}_dram"] for i in range(len(_OUTS)))
    return got[0]
```

```python
from contextlib import ExitStack

import concourse.bass as bass
from concourse import mybir

ALU = mybir.AluOpType
ACT = mybir.ActivationFunctionType
AX_X = mybir.AxisListType.X
F32 = mybir.dt.float32
BF16 = mybir.dt.bfloat16
I32 = mybir.dt.int32

P = 128
QUAD = 96
N = 50000
E = 25000
W = 256
D = 128
HEADS = 8
HD = D // HEADS
NT = -(-E // P)
EP = NT * P
HT = NT // 2
ET = 4
EG = NT // ET
G = 3
NG = N // (G * P)
TAIL = N - NG * G * P
DIG = 256
KEYS = DIG * DIG
EW = D + 4
XW = W + 8
LIST = EP + P
SKIP = 100000.0
EPS_X = 1e-5
EPS_E = 1e-6
EPS_ATT = 1e-8
EPS_L2 = 1e-12
BETA = 0.1
assert TAIL <= P and NT % (2 * ET) == ET and N <= KEYS


def need(eng, sem, count):
    if isinstance(count, int) and count <= 0:
        return
    eng.wait_ge(sem, count)


def pace(eng, passed, sem, count):
    if isinstance(count, int) and count <= 0:
        return
    eng.wait_ge(sem, count)
    eng.sem_inc(passed, 1)


def dma_count(g, slot, slots, per=16):
    return (g - slot) * (per // slots) + per


def phase_sems(nc, ctx, suffix=""):
    held = []

    def close():
        nc.clear_and_free_semaphores(held)
        nc.all_engine_barrier()

    def sem(name):
        held.append(nc.alloc_semaphore(name + suffix))
        return held[-1]

    ctx.callback(close)
    return sem


def run_steps(eng, step, total, lo, hi, unroll):
    assert (hi - lo) % unroll == 0
    for s in range(lo):
        step(s, s % unroll)
    with eng.Fori(lo, hi - unroll + 1, unroll) as i:
        for u in range(unroll):
            step(i + u, (lo + u) % unroll)
    for s in range(hi, total):
        step(s, s % unroll)


def program(nc, x, src, dst, W_P_w, W_P_b, W_pos, q1, k1, v1, ln1_s, ln1_b, q2, k2, v2, ln2_s,
            ln2_b, inv_w, inv_b, W_gcn, b_gcn, W_V, out):
    def dram(name, shape, dt=F32):
        return nc.dram_tensor(name, shape, dt, kind="Internal").ap()

    t = {
        "E0": dram("embed0", [N, EW]), "E1": dram("embed1", [N, EW]), "X2": dram("x2_rows", [N, XW]),
        "SORTED": dram("sorted_pairs", [2 * LIST, 2], I32),
        "DIGROW": dram("key_rows", [2, 2, EP]), "KEYROW": dram("sorted_key_rows", [2, EP]),
        "AUX": dram("node_aux", [2, KEYS]),
        "x": x, "src": src, "dst": dst, "out": out,
    }
    with ExitStack() as ctx:
        def sb(name, shape, dt=F32):
            return ctx.enter_context(nc.sbuf_tensor(name, shape, dt))

        c = {}
        for name, shape in (("ident", [P, P]), ("ones", [P, P]), ("wP", [P, 2, D]), ("bias0", [P, D]),
                            ("qkv1", [P, 3, D]), ("qkv2", [P, 3, D]), ("ln1s", [P, D]), ("ln1b", [P, D]),
                            ("w2", [P, W]), ("w2c", [P, W]), ("bias2", [P, W]), ("wg", [P, 2, W]), ("bg", [P, W]),
                            ("wv", [P, 2, W]), ("hth", [P, 2, W]), ("eps", [P, 2]), ("e127", [P, 1])):
            c[name] = sb(name, shape)
        c["posI"] = sb("posI", [P, 2 * NT], I32)
        c["pairs"] = sb("pairs", [P, 2 * NT, 2], I32)
        c["ek"] = sb("ek", [P, 3, 2, NT])
        c["fin"] = sb("fin", [P, 2, NT])
        for name in ("keyI", "otherI", "finI"):
            c[name] = sb(name, [P, 2, NT], I32)
        weights(nc, c, W_P_w, W_P_b, W_pos, q1, k1, v1, ln1_s, ln1_b, q2, k2, v2, ln2_s, ln2_b,
                inv_w, inv_b, W_gcn, b_gcn, W_V)
        rank_edges(nc, c, t)
        dense_embed(nc, c, t)
        unpack_lists(nc, c, t)
        edge_attention(nc, c, t, 1)
        edge_attention(nc, c, t, 2)
        dense_gcn(nc, c, t)
        edge_gcn(nc, c, t)


def weights(nc, c, W_P_w, W_P_b, W_pos, q1, k1, v1, ln1_s, ln1_b, q2, k2, v2, ln2_s, ln2_b,
            inv_w, inv_b, W_gcn, b_gcn, W_V):
    with ExitStack() as ctx:
        def sb(name, shape, dt=F32):
            return ctx.enter_context(nc.sbuf_tensor(name, shape, dt))

        sem = phase_sems(nc, ctx)

        pos_b = sb("pos_b", [P, D])
        ln2s_col = sb("ln2s_col", [P, 1])
        ln2b_col = sb("ln2b_col", [P, 1])
        ln2b_all = sb("ln2b_all", [P, P])
        invb = sb("invb", [P, W])
        ps_bias = ctx.enter_context(nc.psum_tensor("ps_bias", [P, W], F32))
        ps_mean = ctx.enter_context(nc.psum_tensor("ps_mean", [P, W], F32))
        loaded = sem("weights_loaded")
        ones_set = sem("ones_set")
        ident_set = sem("ident_set")
        col_spread = sem("ln2b_spread")
        bias_mm = sem("bias_mm")
        scaled = sem("w2_scaled")
        mean_mm = sem("w2_mean_mm")
        row = lambda a: a.partition_broadcast(P)
        loads = [
            (c["wP"][:, :, :], W_P_w.rearrange("(h p) n -> p h n", p=P)),
            (c["wg"][:, :, :], W_gcn.rearrange("(h p) n -> p h n", p=P)),
            (c["wv"][:, :, :], W_V.rearrange("(h p) n -> p h n", p=P)),
            (c["w2"][:, :], inv_w), (ln2s_col[:, :], ln2_s.rearrange("(p a) -> p a", a=1)),
            (ln2b_col[:, :], ln2_b.rearrange("(p a) -> p a", a=1)),
            (c["bias0"][:, :], row(W_P_b)), (pos_b[:, :], row(W_pos[0])),
            (c["ln1s"][:, :], row(ln1_s)), (c["ln1b"][:, :], row(ln1_b)),
            (invb[:, :], row(inv_b)), (c["bg"][:, :], row(b_gcn)),
        ]
        for name, ws in (("qkv1", (q1, k1, v1)), ("qkv2", (q2, k2, v2))):
            loads += [(c[name][:, i, :], w) for i, w in enumerate(ws)]
        block = ctx.enter_context(nc.Block())

        @block.sync
        def _(sp):
            for o, i in loads:
                sp.dma_start(o, i).then_inc(loaded, 16)

        @block.gpsimd
        def _(pool):
            pool.memset(c["ones"][:, :], 1.0).then_inc(ones_set, 1)
            pool.memset(c["eps"][:, 0:1], EPS_X)
            pool.memset(c["eps"][:, 1:2], EPS_E)
            pool.wait_ge(ones_set, 1)
            pool.affine_select(out=c["ident"][:, :], in_=c["ones"][:, :], compare_op=ALU.is_equal, fill=0.0,
                               base=0, pattern=[[1, P]], channel_multiplier=-1)
            pool.affine_select(out=c["e127"][:, :], in_=c["ones"][:, 0:1], compare_op=ALU.is_equal, fill=0.0,
                               base=1 - P, pattern=[[0, 1]], channel_multiplier=1).then_inc(ident_set, 1)

        @block.vector
        def _(dve):
            dve.wait_ge(loaded, 16 * len(loads))
            dve.wait_ge(ones_set, 1)
            dve.tensor_scalar(ln2b_all[:, :], c["ones"][:, :], ln2b_col[:, :], None, ALU.mult).then_inc(col_spread, 1)
            dve.tensor_tensor(c["bias0"][:, :], c["bias0"][:, :], pos_b[:, :], ALU.add)
            dve.wait_ge(bias_mm, 1)
            dve.tensor_tensor(c["bias2"][:, :], ps_bias[:, :], invb[:, :], ALU.add)
            dve.tensor_scalar(c["w2"][:, :], c["w2"][:, :], ln2s_col[:, :], None, ALU.mult).then_inc(scaled, 1)
            dve.wait_ge(mean_mm, 1)
            dve.scalar_tensor_tensor(out=c["w2c"][:, :], in0=ps_mean[:, :], scalar=-1.0 / D, in1=c["w2"][:, :],
                                     op0=ALU.mult, op1=ALU.add)

        @block.tensor
        def _(pe):
            pe.wait_ge(col_spread, 1)
            pe.matmul(ps_bias[:, :], ln2b_all[:, :], c["w2"][:, :], start=True, stop=True).then_inc(bias_mm, 1)
            pe.wait_ge(scaled, 1)
            pe.matmul(ps_mean[:, :], c["ones"][:, :], c["w2"][:, :], start=True, stop=True).then_inc(mean_mm, 1)


def rank_edges(nc, c, t):
    with ExitStack() as ctx:
        def sb(name, shape, dt=F32):
            return ctx.enter_context(nc.sbuf_tensor(name, shape, dt))

        def ps(name, shape):
            return ctx.enter_context(nc.psum_tensor(name, shape, F32))

        sem = phase_sems(nc, ctx)

        keyT = sb("keyT", [HT, 2, 2, P], I32)
        digT = sb("digT", [HT, 2, 2, 2, P], I32)
        keyTF = sb("keyTF", [HT, 3, 2, 2, P])
        ke = sb("ke", [P, 3, 2, NT])
        iota = sb("iota_digit", [P, DIG], BF16)
        pcol = sb("pcol", [P, 2])
        below = sb("below", [P, P])
        earlier = sb("earlier", [P, ET * P])
        oh = sb("onehot", [P, 2 * ET, 2, DIG], BF16)
        cnt = sb("cnt", [P, 2, 2, DIG])
        inc = sb("inc", [P, 2, 2, DIG])
        onesw = sb("onesw", [P, DIG])
        aux = sb("aux_out", [P, 2, 2, DIG])
        base = sb("base", [P, 4])
        start = sb("start", [P, 2, 2, DIG])
        seen = sb("seen", [P, 2, 2, DIG])
        krow = sb("krow", [P, 2, ET * P])
        hrow = sb("hrow", [P, 2, ET * P])
        ohT = sb("onehotT", [P, 2, 2, ET * P])
        dupj = sb("dup_junk", [P, ET, ET * P])
        selj = sb("sel_junk", [P, ET, DIG])
        dup = sb("dup", [P, ET])
        sel = sb("sel", [P, ET])
        pos = sb("pos", [P, 2 * NT])
        sentinel = sb("sentinel", [2, 2], I32)
        hist = [ps(f"hist{i}", [P, 512]) for i in range(4)]
        rows = ps("rows", [P, ET, DIG])
        runs = [ps(f"runs{i}", [P, 512]) for i in range(2)]

        padded = sem("keys_padded")
        loaded = sem("keys_loaded")
        digits = sem("digits")
        floats = sem("floats")
        rows_stored = sem("key_rows_stored")
        consts = sem("rank_consts")
        turned = sem("keys_turned")
        ke_ready = sem("ke_ready")
        oh_ready = sem("onehot_ready")
        oh_used = sem("onehot_used")
        cnt_ready = sem("cnt_ready")
        aux_ready = sem("aux_ready")
        aux_root = sem("aux_root")
        aux_stored = sem("aux_stored")
        scanned = sem("scanned")
        base_mm = sem("base_mm")
        base_ready = sem("base_ready")
        start_ready = sem("start_ready")
        krow_loaded = [sem(f"krow_loaded{i}") for i in range(2)]
        sp_passed = sem("rank_sp_passed")
        ohT_ready = sem("onehotT_ready")
        dup_ready = sem("dup_ready")
        rows_ready = sem("rows_ready")
        sel_ready = sem("sel_ready")
        oh2_ready = sem("onehot2_ready")
        run_ready = sem("run_ready")
        seen_ready = sem("seen_ready")
        pos_ready = sem("pos_ready")
        block = ctx.enter_context(nc.Block())

        def rank_steps(eng, step, l):
            for b in range(l * EG, l * EG + 3):
                step(b, b, l)
            with eng.Fori(l * EG + 3, (l + 1) * EG - 1, 2) as i:
                for u in range(2):
                    step(i + u, l * EG + 3 + u, l)

        @block.sync
        def _(sp):
            sp.wait_ge(padded, 1)
            full = (NT - 1) * P
            for l, a in enumerate((t["src"], t["dst"])):
                sp.dma_start(keyT[:, l, 0, :], a[0:HT * P].rearrange("(r c) -> r c", c=P)).then_inc(loaded, 16)
                sp.dma_start(keyT[0:HT - 1, l, 1, :], a[HT * P:full].rearrange("(r c) -> r c", c=P)).then_inc(loaded, 16)
                sp.dma_start(keyT[HT - 1:HT, l, 1, 0:E - full], a[full:E].rearrange("(r c) -> r c", r=1)).then_inc(loaded, 16)
            sp.wait_ge(floats, 2)
            for kind in range(2):
                for l in range(2):
                    sp.dma_start(t["DIGROW"][kind, l].rearrange("(a r c) -> r a c", a=2, c=P),
                                 keyTF[:, kind, l, :, :]).then_inc(rows_stored, 16)
            for l in range(2):
                sp.dma_start(t["SORTED"][l * LIST + EP:l * LIST + EP + 2, :], sentinel[:, :]).then_inc(rows_stored, 16)
            sp.wait_ge(rows_stored, 96)

            def step(b, m, l):
                pace(sp, sp_passed, dup_ready, b - 1)
                off = (b - l * EG) * (ET * P)
                for tile, kind in ((krow, 0), (hrow, 1)):
                    sp.dma_start(tile[:, m % 2, :], t["DIGROW"][kind, l, bass.ds(off, ET * P)].partition_broadcast(P)
                                 ).then_inc(krow_loaded[m % 2], 16)

            step(0, 0, 0)
            step(1, 1, 0)
            for l in range(2):
                if l == 1:
                    step(EG, EG, 1)
                    step(EG + 1, EG + 1, 1)
                lo = l * EG + 2
                with sp.Fori(lo, (l + 1) * EG - 2, 2) as i:
                    for u in range(2):
                        step(i + u, lo + u, l)
                step((l + 1) * EG - 1, (l + 1) * EG - 1, l)
            sp.wait_ge(aux_ready, 2)
            for k in range(2):
                sp.dma_start(t["AUX"][k].rearrange("(h p l) -> p h l", h=2, l=DIG), aux[:, k, :, :]).then_inc(aux_stored, 16)
            sp.wait_ge(aux_stored, 32)

        @block.gpsimd
        def _(pool):
            pool.iota(iota[:, :], [[1, DIG]], base=0, channel_multiplier=0, allow_small_or_imprecise_dtypes=True)
            for h in range(2):
                pool.iota(pcol[:, h:h + 1], [[0, 1]], base=h * P, channel_multiplier=1,
                          allow_small_or_imprecise_dtypes=True)
            pool.memset(onesw[:, :], 1.0)
            pool.memset(earlier[:, 0:(ET - 1) * P], 1.0)
            pool.affine_select(out=below[:, :], in_=c["ones"][:, :], compare_op=ALU.is_gt, fill=0.0,
                               base=0, pattern=[[1, P]], channel_multiplier=-1)
            pool.affine_select(out=earlier[:, (ET - 1) * P:], in_=c["ones"][:, :], compare_op=ALU.is_gt, fill=0.0,
                               base=0, pattern=[[-1, P]], channel_multiplier=1).then_inc(consts, 1)

        @block.vector
        def _(dve):
            dve.memset(sentinel[:, :], 2 * N)
            dve.memset(keyT[:, :, :, :], N).then_inc(padded, 1)
            dve.wait_ge(loaded, 96)
            dve.tensor_scalar(digT[:, 0, :, :, :], keyT[:, :, :, :], 8, None, ALU.logical_shift_right)
            dve.tensor_scalar(digT[:, 1, :, :, :], keyT[:, :, :, :], 255, None, ALU.bitwise_and).then_inc(digits, 1)
            dve.tensor_copy(keyTF[:, 0, :, :, :], keyT[:, :, :, :]).then_inc(floats, 1)
            dve.wait_ge(digits, 1)
            dve.tensor_copy(keyTF[:, 1, :, :, :], digT[:, 0, :, :, :]).then_inc(floats, 1)
            dve.tensor_copy(keyTF[:, 2, :, :, :], digT[:, 1, :, :, :]).then_inc(floats, 1)
            dve.wait_ge(ke_ready, 3)
            for copy in range(2):
                for l in range(2):
                    dve.tensor_copy(c["pairs"][:, copy * NT:(copy + 1) * NT, l], ke[:, 0, l, :])
            dve.wait_ge(consts, 1)

            def onehots(tile, j, l, ready):
                for d in range(2):
                    o = dve.tensor_scalar(oh[:, j, d, :], iota[:, :], ke[:, 1 + d, l, bass.ds(tile, 1)], None, ALU.is_equal)
                o.then_inc(ready, 1)

            def count_tiles(base_tile, l, first):
                for j in range(ET):
                    n = base_tile + j + l * NT
                    if not first:
                        need(dve, oh_used, n + 1 - ET)
                    onehots(base_tile + j, j, l, oh_ready)

            for l in range(2):
                count_tiles(0, l, l == 0)
                with dve.Fori(ET, NT - 2 * ET + 1, ET) as i:
                    count_tiles(i, l, False)
                count_tiles(NT - ET, l, False)

            dve.wait_ge(oh_used, 2 * NT)
            for l in range(2):
                for h in range(2):
                    o = dve.tensor_copy(cnt[:, l, h, :], hist[2 * l + h][:, 0:DIG])
            o.then_inc(cnt_ready, 1)
            dve.wait_ge(cnt_ready, 1)
            dve.tensor_scalar(aux[:, 0, :, :], cnt[:, 0, :, :], 0.0, None, ALU.is_equal).then_inc(aux_ready, 1)
            dve.tensor_scalar(aux[:, 1, :, :], cnt[:, 1, :, :], 1.0, 1e-30, ALU.add, ALU.max).then_inc(aux_root, 1)
            for l in range(2):
                for h in range(2):
                    o = dve.tensor_tensor_scan(inc[:, l, h, :], onesw[:, :], cnt[:, l, h, :], 0.0, ALU.mult, ALU.add)
            o.then_inc(scanned, 1)
            dve.wait_ge(aux_root, 2)
            dve.reciprocal(aux[:, 1, :, :], aux[:, 1, :, :]).then_inc(aux_ready, 1)
            dve.wait_ge(base_mm, 1)
            dve.tensor_copy(base[:, :], rows[:, 0, 0:4]).then_inc(base_ready, 1)
            dve.wait_ge(base_ready, 1)
            dve.wait_ge(scanned, 1)
            for l in range(2):
                for h in range(2):
                    o = dve.scalar_tensor_tensor(out=start[:, l, h, :], in0=inc[:, l, h, :],
                                                 scalar=base[:, 2 * l + h:2 * l + h + 1], in1=cnt[:, l, h, :],
                                                 op0=ALU.add, op1=ALU.subtract)
            o.then_inc(start_ready, 1)

            def step(b, m, l):
                slot = m % 2
                tile = (b - l * EG) * ET
                dve.wait_ge(krow_loaded[slot], dma_count(b, slot, 2, 32))
                need(dve, rows_ready, b - 1)
                for h in range(2):
                    o = dve.tensor_scalar(ohT[:, slot, h, :], hrow[:, slot, :], pcol[:, h:h + 1], None, ALU.is_equal)
                o.then_inc(ohT_ready, 1)
                need(dve, run_ready, b - 1)
                for j in range(ET):
                    onehots(tile + j, slot * ET + j, l, oh2_ready)
                need(dve, pos_ready, b)
                for j in range(ET):
                    w = (j + 1) * P
                    o = dve.scalar_tensor_tensor(out=dupj[:, j, 0:w], in0=krow[:, slot, 0:w],
                                                 scalar=ke[:, 0, l, bass.ds(tile + j, 1)],
                                                 in1=earlier[:, (ET - 1 - j) * P:], op0=ALU.is_equal,
                                                 op1=ALU.mult, accum_out=dup[:, j:j + 1])
                o.then_inc(dup_ready, 1)
                need(dve, rows_ready, b + 1)
                need(dve, oh2_ready, (b + 1) * ET)
                for j in range(ET):
                    o = dve.tensor_tensor_reduce(out=selj[:, j, :], in0=rows[:, j, :], in1=oh[:, slot * ET + j, 1, :],
                                                 scale=1.0, scalar=0.0, op0=ALU.mult, op1=ALU.add,
                                                 accum_out=sel[:, j:j + 1])
                o.then_inc(sel_ready, 1)
                need(dve, sel_ready, b + 1)
                need(dve, dup_ready, b + 1)
                dve.tensor_tensor(pos[:, bass.ds(b * ET, ET)], sel[:, :], dup[:, :], ALU.add).then_inc(pos_ready, 1)

            dve.wait_ge(start_ready, 1)
            for l in range(2):
                rank_steps(dve, step, l)
            dve.wait_ge(pos_ready, 2 * EG)
            dve.tensor_copy(c["posI"][:, 0:NT], pos[:, 0:NT])
            dve.tensor_scalar(c["posI"][:, NT:], pos[:, NT:], float(LIST), None, ALU.add)

        @block.scalar
        def _(act):
            for kind in range(3):
                act.wait_ge(turned, kind + 1)
                nc.scalar.copy(ke[:, kind, :, :].rearrange("p l t -> p (l t)"), hist[kind][:, 0:2 * NT]).then_inc(ke_ready, 1)
            act.wait_ge(aux_root, 1)
            nc.scalar.activation(aux[:, 1, :, :], aux[:, 1, :, :], ACT.Sqrt).then_inc(aux_root, 1)

            def step(b, m, l):
                need(act, run_ready, b + 1)
                need(act, rows_ready, b)
                for h in range(2):
                    o = nc.scalar.copy(seen[:, (m + 1) % 2, h, :], runs[h][:, 0:DIG])
                o.then_inc(seen_ready, 1)

            for l in range(2):
                rank_steps(act, step, l)

        @block.tensor
        def _(pe):
            for kind in range(3):
                pe.wait_ge(floats, kind + 1)
                for l in range(2):
                    for a in range(2):
                        at = (l * 2 + a) * HT
                        o = pe.transpose(hist[kind][:, at:at + HT], keyTF[:, kind, l, a, :], c["ident"][0:HT, 0:HT])
                o.then_inc(turned, 1)
            pe.wait_ge(ke_ready, 3)

            def count(base_tile, l, first, last):
                for j in range(ET):
                    n = base_tile + j + l * NT
                    need(pe, oh_ready, n + 1)
                    for h in range(2):
                        o = pe.matmul(hist[2 * l + h][:, 0:DIG], oh[:, j, 0, h * P:(h + 1) * P], oh[:, j, 1, :],
                                      start=first and j == 0, stop=last and j == ET - 1)
                    o.then_inc(oh_used, 1)

            for l in range(2):
                count(0, l, True, False)
                with pe.Fori(ET, NT - 2 * ET + 1, ET) as i:
                    count(i, l, False, False)
                count(NT - ET, l, False, True)
            pe.wait_ge(scanned, 1)
            pe.wait_ge(consts, 1)
            for l in range(2):
                pe.matmul(rows[:, 0, 2 * l:2 * l + 1], below[:, :], inc[:, l, 0, DIG - 1:DIG], start=True, stop=True)
                pe.matmul(rows[:, 0, 2 * l + 1:2 * l + 2], below[:, :], inc[:, l, 1, DIG - 1:DIG], start=True, stop=False)
                o = pe.matmul(rows[:, 0, 2 * l + 1:2 * l + 2], c["ones"][:, :], inc[:, l, 0, DIG - 1:DIG],
                              start=False, stop=True)
            o.then_inc(base_mm, 1)
            pe.wait_ge(start_ready, 1)

            def step(b, m, l):
                slot = m % 2
                first = m == l * EG
                need(pe, ohT_ready, b + 1)
                need(pe, seen_ready, b)
                need(pe, sel_ready, b)
                table = start[:, l, :, :] if first else seen[:, slot, :, :]
                for j in range(ET):
                    for h in range(2):
                        o = pe.matmul(rows[:, j, :], ohT[:, slot, h, j * P:(j + 1) * P], table[:, h, :],
                                      start=(h == 0 and j % 2 == 0), stop=(h == 1), skip_group_check=True)
                o.then_inc(rows_ready, 1)
                need(pe, oh2_ready, (b + 1) * ET)
                for h in range(2):
                    if first:
                        pe.matmul(runs[h][:, 0:DIG], c["ident"][:, :], start[:, l, h, :], start=True, stop=False,
                                  skip_group_check=True)
                    for j in range(ET):
                        o = pe.matmul(runs[h][:, 0:DIG], oh[:, slot * ET + j, 0, h * P:(h + 1) * P],
                                      oh[:, slot * ET + j, 1, :], start=False, stop=j == ET - 1, skip_group_check=True)
                o.then_inc(run_ready, 1)

            for l in range(2):
                rank_steps(pe, step, l)


def spread(row, p, n, w):
    return row[0:p, :].unsqueeze(1).to_broadcast([p, n, w])


def dense_embed(nc, c, t):
    UN = 8
    LO, SCATTER_LO, SCATTER_HI, HI = 16, 8, 96, 128
    A, B, Z, L, M, X, R, H, T = range(9)
    STEPS = NG + 1 + T
    with ExitStack() as ctx:
        def sb(name, shape, dt=F32):
            return ctx.enter_context(nc.sbuf_tensor(name, shape, dt))

        def ps(name, shape):
            return ctx.enter_context(nc.psum_tensor(name, shape, F32))

        sem = phase_sems(nc, ctx)
        xt = sb("xt", [P, UN, G, W])
        h0 = sb("h0", [P, 2, G, W])
        hT = sb("hT", [P, 2, G, 2, P])
        e0 = sb("e0", [P, 4, G, EW])
        n1 = sb("n1", [P, 2, G, D])
        e1 = sb("e1", [P, 4, G, EW])
        e1T = sb("e1T", [P, 2, G, P])
        x2 = sb("x2", [P, 4, G, XW])
        r = sb("r", [P, 4, G, W])
        rsq = sb("rsq", [P, G, W])
        rw = sb("rw", [P, 2, G, W])
        SX, SX2, SE0, SE1 = range(4)
        st = sb("st", [P, 4, G, 6])
        mv = sb("mv", [P, 4, 4, G, 2])
        nmean = sb("nmean", [P, 4, 4, G])
        std = sb("std", [P, 4, 4, G])
        rstd = sb("rstd", [P, 4, 4, G])
        ss = sb("ss", [P, 2, G])
        root = sb("root", [P, 2, G])
        nrm = sb("nrm", [P, 2, 2, G])
        inv = sb("inv", [P, 2, G])
        k = sb("k", [P, 2, G])
        kn = sb("kn", [P, 2, G])
        w = sb("w", [P, 2, G])
        aux = sb("aux", [P, 2, (NG + 1) * G])
        idx = sb("scatter_idx", [P, 4, ET], I32)
        pay = sb("scatter_pairs", [P, 4, ET, 2], I32)
        ps_h = ps("ps_h", [P, 4, 2, P])
        ps_z = ps("ps_z", [P, 4, D])
        ps_e = ps("ps_e", [P, 4, D])
        ps_x = ps("ps_x", [P, 4, W])
        ps_hth = ps("ps_hth", [P, 2, W])

        x_loaded = [sem(f"x_loaded{i}") for i in range(UN)]
        e0_stored = [sem(f"e0_stored{i}") for i in range(4)]
        e1_stored = [sem(f"e1_stored{i}") for i in range(4)]
        x2_stored = [sem(f"x2_stored{i}") for i in range(4)]
        pair_stored = [sem(f"pair_stored{i}") for i in range(4)]
        aux_loaded = sem("aux_loaded")
        sp_passed = sem("embed_sp_passed")
        pool_passed = sem("embed_pool_passed")
        dve_passed = sem("embed_dve_passed")
        cleared = sem("cleared")
        stat = [sem(f"stat{i}") for i in range(4)]
        mv_ready = sem("mv_ready")
        nmean_ready = sem("nmean_ready")
        std_ready = sem("std_ready")
        rstd_ready = sem("rstd_ready")
        h0_ready = sem("h0_ready")
        h0_turned = sem("h0_turned")
        hT_ready = sem("hT_ready")
        z_mm = sem("z_mm")
        e0_ready = sem("e0_ready")
        e0_aux = sem("e0_aux")
        n1_ready = sem("n1_ready")
        e1_scaled = sem("e1_scaled")
        e1_ready = sem("e1_ready")
        e1_turned = sem("e1_turned")
        e1T_ready = sem("e1T_ready")
        x2_mm = sem("x2_mm")
        xb_ready = sem("xb_ready")
        x2_ready = sem("x2_ready")
        r_ready = sem("r_ready")
        ss_ready = sem("ss_ready")
        root_ready = sem("root_ready")
        nrm_ready = sem("nrm_ready")
        nmax_ready = sem("nmax_ready")
        inv_ready = sem("inv_ready")
        k_ready = sem("k_ready")
        kn_ready = sem("kn_ready")
        w_ready = sem("w_ready")
        rw_ready = sem("rw_ready")
        hth_mm = sem("hth_mm")
        b_ready = sem("b_ready")
        row_ready = sem("row_ready")
        idx_ready = sem("idx_ready")
        block = ctx.enter_context(nc.Block())

        def exists(g):
            return not isinstance(g, int) or 0 <= g <= NG

        def shape(g):
            return (TAIL, 1) if isinstance(g, int) and g == NG else (P, G)

        def nodes(ap, g):
            p, n = shape(g)
            return ap[bass.ds(g * (P * G), p * n), :].rearrange("(p k) c -> p k c", k=n)

        def stored(eng, sems, g, m, passed=None):
            if not isinstance(g, int) or g >= 4:
                eng.wait_ge(sems[m % 4], dma_count(g - 4, m % 4, 4))
                if passed is not None:
                    eng.sem_inc(passed, 1)

        def measured(s):
            return not isinstance(s, int) or 0 <= s <= NG + X

        @block.sync
        def _(sp):
            for i in range(2):
                sp.dma_start(aux[:, i, 0:NG * G].rearrange("p (g k) -> p g k", k=G),
                             t["AUX"][i, 0:NG * P * G].rearrange("(g p k) -> p g k", p=P, k=G)).then_inc(aux_loaded, 16)
                sp.dma_start(aux[0:TAIL, i, NG * G:NG * G + 1],
                             t["AUX"][i, NG * P * G:N].rearrange("(p k) -> p k", k=1)).then_inc(aux_loaded, 16)

            def load(g, m):
                if exists(g):
                    p, n = shape(g)
                    pace(sp, sp_passed, x2_ready, g - UN + 1)
                    sp.dma_start(xt[0:p, m % UN, 0:n, :], nodes(t["x"], g)).then_inc(x_loaded[m % UN], 16)

            def step(s, m):
                load(s + 2, m + 2)
                g, mg = s - L, m - L
                if exists(g):
                    p, n = shape(g)
                    pace(sp, sp_passed, e0_ready, g + 1)
                    pace(sp, sp_passed, e0_aux, g + 1)
                    sp.dma_start(nodes(t["E0"], g), e0[0:p, mg % 4, 0:n, :]).then_inc(e0_stored[mg % 4], 16)
                g, mg = s - M, m - M
                if exists(g):
                    p, n = shape(g)
                    pace(sp, sp_passed, e1_ready, g + 1)
                    sp.dma_start(nodes(t["E1"], g), e1[0:p, mg % 4, 0:n, :]).then_inc(e1_stored[mg % 4], 16)
                g, mg = s - T, m - T
                if exists(g):
                    p, n = shape(g)
                    pace(sp, sp_passed, row_ready, g + 1)
                    sp.dma_start(nodes(t["X2"], g), x2[0:p, mg % 4, 0:n, :]).then_inc(x2_stored[mg % 4], 16)

            load(0, 0)
            load(1, 1)
            run_steps(sp, step, STEPS, LO, HI - UN, UN)
            for stores in (e0_stored, e1_stored, x2_stored):
                for i in range(4):
                    sp.wait_ge(stores[i], 16 * len(range(i, NG + 1, 4)))

        @block.gpsimd
        def _(pool):
            pool.memset(e0[:, :, :, D:], 0.0)
            pool.memset(e1[:, :, :, D:], 0.0)
            pool.memset(x2[:, :, :, W:], 0.0)
            pool.memset(mv[:, :, :, :, :], 1.0).then_inc(cleared, 1)
            pool.wait_ge(cleared, 1)
            pool.wait_ge(aux_loaded, 64)

            def scatter(q, m):
                if not isinstance(q, int) or q >= 4:
                    pool.wait_ge(pair_stored[m % 4], dma_count(q - 4, m % 4, 4, 16 * ET))
                    pool.sem_inc(pool_passed, 1)
                pool.tensor_copy(idx[:, m % 4, :], c["posI"][:, bass.ds(q * ET, ET)])
                pool.tensor_copy(pay[:, m % 4, :, :], c["pairs"][:, bass.ds(q * ET, ET), :]).then_inc(idx_ready, 1)
                pace(pool, pool_passed, idx_ready, q + 1)
                for j in range(ET):
                    pool.indirect_dma_start(t["SORTED"][:, :], bass.IndirectOffsetOnAxis(idx[:, m % 4, j:j + 1], 0),
                                            pay[:, m % 4, j, :], None).then_inc(pair_stored[m % 4], 16)

            def step(s, m):
                g, mg = s - Z, m - Z
                if exists(g):
                    p, n = shape(g)
                    xs = xt[0:p, mg % UN, 0:n, :]
                    pace(pool, pool_passed, h0_ready, g + 1)
                    pool.tensor_tensor(xs, xs, spread(c["bias2"], p, n, W), ALU.add).then_inc(xb_ready, 1)
                    stored(pool, e0_stored, g, mg, pool_passed)
                    pool.tensor_copy(e0[0:p, mg % 4, 0:n, D], aux[0:p, 1, bass.ds(g * G, n)]).then_inc(e0_aux, 1)
                g, mg = s - H, m - H
                if exists(g):
                    p, n = shape(g)
                    at = (m - 2) % 4
                    row = x2[0:p, mg % 4, 0:n, :]
                    pace(pool, pool_passed, k_ready, g + 1)
                    pool.tensor_copy(row[:, :, W], k[0:p, mg % 2, 0:n])
                    pool.tensor_copy(row[:, :, W + 4], aux[0:p, 1, bass.ds(g * G, n)])
                    pool.tensor_tensor(row[:, :, W + 1], nmean[0:p, at, SX2, 0:n], k[0:p, mg % 2, 0:n], ALU.mult).then_inc(b_ready, 1)
                    pace(pool, pool_passed, b_ready, g + 1)
                    pool.tensor_tensor(row[:, :, W + 2], row[:, :, W], row[:, :, W + 4], ALU.mult)
                    pool.tensor_tensor(row[:, :, W + 3], row[:, :, W + 1], row[:, :, W + 4], ALU.mult).then_inc(row_ready, 1)
                g, mg = s - L, m - L
                if exists(g):
                    p, n = shape(g)
                    es = e1[0:p, mg % 4, 0:n, 0:D]
                    stored(pool, e1_stored, g, mg, pool_passed)
                    pace(pool, pool_passed, stat[SE1], g - 3)
                    pace(pool, pool_passed, e1_turned, g - 3)
                    pool.tensor_copy(e1[0:p, mg % 4, 0:n, D], aux[0:p, 1, bass.ds(g * G, n)])
                    pace(pool, pool_passed, n1_ready, g + 1)
                    pool.tensor_tensor(es, n1[0:p, mg % 2, 0:n, :], spread(c["ln1s"], p, n, D), ALU.mult).then_inc(e1_scaled, 1)
                    pace(pool, pool_passed, e1_scaled, g + 1)
                    pool.tensor_tensor(es, es, spread(c["ln1b"], p, n, D), ALU.add).then_inc(e1_ready, 1)

            for s in range(LO):
                if s >= SCATTER_LO:
                    scatter(s - SCATTER_LO, s - SCATTER_LO)
                step(s, s)
            with pool.Fori(LO, SCATTER_HI - UN + 1, UN) as i:
                for u in range(UN):
                    scatter(i + (u - SCATTER_LO), u)
                    step(i + u, u)
            with pool.Fori(SCATTER_HI, HI - UN + 1, UN) as i:
                for u in range(UN):
                    step(i + u, u)
            for s in range(HI, STEPS):
                q = SCATTER_HI - SCATTER_LO + s - HI
                if q < 2 * EG:
                    scatter(q, q)
                step(s, s)
            for i in range(4):
                pool.wait_ge(pair_stored[i], 16 * ET * len(range(i, 2 * EG, 4)))

        @block.vector
        def _(dve):
            def stats(tile, place, m, p, n, g):
                for j in range(n):
                    o = dve.bn_stats(st[0:p, place, j, :], tile[:, j, :])
                o.then_inc(stat[place], 1)
                need(dve, stat[place], g + 1)
                dve.sem_inc(dve_passed, 1)
                for j in range(n):
                    o = dve.bn_aggr(mv[0:p, m % 4, place, j, :], st[0:p, place, j, :])
                return o

            def step(s, m):
                par, before = m % 4, (m - 1) % 4
                gh, mh = s - H, m - H
                ph, nh = shape(gh)
                hs = mh % 2
                if exists(gh):
                    need(dve, root_ready, gh + 1)
                    dve.tensor_tensor(nrm[0:ph, hs, 0, 0:nh], root[0:ph, hs, 0:nh], rstd[0:ph, (m - 2) % 4, SX2, 0:nh],
                                      ALU.mult).then_inc(nrm_ready, 1)
                if exists(s):
                    p, n = shape(s)
                    dve.wait_ge(x_loaded[m % UN], dma_count(s, m % UN, UN))
                    last = stats(xt[0:p, m % UN, 0:n, :], SX, m, p, n, s)
                if exists(gh):
                    need(dve, nrm_ready, gh + 1)
                    dve.tensor_scalar(nrm[0:ph, hs, 1, 0:nh], nrm[0:ph, hs, 0, 0:nh], EPS_L2, None, ALU.max).then_inc(nmax_ready, 1)
                if measured(s - 1):
                    need(dve, std_ready, s)
                    dve.reciprocal(rstd[:, before, :, :], std[:, before, :, :]).then_inc(rstd_ready, 1)
                g, mg = s - M, m - M
                if exists(g):
                    p, n = shape(g)
                    need(dve, e1_ready, g + 1)
                    last = stats(e1[0:p, mg % 4, 0:n, 0:D], SE1, m, p, n, g)
                if exists(gh):
                    need(dve, nmax_ready, gh + 1)
                    dve.reciprocal(inv[0:ph, hs, 0:nh], nrm[0:ph, hs, 1, 0:nh]).then_inc(inv_ready, 1)
                if measured(s - 1):
                    need(dve, rstd_ready, s)
                g, mg = s - L, m - L
                if exists(g):
                    p, n = shape(g)
                    need(dve, e1_scaled, g - 1)
                    for j in range(n):
                        o = dve.tensor_scalar(n1[0:p, mg % 2, j, :], e0[0:p, mg % 4, j, 0:D],
                                              nmean[0:p, before, SE0, j:j + 1], rstd[0:p, before, SE0, j:j + 1],
                                              ALU.add, ALU.mult)
                    o.then_inc(n1_ready, 1)
                if exists(gh):
                    need(dve, inv_ready, gh + 1)
                    need(dve, row_ready, gh - 1)
                    dve.tensor_tensor(k[0:ph, hs, 0:nh], inv[0:ph, hs, 0:nh], rstd[0:ph, (m - 2) % 4, SX2, 0:nh],
                                      ALU.mult).then_inc(k_ready, 1)
                g, mg = s - X, m - X
                if exists(g):
                    p, n = shape(g)
                    need(dve, x2_mm, g + 1)
                    need(dve, xb_ready, g + 1)
                    need(dve, r_ready, g - 3)
                    stored(dve, x2_stored, g, mg)
                    for j in range(n):
                        o = dve.scalar_tensor_tensor(out=x2[0:p, mg % 4, j, 0:W], in0=ps_x[0:p, j, :],
                                                     scalar=rstd[0:p, before, SE1, j:j + 1],
                                                     in1=xt[0:p, mg % UN, j, :], op0=ALU.mult, op1=ALU.add)
                    o.then_inc(x2_ready, 1)
                    if exists(gh):
                        need(dve, k_ready, gh + 1)
                        dve.tensor_tensor(kn[0:ph, hs, 0:nh], k[0:ph, hs, 0:nh], aux[0:ph, 0, bass.ds(gh * G, nh)],
                                          ALU.mult).then_inc(kn_ready, 1)
                    need(dve, x2_ready, g + 1)
                    last = stats(x2[0:p, mg % 4, 0:n, 0:W], SX2, m, p, n, g)
                elif exists(gh):
                    need(dve, k_ready, gh + 1)
                    dve.tensor_tensor(kn[0:ph, hs, 0:nh], k[0:ph, hs, 0:nh], aux[0:ph, 0, bass.ds(gh * G, nh)],
                                      ALU.mult).then_inc(kn_ready, 1)
                if exists(gh):
                    need(dve, kn_ready, gh + 1)
                    need(dve, rw_ready, gh - 1)
                    dve.tensor_tensor(w[0:ph, hs, 0:nh], kn[0:ph, hs, 0:nh], k[0:ph, hs, 0:nh], ALU.mult).then_inc(w_ready, 1)
                g, mg = s - Z, m - Z
                if exists(g):
                    p, n = shape(g)
                    need(dve, z_mm, g + 1)
                    stored(dve, e0_stored, g, mg)
                    for j in range(n):
                        o = dve.scalar_tensor_tensor(out=e0[0:p, mg % 4, j, 0:D], in0=ps_z[0:p, j, :],
                                                     scalar=rstd[0:p, (m - 2) % 4, SX, j:j + 1],
                                                     in1=c["bias0"][0:p, :], op0=ALU.mult, op1=ALU.add)
                    o.then_inc(e0_ready, 1)
                    need(dve, e0_ready, g + 1)
                    last = stats(e0[0:p, mg % 4, 0:n, 0:D], SE0, m, p, n, g)
                if measured(s):
                    last.then_inc(mv_ready, 1)
                    need(dve, mv_ready, s + 1)
                    need(dve, row_ready, s - 8)
                    dve.tensor_scalar(nmean[:, par, :, :], mv[:, par, :, :, 0], -1.0, None, ALU.mult).then_inc(nmean_ready, 1)

            dve.wait_ge(cleared, 1)
            dve.wait_ge(aux_loaded, 64)
            run_steps(dve, step, STEPS - 1, LO, HI, UN)
            need(dve, hth_mm, NG + 1)
            dve.tensor_copy(c["hth"][:, :, :], ps_hth[:, :, :])

        @block.scalar
        def _(act):
            def step(s, m):
                before = (m - 1) % 4
                if measured(s - 1):
                    need(act, mv_ready, s)
                    nc.scalar.activation(std[:, before, 0:2, :], mv[:, before, 0:2, :, 1], ACT.Sqrt, bias=c["eps"][:, 0:1])
                    nc.scalar.activation(std[:, before, 2:4, :], mv[:, before, 2:4, :, 1], ACT.Sqrt,
                                         bias=c["eps"][:, 1:2]).then_inc(std_ready, 1)
                g, mg = s - H, m - H
                if exists(g):
                    p, n = shape(g)
                    need(act, ss_ready, g + 1)
                    need(act, nrm_ready, g - 1)
                    nc.scalar.activation(root[0:p, mg % 2, 0:n], ss[0:p, mg % 2, 0:n], ACT.Sqrt).then_inc(root_ready, 1)
                g, mg = s - B, m - B
                if exists(g):
                    p, n = shape(g)
                    need(act, nmean_ready, g + 1)
                    need(act, h0_turned, g - 1)
                    for j in range(n):
                        o = nc.scalar.activation(h0[0:p, mg % 2, j, :], xt[0:p, mg % UN, j, :], ACT.Relu,
                                                 bias=nmean[0:p, before, SX, j:j + 1])
                    o.then_inc(h0_ready, 1)
                g, mg = s - R, m - R
                if exists(g):
                    p, n = shape(g)
                    need(act, nmean_ready, s)
                    need(act, hth_mm, g - 3)
                    for j in range(n):
                        o = nc.scalar.activation(r[0:p, mg % 4, j, :], x2[0:p, mg % 4, j, 0:W], ACT.Relu,
                                                 bias=nmean[0:p, before, SX2, j:j + 1])
                    o.then_inc(r_ready, 1)
                g, mg = s - M, m - M
                if exists(g):
                    p, n = shape(g)
                    need(act, e1_turned, g + 1)
                    need(act, x2_mm, g - 1)
                    nc.scalar.copy(e1T[:, mg % 2, 0:n, 0:p], ps_e[:, 0:n, 0:p]).then_inc(e1T_ready, 1)
                g, mg = s - B, m - B
                if exists(g):
                    p, n = shape(g)
                    need(act, h0_turned, g + 1)
                    need(act, z_mm, g - 1)
                    nc.scalar.copy(hT[:, mg % 2, 0:n, :, 0:p], ps_h[:, 0:n, :, 0:p]).then_inc(hT_ready, 1)
                g, mg = s - R, m - R
                if exists(g):
                    p, n = shape(g)
                    need(act, r_ready, g + 1)
                    need(act, ss_ready, g)
                    for j in range(n):
                        o = nc.scalar.activation(rsq[0:p, j, :], r[0:p, mg % 4, j, :], ACT.Square,
                                                 accum_out=ss[0:p, mg % 2, j:j + 1])
                    o.then_inc(ss_ready, 1)
                g, mg = s - H, m - H
                if exists(g):
                    p, n = shape(g)
                    need(act, w_ready, g + 1)
                    need(act, hth_mm, g - 1)
                    for j in range(n):
                        o = nc.scalar.mul(rw[0:p, mg % 2, j, :], r[0:p, mg % 4, j, :], w[0:p, mg % 2, j:j + 1])
                    o.then_inc(rw_ready, 1)

            run_steps(act, step, STEPS - 1, LO, HI, UN)

        @block.tensor
        def _(pe):
            def step(s, m):
                g, mg = s - T, m - T
                if exists(g):
                    p, n = shape(g)
                    need(pe, rw_ready, g + 1)
                    for j in range(n):
                        for h in range(2):
                            o = pe.matmul(ps_hth[:, h, :], rw[0:p, mg % 2, j, h * P:(h + 1) * P], r[0:p, mg % 4, j, :],
                                          start=isinstance(g, int) and g == 0 and j == 0 and h == 0,
                                          stop=isinstance(g, int) and g == NG, skip_group_check=True)
                    o.then_inc(hth_mm, 1)
                g, mg = s - M, m - M
                if exists(g):
                    p, n = shape(g)
                    need(pe, e1_ready, g + 1)
                    need(pe, e1T_ready, g)
                    for j in range(n):
                        o = pe.transpose(ps_e[:, j, 0:p], e1[0:p, mg % 4, j, 0:D], c["ident"][0:p, 0:p])
                    o.then_inc(e1_turned, 1)
                g, mg = s - Z, m - Z
                if exists(g):
                    p, n = shape(g)
                    need(pe, hT_ready, g + 1)
                    need(pe, e0_ready, g)
                    for j in range(n):
                        for h in range(2):
                            o = pe.matmul(ps_z[0:p, j, :], hT[:, mg % 2, j, h, 0:p], c["wP"][:, h, :],
                                          start=h == 0, stop=h == 1)
                    o.then_inc(z_mm, 1)
                g, mg = s - B, m - B
                if exists(g):
                    p, n = shape(g)
                    need(pe, h0_ready, g + 1)
                    need(pe, hT_ready, g)
                    for j in range(n):
                        for h in range(2):
                            o = pe.transpose(ps_h[:, j, h, 0:p], h0[0:p, mg % 2, j, h * P:(h + 1) * P], c["ident"][0:p, 0:p])
                    o.then_inc(h0_turned, 1)
                g, mg = s - M, m - M
                if exists(g):
                    p, n = shape(g)
                    need(pe, e1T_ready, g + 1)
                    need(pe, x2_ready, g)
                    for j in range(n):
                        o = pe.matmul(ps_x[0:p, j, :], e1T[:, mg % 2, j, 0:p], c["w2c"][:, :], start=True, stop=True)
                    o.then_inc(x2_mm, 1)

            run_steps(pe, step, STEPS, LO, HI, UN)


def unpack_lists(nc, c, t):
    with ExitStack() as ctx:
        def sb(name, shape, dt=F32):
            return ctx.enter_context(nc.sbuf_tensor(name, shape, dt))

        sem = phase_sems(nc, ctx)

        pairT = sb("pairT", [HT, 2, 2, P, 2], I32)
        nextT = sb("nextT", [HT, 2, 2, P, 2], I32)
        listT = sb("listT", [HT, 3, 2, 2, P])
        ends = sb("ends", [P, 2, NT])
        skip = sb("skip", [P, 2, NT])
        turn = [ctx.enter_context(nc.psum_tensor(f"turn{i}", [P, 512], F32)) for i in range(3)]
        loaded = sem("lists_loaded")
        floats = sem("list_floats")
        stored = sem("list_rows_stored")
        turned = sem("list_turned")
        ready = sem("list_ready")
        ends_ready = sem("ends_ready")
        fin_ready = sem("fin_ready")
        skip_ready = sem("skip_ready")
        block = ctx.enter_context(nc.Block())

        @block.sync
        def _(sp):
            for l in range(2):
                for off, tile in ((0, pairT), (1, nextT)):
                    at = l * LIST + off
                    sp.dma_start(tile[:, l, :, :, :], t["SORTED"][at:at + EP, :].rearrange(
                        "(a r c) k -> r a (c k)", a=2, c=P).rearrange("r a (c k) -> r a c k", k=2)).then_inc(loaded, 16)
            sp.wait_ge(floats, 2)
            for l in range(2):
                sp.dma_start(t["KEYROW"][l].rearrange("(a r c) -> r a c", a=2, c=P), listT[:, 0, l, :, :]).then_inc(stored, 16)
            sp.wait_ge(stored, 32)

        @block.vector
        def _(dve):
            dve.wait_ge(loaded, 64)
            for kind, tile, who in ((0, pairT, (0, 1)), (1, pairT, (1, 0)), (2, nextT, (0, 1))):
                for l in range(2):
                    dve.tensor_copy(listT[:, kind, l, :, :], tile[:, l, :, :, who[l]]).then_inc(floats, 1)
            dve.wait_ge(ready, 3)
            ek = c["ek"]
            dve.tensor_tensor(ends[:, :, :], ek[:, 0, :, :], ek[:, 2, :, :], ALU.not_equal).then_inc(ends_ready, 1)
            dve.tensor_scalar(c["keyI"][:, :, :], ek[:, 0, :, :], float(N - 1), None, ALU.min)
            dve.tensor_scalar(c["otherI"][:, :, :], ek[:, 1, :, :], float(N - 1), None, ALU.min)
            dve.wait_ge(ends_ready, 1)
            dve.scalar_tensor_tensor(out=c["fin"][:, :, :], in0=ek[:, 0, :, :], scalar=float(N), in1=ends[:, :, :],
                                     op0=ALU.is_lt, op1=ALU.mult).then_inc(fin_ready, 1)
            dve.wait_ge(fin_ready, 1)
            dve.tensor_scalar(skip[:, :, :], c["fin"][:, :, :], -SKIP, SKIP, ALU.mult, ALU.add).then_inc(skip_ready, 1)
            dve.wait_ge(skip_ready, 1)
            dve.tensor_tensor(c["finI"][:, :, :], skip[:, :, :], ek[:, 0, :, :], ALU.add)

        @block.scalar
        def _(act):
            for kind in range(3):
                act.wait_ge(turned, kind + 1)
                nc.scalar.copy(c["ek"][:, kind, :, :].rearrange("p l t -> p (l t)"), turn[kind][:, 0:2 * NT]).then_inc(ready, 1)

        @block.tensor
        def _(pe):
            for kind in range(3):
                pe.wait_ge(floats, 2 * kind + 2)
                for l in range(2):
                    for a in range(2):
                        at = (l * 2 + a) * HT
                        o = pe.transpose(turn[kind][:, at:at + HT], listT[:, kind, l, a, :], c["ident"][0:HT, 0:HT])
                o.then_inc(turned, 1)


def edge_attention(nc, c, t, layer):
    last = layer == 2
    UN, LO, HI = 8, 9, 49
    B, C, M, X, H, T = 1, 2, 3, 4, 5, 6
    SC = 6 if last else 3
    STEPS = EG + SC
    VW = D + HEADS
    R4 = ET
    table = t["E1"] if last else t["E0"]
    wt = c["qkv2"] if last else c["qkv1"]
    L = f"_{layer}"
    with ExitStack() as ctx:
        def sb(name, shape, dt=F32):
            return ctx.enter_context(nc.sbuf_tensor(name + L, shape, dt))

        def ps(name, shape):
            return ctx.enter_context(nc.psum_tensor(name + L, shape, F32))

        sem = phase_sems(nc, ctx, L)

        idx = sb("gather_idx", [P, 4, 2, ET], I32)
        fidx = sb("final_idx", [P, 4, ET], I32)
        rrow = sb("src_rows", [P, 4, ET, EW])
        crow = sb("dst_rows", [P, 2, ET, EW])
        keys = sb("keys", [P, 2, ET * P])
        kc = sb("key_cols", [P, 2, ET + 1])
        dv = sb("dinv", [P, 8, ET])
        S = sb("same_src", [P, 2, ET, P])
        cm = sb("carry_to", [P, 2, ET, P])
        rT = sb("rT", [P, ET, P])
        cT = sb("cT", [P, ET, P])
        qs = sb("qs", [P, ET, D])
        qk = sb("qk", [P, ET, D])
        att = sb("att", [P, 2, ET * HEADS])
        vals = sb("vals", [P, 2, ET, VW])
        carry = sb("carry", [P, ET, VW])
        den = sb("den", [P, 2, ET, HEADS])
        emb = sb("emb", [P, 2, 2, ET, D])
        nrmd = sb("normalised", [P, 2, ET, D])
        st = sb("st", [P, 2, ET, 6])
        mv = sb("mv", [P, 2, 2, ET, 2])
        std = sb("std", [P, 2, 2, ET])
        rstd = sb("rstd", [P, 2, 2, ET])
        nb = sb("nb", [P, 2, 2, ET])
        ps_r = ps("ps_r", [P, ET, P])
        ps_c = ps("ps_c", [P, ET, P])
        ps_q = ps("ps_q", [P, ET, D])
        ps_kv = ps("ps_kv", [P, ET, 2, D])
        ps_a = ps("ps_a", [P, ET, 2 * D])
        if last:
            xr = sb("x_rows", [P, 4, ET, W])
            x2 = sb("x2_new", [P, 4, ET, XW])
            n2T = sb("n2T", [P, ET, P])
            r = sb("r", [P, 2, ET, W])
            rsq = sb("rsq", [P, ET, W])
            rw = sb("rw", [P, 2, ET, W])
            ss = sb("ss", [P, 2, ET])
            nrm = sb("nrm", [P, 2, ET])
            inv = sb("inv", [P, 2, ET])
            w1 = sb("w1", [P, 2, ET])
            ps_hth = ps("ps_hth", [P, 2, W])
        else:
            e1 = sb("e1_new", [P, 2, 2, ET, EW])

        r_loaded = [sem(f"r_loaded{i}") for i in range(4)]
        c_loaded = [sem(f"c_loaded{i}") for i in range(2)]
        x_loaded = [sem(f"xr_loaded{i}") for i in range(4)] if last else None
        keys_loaded = [sem(f"keys_loaded{i}") for i in range(2)]
        new_stored = [sem(f"new_stored{i}") for i in range(4)]
        names = ("sp_passed", "pool_passed", "dve_passed", "cleared", "idx_ready", "fidx_ready", "kc_ready",
                 "S_ready", "dv_ready", "r_turned", "c_turned", "rT_ready", "cT_ready", "q_mm", "kv_mm", "q_ready",
                 "qk_ready", "att_ready", "clip_ready", "exp_ready", "vals_ready", "agg_mm", "carry_ready",
                 "den_ready", "rec_ready", "avg_ready", "emb_ready", "stat", "mv_ready", "std_ready", "rstd_ready",
                 "nb_ready", "n_ready", "scaled", "new_ready")
        if last:
            names += ("n2_turned", "n2T_ready", "x2_mm", "x2_ready", "x2_stat", "r_ready", "ss_ready", "nrm_ready",
                      "nmax_ready", "inv_ready", "k_ready", "rw_ready", "hth_mm")
        sems = {name: sem(name) for name in names}
        (sp_passed, pool_passed, dve_passed, cleared, idx_ready, fidx_ready, kc_ready, S_ready, dv_ready, r_turned,
         c_turned, rT_ready, cT_ready, q_mm, kv_mm, q_ready, qk_ready, att_ready, clip_ready, exp_ready, vals_ready,
         agg_mm, carry_ready, den_ready, rec_ready, avg_ready, emb_ready, stat, mv_ready, std_ready, rstd_ready,
         nb_ready, n_ready, scaled, new_ready) = (sems[name] for name in names[:35])
        if last:
            (n2_turned, n2T_ready, x2_mm, x2_ready, x2_stat, r_ready, ss_ready, nrm_ready, nmax_ready, inv_ready,
             k_ready, rw_ready, hth_mm) = (sems[name] for name in names[35:])
        block = ctx.enter_context(nc.Block())

        def exists(g):
            return not isinstance(g, int) or 0 <= g < EG

        @block.sync
        def _(sp):
            def step(s, m):
                if exists(s):
                    pace(sp, sp_passed, S_ready, s - 1)
                    sp.dma_start(keys[:, m % 2, :], t["KEYROW"][0, bass.ds(s * (ET * P), ET * P)].partition_broadcast(P)
                                 ).then_inc(keys_loaded[m % 2], 16)

            run_steps(sp, step, EG, LO, HI, UN)

        @block.gpsimd
        def _(pool):
            bound = pool.to_reg(N - 1)

            def gather(tile, slot, source, kind, islot, loaded):
                for j in range(ET):
                    pool.indirect_dma_start(tile[:, slot, j, :], None, source[:, :],
                                            bass.IndirectOffsetOnAxis(idx[:, islot, kind, j:j + 1], 0)
                                            ).then_inc(loaded[slot], 16)

            def step(s, m):
                if exists(s):
                    if not isinstance(s, int) or s >= 4:
                        for loaded in ((r_loaded, x_loaded) if last else (r_loaded,)):
                            pool.wait_ge(loaded[m % 4], dma_count(s - 4, m % 4, 4, 16 * ET))
                            pool.sem_inc(pool_passed, 1)
                    if not isinstance(s, int) or s >= 2:
                        pool.wait_ge(c_loaded[m % 2], dma_count(s - 2, m % 2, 2, 16 * ET))
                        pool.sem_inc(pool_passed, 1)
                    pool.tensor_copy(idx[:, m % 4, 0, :], c["keyI"][:, 0, bass.ds(s * ET, ET)])
                    pool.tensor_copy(idx[:, m % 4, 1, :], c["otherI"][:, 0, bass.ds(s * ET, ET)]).then_inc(idx_ready, 1)
                    pace(pool, pool_passed, idx_ready, s + 1)
                    pace(pool, pool_passed, emb_ready, s - 3)
                    pace(pool, pool_passed, r_turned, s - 3)
                    pace(pool, pool_passed, dv_ready, s - 3)
                    gather(rrow, m % 4, table, 0, m % 4, r_loaded)
                    pace(pool, pool_passed, c_turned, s - 1)
                    gather(crow, m % 2, table, 1, m % 4, c_loaded)
                    if last:
                        pace(pool, pool_passed, x2_ready, s - 3)
                        gather(xr, m % 4, t["x"], 0, m % 4, x_loaded)
                g, mg = s - SC, m - SC
                if exists(g):
                    if not isinstance(g, int) or g >= 4:
                        pool.wait_ge(new_stored[mg % 4], dma_count(g - 4, mg % 4, 4, 16 * ET))
                        pool.sem_inc(pool_passed, 1)
                    pool.tensor_copy(fidx[:, mg % 4, :], c["finI"][:, 0, bass.ds(g * ET, ET)]).then_inc(fidx_ready, 1)
                    pace(pool, pool_passed, fidx_ready, g + 1)
                    pace(pool, pool_passed, new_ready, g + 1)
                    for j in range(ET):
                        new = x2[:, mg % 4, j, :] if last else e1[:, 1, mg % 2, j, :]
                        pool.indirect_dma_start(t["X2" if last else "E1"][:, :],
                                                bass.IndirectOffsetOnAxis(fidx[:, mg % 4, j:j + 1], 0), new, None,
                                                bounds_check=bound, oob_is_err=False).then_inc(new_stored[mg % 4], 16)

            run_steps(pool, step, STEPS, LO, HI, UN)
            for k in range(4):
                pool.wait_ge(new_stored[k], 16 * ET * len(range(k, EG, 4)))

        @block.vector
        def _(dve):
            def stats(tile, place, m, done, g):
                for j in range(ET):
                    o = dve.bn_stats(st[:, place, j, :], tile[:, j, :])
                o.then_inc(done, 1)
                need(dve, done, g + 1)
                dve.sem_inc(dve_passed, 1)
                for j in range(ET):
                    o = dve.bn_aggr(mv[:, m % 2, place, j, :], st[:, place, j, :])
                return o

            def step(s, m):
                par, before = m % 2, (m - 1) % 2
                if last:
                    g, mg = s - X, m - X
                    if exists(g):
                        need(dve, x2_mm, g + 1)
                        dve.wait_ge(x_loaded[mg % 4], dma_count(g, mg % 4, 4, 16 * ET))
                        need(dve, r_ready, g - 3)
                        if not isinstance(g, int) or g >= 4:
                            dve.wait_ge(new_stored[mg % 4], dma_count(g - 4, mg % 4, 4, 16 * ET))
                        dve.tensor_tensor(x2[:, mg % 4, :, 0:W], ps_kv[:, :, :, :].rearrange("p j k d -> p j (k d)"),
                                          xr[:, mg % 4, :, :], ALU.add).then_inc(x2_ready, 1)
                        need(dve, x2_ready, g + 1)
                        tail = stats(x2[:, mg % 4, :, 0:W], 1, m, x2_stat, g)
                    g, mg = s - M, m - M
                    if exists(g):
                        need(dve, n2_turned, g + 1)
                        need(dve, x2_mm, g)
                        dve.tensor_copy(n2T[:, :, :], ps_r[:, :, :]).then_inc(n2T_ready, 1)
                g, mg = s - B, m - B
                if exists(g):
                    p2 = mg % 2
                    lo = 1 if isinstance(g, int) and g == 0 else 0
                    if lo:
                        dve.memset(kc[:, p2, 0:1], -1.0)
                    dve.tensor_copy(kc[:, p2, lo:], c["ek"][:, 0, 0, bass.ds(g * ET - 1 + lo, ET + 1 - lo)]).then_inc(kc_ready, 1)
                    need(dve, kc_ready, g + 1)
                    dve.wait_ge(keys_loaded[p2], dma_count(g, p2, 2))
                    need(dve, agg_mm, (g - 1) * ET)
                    for j in range(ET):
                        kj = keys[:, p2, j * P:(j + 1) * P]
                        dve.tensor_scalar(S[:, p2, j, :], kj, kc[:, p2, j + 1:j + 2], None, ALU.is_equal)
                        o = dve.tensor_scalar(cm[QUAD:, p2, j, :], kj[QUAD:, :], kc[QUAD:, p2, j:j + 1],
                                              c["e127"][QUAD:, :], ALU.is_equal, ALU.mult)
                    o.then_inc(S_ready, 1)
                    dve.wait_ge(r_loaded[mg % 4], dma_count(g, mg % 4, 4, 16 * ET))
                    dve.tensor_copy(dv[:, mg % 8, :], rrow[:, mg % 4, :, D]).then_inc(dv_ready, 1)
                    need(dve, c_turned, g + 1)
                    need(dve, kv_mm, g)
                    dve.tensor_copy(cT[:, :, :], ps_c[:, :, :]).then_inc(cT_ready, 1)
                g, mg = s - C, m - C
                if exists(g):
                    p2 = mg % 2
                    need(dve, carry_ready, (g + 1) * ET)
                    dve.tensor_scalar(den[:, 0, :, :], ps_a[:, :, D:VW], EPS_ATT, None, ALU.add).then_inc(den_ready, 1)
                    need(dve, den_ready, g + 1)
                    dve.reciprocal(den[:, 1, :, :], den[:, 0, :, :]).then_inc(rec_ready, 1)
                    need(dve, rec_ready, g + 1)
                    need(dve, n_ready, g - 1)
                    dve.tensor_tensor(
                        emb[:, 0, p2, :, :].rearrange("p j (h d) -> p j h d", h=HEADS),
                        ps_a[:, :, 0:D].rearrange("p j (h d) -> p j h d", h=HEADS),
                        den[:, 1, :, :].unsqueeze(3).to_broadcast([P, ET, HEADS, HD]), ALU.mult).then_inc(avg_ready, 1)
                    need(dve, avg_ready, g + 1)
                    dve.tensor_tensor(emb[:, 1, p2, :, :], emb[:, 0, p2, :, :], rrow[:, mg % 4, :, 0:D],
                                      ALU.add).then_inc(emb_ready, 1)
                    need(dve, emb_ready, g + 1)
                    tail = stats(emb[:, 1, p2, :, :], 0, m, stat, g)
                if not isinstance(s, int) or C <= s < EG + (X if last else C):
                    tail.then_inc(mv_ready, 1)
                n = s - C
                g, mg = s - B, m - B
                if exists(g):
                    need(dve, q_ready, g + 1)
                    need(dve, kv_mm, g + 1)
                    dve.tensor_tensor(qk[:, :, :], qs[:, :, :], ps_kv[:, :, 0, :], ALU.mult).then_inc(qk_ready, 1)
                    need(dve, qk_ready, g + 1)
                    need(dve, exp_ready, g - 1)
                    dve.tensor_reduce(att[:, mg % 2, :], qk[:, :, :].rearrange("p j (h d) -> p (j h) d", h=HEADS),
                                      AX_X, ALU.add).then_inc(att_ready, 1)
                    need(dve, att_ready, g + 1)
                    dve.tensor_scalar(att[:, mg % 2, :], att[:, mg % 2, :], -10.0, 10.0, ALU.max, ALU.min).then_inc(clip_ready, 1)
                if not isinstance(s, int) or C <= s < EG + (X if last else C):
                    need(dve, n_ready, n - 1 if not isinstance(n, int) else min(n - 1, EG))
                    if last:
                        need(dve, r_ready, s - H)
                        need(dve, new_ready, s - H)
                    need(dve, std_ready, n + 1)
                    dve.reciprocal(rstd[:, par, :, :], std[:, par, :, :]).then_inc(rstd_ready, 1)
                    need(dve, rstd_ready, n + 1)
                    dve.scalar_tensor_tensor(out=nb[:, par, :, :], in0=mv[:, par, :, :, 0], scalar=-1.0,
                                             in1=rstd[:, par, :, :], op0=ALU.mult, op1=ALU.mult).then_inc(nb_ready, 1)
                g, mg = s - B, m - B
                if exists(g):
                    p2 = mg % 2
                    need(dve, exp_ready, g + 1)
                    dve.tensor_tensor(
                        vals[:, p2, :, 0:D].rearrange("p j (h d) -> p j h d", h=HEADS),
                        ps_kv[:, :, 1, :].rearrange("p j (h d) -> p j h d", h=HEADS),
                        vals[:, p2, :, D:VW].unsqueeze(3).to_broadcast([P, ET, HEADS, HD]), ALU.mult).then_inc(vals_ready, 1)
                if not last:
                    g, mg = s - C, m - C
                    if exists(g):
                        p2 = mg % 2
                        need(dve, n_ready, g + 1)
                        if not isinstance(g, int) or g >= 2:
                            dve.wait_ge(new_stored[(mg - 2) % 4], dma_count(g - 2, (mg - 2) % 4, 4, 16 * ET))
                        dve.tensor_tensor(e1[:, 0, p2, :, 0:D], nrmd[:, p2, :, :], spread(c["ln1s"], P, ET, D), ALU.mult)
                        dve.tensor_copy(e1[:, 1, p2, :, D], dv[:, mg % 8, :]).then_inc(scaled, 1)
                        need(dve, scaled, g + 1)
                        dve.tensor_tensor(e1[:, 1, p2, :, 0:D], e1[:, 0, p2, :, 0:D], spread(c["ln1b"], P, ET, D),
                                          ALU.add).then_inc(new_ready, 1)
                else:
                    g, mg = s - H, m - H
                    if exists(g):
                        p2 = mg % 2
                        row = x2[:, mg % 4, :, :]
                        need(dve, nrm_ready, g + 1)
                        dve.tensor_scalar(nrm[:, p2, :], nrm[:, p2, :], EPS_L2, None, ALU.max).then_inc(nmax_ready, 1)
                        need(dve, nmax_ready, g + 1)
                        dve.reciprocal(inv[:, p2, :], nrm[:, p2, :]).then_inc(inv_ready, 1)
                        need(dve, inv_ready, g + 1)
                        dve.tensor_tensor(w1[:, p2, :], inv[:, p2, :], c["fin"][:, 0, bass.ds(g * ET, ET)], ALU.mult)
                        dve.tensor_tensor(row[:, :, W], rstd[:, before, 1, :], inv[:, p2, :], ALU.mult)
                        dve.tensor_copy(row[:, :, W + 4], dv[:, mg % 8, :])
                        dve.tensor_tensor(row[:, :, W + 1], nb[:, before, 1, :], inv[:, p2, :], ALU.mult).then_inc(k_ready, 1)
                        need(dve, k_ready, g + 1)
                        dve.tensor_tensor(row[:, :, W + 2], row[:, :, W], row[:, :, W + 4], ALU.mult)
                        dve.tensor_tensor(row[:, :, W + 3], row[:, :, W + 1], row[:, :, W + 4], ALU.mult).then_inc(new_ready, 1)
                        need(dve, hth_mm, g - 1)
                        for j in range(ET):
                            o = dve.tensor_scalar(rw[:, p2, j, :], r[:, p2, j, :], inv[:, p2, j:j + 1],
                                                  w1[:, p2, j:j + 1], ALU.mult, ALU.mult)
                        o.then_inc(rw_ready, 1)

            dve.memset(mv[:, :, :, :, :], 1.0).then_inc(cleared, 1)
            if last:
                dve.memset(x2[:, :, :, W:], 0.0).then_inc(cleared, 1)
            else:
                dve.memset(e1[:, :, :, :, D:], 0.0).then_inc(cleared, 1)
            dve.wait_ge(cleared, 2)
            run_steps(dve, step, EG + (H if last else C) , LO, HI, UN)
            if last:
                need(dve, hth_mm, EG)
                dve.tensor_tensor(c["hth"][:, :, :], c["hth"][:, :, :], ps_hth[:, :, :], ALU.add)

        @block.scalar
        def _(act):
            def step(s, m):
                par, before = m % 2, (m - 1) % 2
                if last:
                    g, mg = s - H, m - H
                    if exists(g):
                        p2 = mg % 2
                        need(act, nb_ready, s - C)
                        need(act, hth_mm, g - 1)
                        need(act, rw_ready, g - 1)
                        for j in range(ET):
                            o = nc.scalar.activation(r[:, p2, j, :], x2[:, mg % 4, j, 0:W], ACT.Relu,
                                                     bias=nb[:, before, 1, j:j + 1], scale=rstd[:, before, 1, j:j + 1])
                        o.then_inc(r_ready, 1)
                        need(act, r_ready, g + 1)
                        need(act, ss_ready, g)
                        for j in range(ET):
                            o = nc.scalar.activation(rsq[:, j, :], r[:, p2, j, :], ACT.Square, accum_out=ss[:, p2, j:j + 1])
                        o.then_inc(ss_ready, 1)
                        need(act, ss_ready, g + 1)
                        need(act, inv_ready, g - 1)
                        nc.scalar.activation(nrm[:, p2, :], ss[:, p2, :], ACT.Sqrt).then_inc(nrm_ready, 1)
                g, mg = s - B, m - B
                if exists(g):
                    need(act, r_turned, g + 1)
                    need(act, q_mm, g)
                    nc.scalar.copy(rT[:, :, :], ps_r[:, :, :]).then_inc(rT_ready, 1)
                g, mg = s - C, m - C
                if exists(g):
                    for j in range(ET):
                        need(act, agg_mm, g * ET + j + 1)
                        nc.scalar.copy(carry[QUAD:, j, :], ps_a[QUAD:, j, 0:VW]).then_inc(carry_ready, 1)
                g, mg = s - B, m - B
                if exists(g):
                    need(act, q_mm, g + 1)
                    need(act, qk_ready, g)
                    nc.scalar.copy(qs[:, :, :], ps_q[:, :, :]).then_inc(q_ready, 1)
                n = s - C
                if not isinstance(s, int) or C <= s < EG + (X if last else C):
                    need(act, mv_ready, n + 1)
                    need(act, rstd_ready, n - 1)
                    nc.scalar.activation(std[:, par, 0, :], mv[:, par, 0, :, 1], ACT.Sqrt, bias=c["eps"][:, 1:2])
                    nc.scalar.activation(std[:, par, 1, :], mv[:, par, 1, :, 1], ACT.Sqrt,
                                         bias=c["eps"][:, 0:1]).then_inc(std_ready, 1)
                g, mg = s - B, m - B
                if exists(g):
                    p2 = mg % 2
                    need(act, clip_ready, g + 1)
                    need(act, agg_mm, (g - 1) * ET)
                    nc.scalar.activation(vals[:, p2, :, D:VW], att[:, p2, :].rearrange("p (j h) -> p j h", h=HEADS),
                                         ACT.Exp).then_inc(exp_ready, 1)
                g, mg = s - C, m - C
                if exists(g):
                    p2 = mg % 2
                    need(act, nb_ready, n + 1)
                    need(act, n2_turned if last else new_ready, g - 1)
                    for j in range(ET):
                        o = nc.scalar.activation(nrmd[:, p2, j, :], emb[:, 1, p2, j, :], ACT.Identity,
                                                 bias=nb[:, par, 0, j:j + 1], scale=rstd[:, par, 0, j:j + 1])
                    o.then_inc(n_ready, 1)

            run_steps(act, step, EG + (H if last else C), LO, HI, UN)

        @block.tensor
        def _(pe):
            def step(s, m):
                if last:
                    g, mg = s - T, m - T
                    if exists(g):
                        need(pe, rw_ready, g + 1)
                        for j in range(ET):
                            for h in range(2):
                                o = pe.matmul(ps_hth[:, h, :], rw[:, mg % 2, j, h * P:(h + 1) * P], r[:, mg % 2, j, :],
                                              start=isinstance(g, int) and g == 0 and j == 0 and h == 0,
                                              stop=isinstance(g, int) and g == EG - 1 and j == ET - 1,
                                              skip_group_check=True)
                        o.then_inc(hth_mm, 1)
                    g, mg = s - M, m - M
                    if exists(g):
                        need(pe, n_ready, g + 1)
                        need(pe, rT_ready, s - M + 2 if not isinstance(s, int) else min(g + 2, EG))
                        for j in range(ET):
                            o = pe.transpose(ps_r[:, j, :], nrmd[:, mg % 2, j, :], c["ident"][:, :])
                        o.then_inc(n2_turned, 1)
                g, mg = s - B, m - B
                if exists(g):
                    pe.wait_ge(r_loaded[mg % 4], dma_count(g, mg % 4, 4, 16 * ET))
                    need(pe, rT_ready, g)
                    if last:
                        need(pe, n2T_ready, g - M + B + 1)
                    for j in range(ET):
                        o = pe.transpose(ps_r[:, j, :], rrow[:, mg % 4, j, 0:D], c["ident"][:, :])
                    o.then_inc(r_turned, 1)
                    pe.wait_ge(c_loaded[mg % 2], dma_count(g, mg % 2, 2, 16 * ET))
                    need(pe, cT_ready, g)
                    for j in range(ET):
                        o = pe.transpose(ps_c[:, j, :], crow[:, mg % 2, j, 0:D], c["ident"][:, :])
                    o.then_inc(c_turned, 1)
                g, mg = s - C, m - C
                if exists(g):
                    p2 = mg % 2
                    need(pe, S_ready, g + 1)
                    need(pe, vals_ready, g + 1)
                    need(pe, avg_ready, g)
                    for j in range(ET):
                        first = isinstance(g, int) and g == 0 and j == 0
                        need(pe, carry_ready, g * ET + j)
                        o = pe.matmul(ps_a[:, j, 0:VW], S[:, p2, j, :], vals[:, p2, j, :], start=True, stop=first)
                        if not first:
                            o = pe.matmul(ps_a[:, j, 0:VW], cm[QUAD:, p2, j, :], carry[QUAD:, (j - 1) % ET, :],
                                          start=False, stop=True)
                        o.then_inc(agg_mm, 1)
                g, mg = s - B, m - B
                if exists(g):
                    need(pe, rT_ready, g + 1)
                    need(pe, q_ready, g)
                    for j in range(ET):
                        o = pe.matmul(ps_q[:, j, :], rT[:, j, :], wt[:, 0, :], start=True, stop=True)
                    o.then_inc(q_mm, 1)
                    need(pe, cT_ready, g + 1)
                    need(pe, vals_ready, g)
                    if last:
                        need(pe, x2_ready, g - X + B + 1)
                    for j in range(ET):
                        o = pe.matmul(ps_kv[:, j, :, :], cT[:, j, :], wt[:, 1:3, :], start=True, stop=True)
                    o.then_inc(kv_mm, 1)
                if last:
                    g, mg = s - M, m - M
                    if exists(g):
                        need(pe, n2T_ready, g + 1)
                        need(pe, vals_ready, s - B + 1 if not isinstance(s, int) else min(s - B + 1, EG))
                        need(pe, x2_ready, g)
                        for j in range(ET):
                            x2_out = ps_kv[:, j, :, :].rearrange("p k d -> p (k d)")
                            pe.matmul(x2_out, c["ones"][0:1, :], c["bias2"][0:1, :], start=True, stop=False)
                            o = pe.matmul(x2_out, n2T[:, j, :], c["w2"][:, :], start=False, stop=True)
                        o.then_inc(x2_mm, 1)

            run_steps(pe, step, EG + (T if last else C), LO, HI, UN)


def dense_gcn(nc, c, t):
    UN, LO, HI = 8, 8, 128
    B, V, M, Z, Q, O = 0, 1, 2, 3, 4, 5
    AHEAD = 2
    with ExitStack() as ctx:
        def sb(name, shape, dt=F32):
            return ctx.enter_context(nc.sbuf_tensor("n_" + name, shape, dt))

        def ps(name, shape):
            return ctx.enter_context(nc.psum_tensor("n_" + name, shape, F32))

        sem = phase_sems(nc, ctx)
        wsum = sb("wsum", [P, 2, W])
        x2 = sb("x2_in", [P, 8, G, XW])
        h = sb("h", [P, 2, G, W])
        hT = sb("hT", [P, 2, G, 2, P])
        zb = sb("zb", [P, 2, G, W])
        z = sb("z", [P, 4, G, W])
        zsq = sb("zsq", [P, G, W])
        ss = sb("ss", [P, 2, G])
        nrm = sb("nrm", [P, 2, G])
        inv = sb("inv", [P, 2, G])
        o_sb = sb("o_sb", [P, 4, G, W])
        ps_h = ps("ps_h", [P, 2, 4, 2, P])
        ps_z = ps("ps_z", [P, 2, 4, W])

        x_loaded = [sem(f"x2_loaded{i}") for i in range(8)]
        o_stored = [sem(f"out_stored{i}") for i in range(4)]
        (sp_passed, m_mm, wv_ready, wsum_ready, h_ready, h_turned, hT_ready, z_mm, zb_ready,
         z_ready, ss_ready, nrm_ready, nmax_ready, inv_ready, o_ready) = (sem("gcn_" + s) for s in (
            "sp_passed", "m_mm", "wv_ready", "wsum_ready", "h_ready", "h_turned",
            "hT_ready", "z_mm", "zb_ready", "z_ready", "ss_ready", "nrm_ready", "nmax_ready", "inv_ready", "o_ready"))
        block = ctx.enter_context(nc.Block())

        def exists(g):
            return not isinstance(g, int) or 0 <= g <= NG

        def shape(g):
            return (TAIL, 1) if isinstance(g, int) and g == NG else (P, G)

        def nodes(ap, g):
            p, n = shape(g)
            return ap[bass.ds(g * (P * G), p * n), :].rearrange("(p k) c -> p k c", k=n)

        @block.sync
        def _(sp):
            def load(g, m):
                if exists(g):
                    p, n = shape(g)
                    pace(sp, sp_passed, o_ready, g - 7)
                    sp.dma_start(x2[0:p, m % 8, 0:n, :], nodes(t["X2"], g)).then_inc(x_loaded[m % 8], 16)

            def step(s, m):
                load(s + AHEAD, m + AHEAD)
                g, mg = s - O, m - O
                if exists(g):
                    p, n = shape(g)
                    pace(sp, sp_passed, o_ready, g + 1)
                    sp.dma_start(nodes(t["out"], g), o_sb[0:p, mg % 4, 0:n, :]).then_inc(o_stored[mg % 4], 16)

            for g in range(AHEAD):
                load(g, g)
            run_steps(sp, step, NG + 1 + O, LO, HI, UN)
            for k in range(4):
                sp.wait_ge(o_stored[k], 16 * len(range(k, NG + 1, 4)))

        @block.vector
        def _(dve):
            dve.wait_ge(m_mm, 1)
            dve.tensor_scalar(c["wv"][:, :, :], ps_z[:, 0, 0:2, :], BETA / N, None, ALU.mult).then_inc(wv_ready, 1)
            dve.wait_ge(wv_ready, 1)
            dve.tensor_tensor(wsum[:, :, :], c["wv"][:, :, :], c["wg"][:, :, :], ALU.add).then_inc(wsum_ready, 1)

            def step(s, m):
                g, mg = s - V, m - V
                if exists(g):
                    p, n = shape(g)
                    need(dve, h_turned, g + 1)
                    need(dve, z_mm, g - 1)
                    dve.tensor_copy(hT[:, mg % 2, 0:n, :, 0:p], ps_h[:, mg % 2, 0:n, :, 0:p]).then_inc(hT_ready, 1)
                g, mg = s - Z, m - Z
                if exists(g):
                    p, n = shape(g)
                    need(dve, z_mm, g + 1)
                    need(dve, z_ready, g - 1)
                    dve.tensor_tensor(zb[0:p, mg % 2, 0:n, :], ps_z[0:p, mg % 2, 0:n, :], spread(c["bg"], p, n, W),
                                      ALU.add).then_inc(zb_ready, 1)
                g, mg = s - O, m - O
                if exists(g):
                    p, n = shape(g)
                    p2 = mg % 2
                    need(dve, nrm_ready, g + 1)
                    dve.tensor_scalar(nrm[0:p, p2, 0:n], nrm[0:p, p2, 0:n], EPS_L2, None, ALU.max).then_inc(nmax_ready, 1)
                    need(dve, nmax_ready, g + 1)
                    dve.reciprocal(inv[0:p, p2, 0:n], nrm[0:p, p2, 0:n]).then_inc(inv_ready, 1)
                    need(dve, inv_ready, g + 1)
                    if not isinstance(g, int) or g >= 4:
                        dve.wait_ge(o_stored[mg % 4], dma_count(g - 4, mg % 4, 4))
                    for k in range(n):
                        o = dve.scalar_tensor_tensor(out=o_sb[0:p, mg % 4, k, :], in0=z[0:p, mg % 4, k, :],
                                                     scalar=inv[0:p, p2, k:k + 1], in1=x2[0:p, mg % 8, k, 0:W],
                                                     op0=ALU.mult, op1=ALU.add)
                    o.then_inc(o_ready, 1)

            run_steps(dve, step, NG + 1 + O, LO, HI, UN)

        @block.scalar
        def _(act):
            def step(s, m):
                gq, mq = s - Q, m - Q
                q2 = mq % 2
                if exists(gq):
                    p, n = shape(gq)
                    need(act, zb_ready, gq + 1)
                    need(act, o_ready, gq - 3)
                    nc.scalar.activation(z[0:p, mq % 4, 0:n, :], zb[0:p, q2, 0:n, :], ACT.Relu).then_inc(z_ready, 1)
                g, mg = s - B, m - B
                if exists(g):
                    p, n = shape(g)
                    act.wait_ge(x_loaded[mg % 8], dma_count(g, mg % 8, 8))
                    need(act, h_turned, g - 1)
                    for k in range(n):
                        row = x2[0:p, mg % 8, k, :]
                        o = nc.scalar.activation(h[0:p, mg % 2, k, :], row[:, 0:W], ACT.Relu,
                                                 bias=row[:, W + 1:W + 2], scale=row[:, W:W + 1])
                    o.then_inc(h_ready, 1)
                if exists(gq):
                    p, n = shape(gq)
                    need(act, z_ready, gq + 1)
                    need(act, ss_ready, gq)
                    for k in range(n):
                        o = nc.scalar.activation(zsq[0:p, k, :], z[0:p, mq % 4, k, :], ACT.Square,
                                                 accum_out=ss[0:p, q2, k:k + 1])
                    o.then_inc(ss_ready, 1)
                    need(act, ss_ready, gq + 1)
                    need(act, inv_ready, gq - 1)
                    nc.scalar.activation(nrm[0:p, q2, 0:n], ss[0:p, q2, 0:n], ACT.Sqrt).then_inc(nrm_ready, 1)

            run_steps(act, step, NG + 1 + Q, LO, HI, UN)

        @block.tensor
        def _(pe):
            for i in range(2):
                for k in range(2):
                    o = pe.matmul(ps_z[:, 0, i, :], c["hth"][:, k, i * P:(i + 1) * P], c["wv"][:, k, :],
                                  start=i == 0 and k == 0, stop=i == 1 and k == 1, skip_group_check=True)
            o.then_inc(m_mm, 1)
            pe.wait_ge(wsum_ready, 1)

            def step(s, m):
                g, mg = s - M, m - M
                if exists(g):
                    p, n = shape(g)
                    need(pe, hT_ready, g + 1)
                    need(pe, zb_ready, g - 1)
                    for k in range(n):
                        for i in range(2):
                            o = pe.matmul(ps_z[0:p, mg % 2, k, :], hT[:, mg % 2, k, i, 0:p], wsum[:, i, :],
                                          start=i == 0, stop=i == 1)
                    o.then_inc(z_mm, 1)
                g, mg = s - B, m - B
                if exists(g):
                    p, n = shape(g)
                    need(pe, h_ready, g + 1)
                    need(pe, hT_ready, g - 1)
                    for k in range(n):
                        for i in range(2):
                            o = pe.transpose(ps_h[:, mg % 2, k, i, 0:p], h[0:p, mg % 2, k, i * P:(i + 1) * P],
                                             c["ident"][0:p, 0:p])
                    o.then_inc(h_turned, 1)

            run_steps(pe, step, NG + 1 + M, LO, HI, UN)


def edge_gcn(nc, c, t):
    UN, LO, HI = 8, 9, 49
    B, C, Q, O, SC = 1, 2, 3, 4, 5
    STEPS = EG + SC
    with ExitStack() as ctx:
        def sb(name, shape, dt=F32):
            return ctx.enter_context(nc.sbuf_tensor("g_" + name, shape, dt))

        def ps(name, shape):
            return ctx.enter_context(nc.psum_tensor("g_" + name, shape, F32))

        sem = phase_sems(nc, ctx, "_g")
        idx = sb("gather_idx", [P, 4, 2, ET], I32)
        fidx = sb("final_idx", [P, 4, ET], I32)
        srow = sb("src_rows", [P, 2, ET, XW])
        drow = sb("dst_rows", [P, 4, ET, XW])
        keys = sb("keys", [P, 2, ET * P])
        kc = sb("key_cols", [P, 2, ET + 1])
        S = sb("same_dst", [P, 2, ET, P])
        cm = sb("carry_to", [P, 2, ET, P])
        hs = sb("hs", [P, 2, ET, W])
        carry = sb("carry", [P, ET, W])
        hd = sb("hd", [P, ET, W])
        sums = sb("sums", [P, ET, W])
        both = sb("both", [P, ET, 2, 2, P])
        zb = sb("zb", [P, ET, W])
        z = sb("z", [P, 2, ET, W])
        zsq = sb("zsq", [P, ET, W])
        ss = sb("ss", [P, 2, ET])
        nrm = sb("nrm", [P, 2, ET])
        inv = sb("inv", [P, 2, ET])
        o_sb = sb("o_sb", [P, 4, ET, W])
        ps_a = ps("ps_a", [P, ET, W])
        ps_t = ps("ps_t", [P, ET, 2, 2, P])
        ps_z = ps("ps_z", [P, ET, W])

        s_loaded = [sem(f"s_loaded{i}") for i in range(2)]
        d_loaded = [sem(f"d_loaded{i}") for i in range(4)]
        keys_loaded = [sem(f"keys_loaded{i}") for i in range(2)]
        new_stored = [sem(f"new_stored{i}") for i in range(4)]
        (sp_passed, pool_passed, idx_ready, fidx_ready, kc_ready, S_ready, hs_ready, agg_mm, carry_ready, hd_ready,
         sums_ready, own_ready, hd_turned, sums_turned, both_ready, z_mm, zb_ready, z_ready, ss_ready, nrm_ready,
         nmax_ready, inv_ready, o_ready) = (sem(s) for s in (
            "sp_passed", "pool_passed", "idx_ready", "fidx_ready", "kc_ready", "S_ready", "hs_ready", "agg_mm",
            "carry_ready", "hd_ready", "sums_ready", "own_ready", "hd_turned", "sums_turned", "both_ready", "z_mm",
            "zb_ready", "z_ready", "ss_ready", "nrm_ready", "nmax_ready", "inv_ready", "o_ready"))
        block = ctx.enter_context(nc.Block())

        def exists(g):
            return not isinstance(g, int) or 0 <= g < EG

        @block.sync
        def _(sp):
            def step(s, m):
                pace(sp, sp_passed, S_ready, s - 1)
                sp.dma_start(keys[:, m % 2, :], t["KEYROW"][1, bass.ds(s * (ET * P), ET * P)].partition_broadcast(P)
                             ).then_inc(keys_loaded[m % 2], 16)

            run_steps(sp, step, EG, LO, HI, UN)

        @block.gpsimd
        def _(pool):
            bound = pool.to_reg(N - 1)

            def gather(tile, slot, kind, islot, loaded):
                for j in range(ET):
                    pool.indirect_dma_start(tile[:, slot, j, :], None, t["X2"][:, :],
                                            bass.IndirectOffsetOnAxis(idx[:, islot, kind, j:j + 1], 0)
                                            ).then_inc(loaded[slot], 16)

            def step(s, m):
                if exists(s):
                    if not isinstance(s, int) or s >= 4:
                        pool.wait_ge(d_loaded[m % 4], dma_count(s - 4, m % 4, 4, 16 * ET))
                        pool.sem_inc(pool_passed, 1)
                    if not isinstance(s, int) or s >= 2:
                        pool.wait_ge(s_loaded[m % 2], dma_count(s - 2, m % 2, 2, 16 * ET))
                        pool.sem_inc(pool_passed, 1)
                    pool.tensor_copy(idx[:, m % 4, 0, :], c["keyI"][:, 1, bass.ds(s * ET, ET)])
                    pool.tensor_copy(idx[:, m % 4, 1, :], c["otherI"][:, 1, bass.ds(s * ET, ET)]).then_inc(idx_ready, 1)
                    pace(pool, pool_passed, idx_ready, s + 1)
                    pace(pool, pool_passed, hs_ready, s - 1)
                    gather(srow, m % 2, 1, m % 4, s_loaded)
                    pace(pool, pool_passed, o_ready, s - 3)
                    gather(drow, m % 4, 0, m % 4, d_loaded)
                g, mg = s - SC, m - SC
                if exists(g):
                    if not isinstance(g, int) or g >= 4:
                        pool.wait_ge(new_stored[mg % 4], dma_count(g - 4, mg % 4, 4, 16 * ET))
                        pool.sem_inc(pool_passed, 1)
                    pool.tensor_copy(fidx[:, mg % 4, :], c["finI"][:, 1, bass.ds(g * ET, ET)]).then_inc(fidx_ready, 1)
                    pace(pool, pool_passed, fidx_ready, g + 1)
                    pace(pool, pool_passed, o_ready, g + 1)
                    for j in range(ET):
                        pool.indirect_dma_start(t["out"][:, :], bass.IndirectOffsetOnAxis(fidx[:, mg % 4, j:j + 1], 0),
                                                o_sb[:, mg % 4, j, :], None,
                                                bounds_check=bound, oob_is_err=False).then_inc(new_stored[mg % 4], 16)

            run_steps(pool, step, STEPS, LO, HI, UN)
            for k in range(4):
                pool.wait_ge(new_stored[k], 16 * ET * len(range(k, EG, 4)))

        @block.vector
        def _(dve):
            def step(s, m):
                g, mg = s - O, m - O
                if exists(g):
                    p2 = mg % 2
                    need(dve, nrm_ready, g + 1)
                    dve.tensor_scalar(nrm[:, p2, :], nrm[:, p2, :], EPS_L2, None, ALU.max).then_inc(nmax_ready, 1)
                    need(dve, nmax_ready, g + 1)
                    dve.reciprocal(inv[:, p2, :], nrm[:, p2, :]).then_inc(inv_ready, 1)
                    need(dve, inv_ready, g + 1)
                    if not isinstance(g, int) or g >= 4:
                        dve.wait_ge(new_stored[mg % 4], dma_count(g - 4, mg % 4, 4, 16 * ET))
                    for j in range(ET):
                        o = dve.scalar_tensor_tensor(out=o_sb[:, mg % 4, j, :], in0=z[:, p2, j, :],
                                                     scalar=inv[:, p2, j:j + 1], in1=drow[:, mg % 4, j, 0:W],
                                                     op0=ALU.mult, op1=ALU.add)
                    o.then_inc(o_ready, 1)
                g, mg = s - B, m - B
                if exists(g):
                    p2 = mg % 2
                    lo = 1 if isinstance(g, int) and g == 0 else 0
                    if lo:
                        dve.memset(kc[:, p2, 0:1], -1.0)
                    dve.tensor_copy(kc[:, p2, lo:], c["ek"][:, 0, 1, bass.ds(g * ET - 1 + lo, ET + 1 - lo)]).then_inc(kc_ready, 1)
                    need(dve, kc_ready, g + 1)
                    dve.wait_ge(keys_loaded[p2], dma_count(g, p2, 2))
                    need(dve, agg_mm, (g - 1) * ET)
                    for j in range(ET):
                        kj = keys[:, p2, j * P:(j + 1) * P]
                        dve.tensor_scalar(S[:, p2, j, :], kj, kc[:, p2, j + 1:j + 2], None, ALU.is_equal)
                        o = dve.tensor_scalar(cm[QUAD:, p2, j, :], kj[QUAD:, :], kc[QUAD:, p2, j:j + 1],
                                              c["e127"][QUAD:, :], ALU.is_equal, ALU.mult)
                    o.then_inc(S_ready, 1)
                g, mg = s - C, m - C
                if exists(g):
                    need(dve, carry_ready, (g + 1) * ET)
                    need(dve, hd_ready, g + 1)
                    need(dve, sums_turned, g)
                    for j in range(ET):
                        dinv = drow[:, mg % 4, j, W + 4:W + 5]
                        o = dve.scalar_tensor_tensor(out=sums[:, j, :], in0=hd[:, j, :], scalar=dinv,
                                                     in1=ps_a[:, j, :], op0=ALU.mult, op1=ALU.add)
                    o.then_inc(sums_ready, 1)
                    need(dve, sums_ready, g + 1)
                    for j in range(ET):
                        dinv = drow[:, mg % 4, j, W + 4:W + 5]
                        o = dve.tensor_scalar(sums[:, j, :], sums[:, j, :], dinv, None, ALU.mult)
                    o.then_inc(own_ready, 1)
                    for kind, turned in ((1, hd_turned), (0, sums_turned)):
                        need(dve, turned, g + 1)
                        need(dve, z_mm, g)
                        for b in range(2):
                            o = dve.tensor_copy(both[:, 2 * b:2 * b + 2, kind, :, :], ps_t[:, 2 * b:2 * b + 2, kind, :, :])
                        o.then_inc(both_ready, 1)
                g, mg = s - Q, m - Q
                if exists(g):
                    need(dve, z_mm, g + 1)
                    need(dve, z_ready, g)
                    dve.tensor_tensor(zb[:, :, :], ps_z[:, :, :], spread(c["bg"], P, ET, W), ALU.add).then_inc(zb_ready, 1)

            run_steps(dve, step, EG + O, LO, HI, UN)

        @block.scalar
        def _(act):
            def step(s, m):
                g, mg = s - B, m - B
                if exists(g):
                    act.wait_ge(s_loaded[mg % 2], dma_count(g, mg % 2, 2, 16 * ET))
                    need(act, agg_mm, (g - 1) * ET)
                    for j in range(ET):
                        row = srow[:, mg % 2, j, :]
                        o = nc.scalar.activation(hs[:, mg % 2, j, :], row[:, 0:W], ACT.Relu,
                                                 bias=row[:, W + 3:W + 4], scale=row[:, W + 2:W + 3])
                    o.then_inc(hs_ready, 1)
                g, mg = s - C, m - C
                if exists(g):
                    act.wait_ge(d_loaded[mg % 4], dma_count(g, mg % 4, 4, 16 * ET))
                    need(act, hd_turned, g)
                    need(act, sums_ready, g)
                    for j in range(ET):
                        row = drow[:, mg % 4, j, :]
                        o = nc.scalar.activation(hd[:, j, :], row[:, 0:W], ACT.Relu,
                                                 bias=row[:, W + 1:W + 2], scale=row[:, W:W + 1])
                    o.then_inc(hd_ready, 1)
                    for j in range(ET):
                        need(act, agg_mm, g * ET + j + 1)
                        nc.scalar.copy(carry[QUAD:, j, :], ps_a[QUAD:, j, :]).then_inc(carry_ready, 1)
                g, mg = s - Q, m - Q
                if exists(g):
                    p2 = mg % 2
                    need(act, zb_ready, g + 1)
                    need(act, o_ready, g - 1)
                    nc.scalar.activation(z[:, p2, :, :], zb[:, :, :], ACT.Relu).then_inc(z_ready, 1)
                    need(act, z_ready, g + 1)
                    need(act, ss_ready, g)
                    for j in range(ET):
                        o = nc.scalar.activation(zsq[:, j, :], z[:, p2, j, :], ACT.Square, accum_out=ss[:, p2, j:j + 1])
                    o.then_inc(ss_ready, 1)
                    need(act, ss_ready, g + 1)
                    need(act, inv_ready, g - 1)
                    nc.scalar.activation(nrm[:, p2, :], ss[:, p2, :], ACT.Sqrt).then_inc(nrm_ready, 1)

            run_steps(act, step, EG + Q, LO, HI, UN)

        @block.tensor
        def _(pe):
            def step(s, m):
                g, mg = s - Q, m - Q
                if exists(g):
                    need(pe, both_ready, 2 * g + 2)
                    need(pe, zb_ready, g)
                    for j in range(ET):
                        for kind, w in ((0, c["wg"]), (1, c["wv"])):
                            for i in range(2):
                                o = pe.matmul(ps_z[:, j, :], both[:, j, kind, i, :], w[:, i, :],
                                              start=kind == 0 and i == 0, stop=kind == 1 and i == 1)
                    o.then_inc(z_mm, 1)
                g, mg = s - C, m - C
                if exists(g):
                    p2 = mg % 2
                    need(pe, S_ready, g + 1)
                    need(pe, hs_ready, g + 1)
                    need(pe, sums_ready, g)
                    for j in range(ET):
                        first = isinstance(g, int) and g == 0 and j == 0
                        need(pe, carry_ready, g * ET + j)
                        o = pe.matmul(ps_a[:, j, :], S[:, p2, j, :], hs[:, p2, j, :], start=True, stop=first)
                        if not first:
                            o = pe.matmul(ps_a[:, j, :], cm[QUAD:, p2, j, :], carry[QUAD:, (j - 1) % ET, :],
                                          start=False, stop=True)
                        o.then_inc(agg_mm, 1)
                    for kind, tile, ready, turned in ((1, hd, hd_ready, hd_turned), (0, sums, own_ready, sums_turned)):
                        need(pe, ready, g + 1)
                        need(pe, both_ready, 2 * g + (0 if kind else 1))
                        for j in range(ET):
                            for i in range(2):
                                o = pe.transpose(ps_t[:, j, kind, i, :], tile[:, j, i * P:(i + 1) * P], c["ident"][:, :])
                        o.then_inc(turned, 1)

            run_steps(pe, step, EG + Q, LO, HI, UN)


_INS = ['x', 'src', 'dst', 'L0_gnn_W_P_w', 'L0_gnn_W_P_b', 'L0_gnn_W_pos', 'L0_gnn_q1', 'L0_gnn_k1', 'L0_gnn_v1',
        'L0_gnn_ln1_s', 'L0_gnn_ln1_b', 'L0_gnn_q2', 'L0_gnn_k2', 'L0_gnn_v2', 'L0_gnn_ln2_s', 'L0_gnn_ln2_b',
        'L0_gnn_inv_w', 'L0_gnn_inv_b', 'L1_gnn_W_gcn', 'L1_gnn_b_gcn', 'L1_gnn_W_V']
_OUTS = [((50000, 256), 'float32')]


def kernel(**inputs):
    import numpy as _np
    import concourse.bacc as _bacc
    from concourse import mybir as _mybir
    from concourse.bass_utils import run_bass_kernel_spmd as _run

    nc = _bacc.Bacc("TRN2", target_bir_lowering=False, num_devices=1)
    arrays, args = {}, []
    for name in _INS:
        a = _np.ascontiguousarray(inputs[name])
        arrays[f"in_{name}_dram"] = a
        args.append(nc.dram_tensor(f"in_{name}_dram", a.shape, _mybir.dt.from_np(a.dtype), kind="ExternalInput").ap())
    for i, (shape, dtype) in enumerate(_OUTS):
        dt = _mybir.dt.from_np(_np.dtype(dtype))
        args.append(nc.dram_tensor(f"out_{i}_dram", shape, dt, kind="ExternalOutput").ap())
    program(nc, *args)
    r = _run(nc, [arrays], core_ids=[0])
    got = tuple(r.results[0][f"out_{i}_dram"] for i in range(len(_OUTS)))
    return got[0]
```

```python
from contextlib import ExitStack

import concourse.bass as bass
from concourse import mybir

ALU = mybir.AluOpType
ACT = mybir.ActivationFunctionType
AX_X = mybir.AxisListType.X
F32 = mybir.dt.float32
BF16 = mybir.dt.bfloat16
I32 = mybir.dt.int32

P = 128
QUAD = 96
N = 50000
E = 25000
W = 256
D = 128
HEADS = 8
HD = D // HEADS
NT = -(-E // P)
EP = NT * P
HT = NT // 2
ET = 4
EG = NT // ET
G = 3
NG = N // (G * P)
TAIL = N - NG * G * P
DIG = 256
KEYS = DIG * DIG
EW = D + 4
XW = W + 8
LIST = EP + P
SKIP = 100000.0
EPS_X = 1e-5
EPS_E = 1e-6
EPS_ATT = 1e-8
EPS_L2 = 1e-12
BETA = 0.1
assert TAIL <= P and NT % (2 * ET) == ET and N <= KEYS


def need(eng, sem, count):
    if isinstance(count, int) and count <= 0:
        return
    eng.wait_ge(sem, count)


def pace(eng, passed, sem, count):
    if isinstance(count, int) and count <= 0:
        return
    eng.wait_ge(sem, count)
    eng.sem_inc(passed, 1)


def dma_count(g, slot, slots, per=16):
    return (g - slot) * (per // slots) + per


def phase_sems(nc, ctx, suffix=""):
    held = []

    def close():
        nc.clear_and_free_semaphores(held)
        nc.all_engine_barrier()

    def sem(name):
        held.append(nc.alloc_semaphore(name + suffix))
        return held[-1]

    ctx.callback(close)
    return sem


def run_steps(eng, step, total, lo, hi, unroll):
    assert (hi - lo) % unroll == 0
    for s in range(lo):
        step(s, s % unroll)
    with eng.Fori(lo, hi - unroll + 1, unroll) as i:
        for u in range(unroll):
            step(i + u, (lo + u) % unroll)
    for s in range(hi, total):
        step(s, s % unroll)


def program(nc, x, src, dst, W_P_w, W_P_b, W_pos, q1, k1, v1, ln1_s, ln1_b, q2, k2, v2, ln2_s,
            ln2_b, inv_w, inv_b, W_gcn, b_gcn, W_V, out):
    def dram(name, shape, dt=F32):
        return nc.dram_tensor(name, shape, dt, kind="Internal").ap()

    t = {
        "E0": dram("embed0", [N, EW]), "E1": dram("embed1", [N, EW]), "X2": dram("x2_rows", [N, XW]),
        "SORTED": dram("sorted_pairs", [2 * LIST, 2], I32),
        "DIGROW": dram("key_rows", [2, 2, EP]), "KEYROW": dram("sorted_key_rows", [2, EP]),
        "AUX": dram("node_aux", [2, KEYS]),
        "x": x, "src": src, "dst": dst, "out": out,
    }
    with ExitStack() as ctx:
        def sb(name, shape, dt=F32):
            return ctx.enter_context(nc.sbuf_tensor(name, shape, dt))

        c = {}
        for name, shape in (("ident", [P, P]), ("ones", [P, P]), ("wP", [P, 2, D]), ("bias0", [P, D]),
                            ("qkv1", [P, 3, D]), ("qkv2", [P, 3, D]), ("ln1s", [P, D]), ("ln1b", [P, D]),
                            ("w2", [P, W]), ("w2c", [P, W]), ("bias2", [P, W]), ("wg", [P, 2, W]), ("bg", [P, W]),
                            ("wv", [P, 2, W]), ("hth", [P, 2, W]), ("eps", [P, 2]), ("e127", [P, 1])):
            c[name] = sb(name, shape)
        c["ek"] = sb("ek", [P, 3, 2, NT])
        c["fin"] = sb("fin", [P, 2, NT])
        for name in ("keyI", "otherI", "finI"):
            c[name] = sb(name, [P, 2, NT], I32)
        weights(nc, c, W_P_w, W_P_b, W_pos, q1, k1, v1, ln1_s, ln1_b, q2, k2, v2, ln2_s, ln2_b,
                inv_w, inv_b, W_gcn, b_gcn, W_V)
        rank_edges(nc, c, t)
        dense_embed(nc, c, t)
        unpack_lists(nc, c, t)
        edge_attention(nc, c, t, 1)
        edge_attention(nc, c, t, 2)
        dense_gcn(nc, c, t)
        edge_gcn(nc, c, t)


def weights(nc, c, W_P_w, W_P_b, W_pos, q1, k1, v1, ln1_s, ln1_b, q2, k2, v2, ln2_s, ln2_b,
            inv_w, inv_b, W_gcn, b_gcn, W_V):
    with ExitStack() as ctx:
        def sb(name, shape, dt=F32):
            return ctx.enter_context(nc.sbuf_tensor(name, shape, dt))

        sem = phase_sems(nc, ctx)

        pos_b = sb("pos_b", [P, D])
        ln2s_col = sb("ln2s_col", [P, 1])
        ln2b_col = sb("ln2b_col", [P, 1])
        ln2b_all = sb("ln2b_all", [P, P])
        invb = sb("invb", [P, W])
        ps_bias = ctx.enter_context(nc.psum_tensor("ps_bias", [P, W], F32))
        ps_mean = ctx.enter_context(nc.psum_tensor("ps_mean", [P, W], F32))
        loaded = sem("weights_loaded")
        ones_set = sem("ones_set")
        ident_set = sem("ident_set")
        col_spread = sem("ln2b_spread")
        bias_mm = sem("bias_mm")
        scaled = sem("w2_scaled")
        mean_mm = sem("w2_mean_mm")
        row = lambda a: a.partition_broadcast(P)
        loads = [
            (c["wP"][:, :, :], W_P_w.rearrange("(h p) n -> p h n", p=P)),
            (c["wg"][:, :, :], W_gcn.rearrange("(h p) n -> p h n", p=P)),
            (c["wv"][:, :, :], W_V.rearrange("(h p) n -> p h n", p=P)),
            (c["w2"][:, :], inv_w), (ln2s_col[:, :], ln2_s.rearrange("(p a) -> p a", a=1)),
            (ln2b_col[:, :], ln2_b.rearrange("(p a) -> p a", a=1)),
            (c["bias0"][:, :], row(W_P_b)), (pos_b[:, :], row(W_pos[0])),
            (c["ln1s"][:, :], row(ln1_s)), (c["ln1b"][:, :], row(ln1_b)),
            (invb[:, :], row(inv_b)), (c["bg"][:, :], row(b_gcn)),
        ]
        for name, ws in (("qkv1", (q1, k1, v1)), ("qkv2", (q2, k2, v2))):
            loads += [(c[name][:, i, :], w) for i, w in enumerate(ws)]
        block = ctx.enter_context(nc.Block())

        @block.sync
        def _(sp):
            for o, i in loads:
                sp.dma_start(o, i).then_inc(loaded, 16)

        @block.gpsimd
        def _(pool):
            pool.memset(c["ones"][:, :], 1.0).then_inc(ones_set, 1)
            pool.memset(c["eps"][:, 0:1], EPS_X)
            pool.memset(c["eps"][:, 1:2], EPS_E)
            pool.wait_ge(ones_set, 1)
            pool.affine_select(out=c["ident"][:, :], in_=c["ones"][:, :], compare_op=ALU.is_equal, fill=0.0,
                               base=0, pattern=[[1, P]], channel_multiplier=-1)
            pool.affine_select(out=c["e127"][:, :], in_=c["ones"][:, 0:1], compare_op=ALU.is_equal, fill=0.0,
                               base=1 - P, pattern=[[0, 1]], channel_multiplier=1).then_inc(ident_set, 1)

        @block.vector
        def _(dve):
            dve.wait_ge(loaded, 16 * len(loads))
            dve.wait_ge(ones_set, 1)
            dve.tensor_scalar(ln2b_all[:, :], c["ones"][:, :], ln2b_col[:, :], None, ALU.mult).then_inc(col_spread, 1)
            dve.tensor_tensor(c["bias0"][:, :], c["bias0"][:, :], pos_b[:, :], ALU.add)
            dve.wait_ge(bias_mm, 1)
            dve.tensor_tensor(c["bias2"][:, :], ps_bias[:, :], invb[:, :], ALU.add)
            dve.tensor_scalar(c["w2"][:, :], c["w2"][:, :], ln2s_col[:, :], None, ALU.mult).then_inc(scaled, 1)
            dve.wait_ge(mean_mm, 1)
            dve.scalar_tensor_tensor(out=c["w2c"][:, :], in0=ps_mean[:, :], scalar=-1.0 / D, in1=c["w2"][:, :],
                                     op0=ALU.mult, op1=ALU.add)

        @block.tensor
        def _(pe):
            pe.wait_ge(col_spread, 1)
            pe.matmul(ps_bias[:, :], ln2b_all[:, :], c["w2"][:, :], start=True, stop=True).then_inc(bias_mm, 1)
            pe.wait_ge(scaled, 1)
            pe.matmul(ps_mean[:, :], c["ones"][:, :], c["w2"][:, :], start=True, stop=True).then_inc(mean_mm, 1)


def rank_edges(nc, c, t):
    with ExitStack() as ctx:
        def sb(name, shape, dt=F32):
            return ctx.enter_context(nc.sbuf_tensor(name, shape, dt))

        def ps(name, shape):
            return ctx.enter_context(nc.psum_tensor(name, shape, F32))

        sem = phase_sems(nc, ctx)

        keyT = sb("keyT", [HT, 2, 2, P], I32)
        digT = sb("digT", [HT, 2, 2, 2, P], I32)
        keyTF = sb("keyTF", [HT, 3, 2, 2, P])
        ke = sb("ke", [P, 3, 2, NT])
        iota = sb("iota_digit", [P, DIG], BF16)
        pcol = sb("pcol", [P, 2])
        below = sb("below", [P, P])
        earlier = sb("earlier", [P, ET * P])
        oh = sb("onehot", [P, 2 * ET, 2, DIG], BF16)
        cnt = sb("cnt", [P, 2, 2, DIG])
        inc = sb("inc", [P, 2, 2, DIG])
        onesw = sb("onesw", [P, DIG])
        aux = sb("aux_out", [P, 2, 2, DIG])
        base = sb("base", [P, 4])
        start = sb("start", [P, 2, 2, DIG])
        seen = sb("seen", [P, 2, 2, DIG])
        krow = sb("krow", [P, 2, ET * P])
        hrow = sb("hrow", [P, 2, ET * P])
        ohT = sb("onehotT", [P, 2, 2, ET * P])
        dupj = sb("dup_junk", [P, ET, ET * P])
        selj = sb("sel_junk", [P, ET, DIG])
        dup = sb("dup", [P, 2, ET])
        sel = sb("sel", [P, ET])
        pairs = sb("pairs", [P, NT, 2], I32)
        idx = sb("scatter_idx", [P, 2, ET], I32)
        pay = sb("scatter_pairs", [P, 2, ET, 2], I32)
        nextT = sb("next_dst", [HT, 2, P], I32)
        nextTF = sb("next_dst_f", [HT, 2, P])
        falls = sb("falls", [HT, 2, P])
        fallen = sb("fallen", [HT, 1])
        unsorted = sb("unsorted", [P, 1], I32)
        pairT = sb("pairs_by_row", [HT, 2, P, 2], I32)
        npcol = sb("npcol", [P, 2])
        off = sb("digit_off", [P, 2, ET * P])
        pos = sb("pos", [P, 2 * NT])
        sentinel = sb("sentinel", [2, 2], I32)
        hist = [ps(f"hist{i}", [P, 512]) for i in range(4)]
        rows = ps("rows", [P, ET, DIG])
        runs = [ps(f"runs{i}", [P, 512]) for i in range(2)]

        def chosen(slot, j):
            return hist[j // 2][:, (j % 2) * DIG:(j % 2 + 1) * DIG] if slot else rows[:, j, :]


        padded = sem("keys_padded")
        loaded = sem("keys_loaded")
        digits = sem("digits")
        floats = sem("floats")
        rows_stored = sem("key_rows_stored")
        consts = sem("rank_consts")
        turned = sem("keys_turned")
        ke_ready = sem("ke_ready")
        oh_ready = sem("onehot_ready")
        oh_used = sem("onehot_used")
        cnt_ready = sem("cnt_ready")
        aux_ready = sem("aux_ready")
        aux_root = sem("aux_root")
        aux_stored = sem("aux_stored")
        scanned = sem("scanned")
        base_mm = sem("base_mm")
        base_ready = sem("base_ready")
        start_ready = sem("start_ready")
        krow_loaded = [sem(f"krow_loaded{i}") for i in range(2)]
        sp_passed = sem("rank_sp_passed")
        ohT_ready = sem("onehotT_ready")
        dup_ready = sem("dup_ready")
        rows_ready = sem("rows_ready")
        sel_ready = sem("sel_ready")
        oh2_ready = sem("onehot2_ready")
        run_ready = sem("run_ready")
        seen_ready = sem("seen_ready")
        pos_ready = sem("pos_ready")
        pairs_ready = sem("pairs_ready")
        pairT_ready = sem("pairs_by_row_ready")
        next_ready = sem("next_dst_ready")
        falls_ready = sem("falls_ready")
        fallen_ready = sem("fallen_ready")
        fallen_mm = sem("fallen_mm")
        unsorted_ready = sem("unsorted_ready")
        idx_ready = sem("scatter_idx_ready")
        pool_passed = sem("rank_pool_passed")
        npcol_ready = sem("npcol_ready")
        off_ready = sem("digit_off_ready")
        pair_stored = [sem(f"pair_stored{i}") for i in range(2)]
        block = ctx.enter_context(nc.Block())

        def if_unsorted(eng):
            eng.wait_ge(unsorted_ready, 1)
            return eng.If(eng.value_load(unsorted[0:1, 0:1]) > 0)

        def rank_steps(eng, step, l):
            for b in range(l * EG, l * EG + 3):
                step(b, b, l)
            with eng.Fori(l * EG + 3, (l + 1) * EG - 1, 2) as i:
                for u in range(2):
                    step(i + u, l * EG + 3 + u, l)

        @block.sync
        def _(sp):
            sp.wait_ge(padded, 2)
            full = (NT - 1) * P
            for l, a in enumerate((t["src"], t["dst"])):
                sp.dma_start(keyT[:, l, 0, :], a[0:HT * P].rearrange("(r c) -> r c", c=P)).then_inc(loaded, 16)
                sp.dma_start(keyT[0:HT - 1, l, 1, :], a[HT * P:full].rearrange("(r c) -> r c", c=P)).then_inc(loaded, 16)
                sp.dma_start(keyT[HT - 1:HT, l, 1, 0:E - full], a[full:E].rearrange("(r c) -> r c", r=1)).then_inc(loaded, 16)
            a = t["dst"]
            sp.dma_start(nextT[:, 0, :], a[1:1 + HT * P].rearrange("(r c) -> r c", c=P)).then_inc(loaded, 16)
            sp.dma_start(nextT[0:HT - 1, 1, :], a[1 + HT * P:1 + full].rearrange("(r c) -> r c", c=P)).then_inc(loaded, 16)
            sp.dma_start(nextT[HT - 1:HT, 1, 0:E - full - 1], a[full + 1:E].rearrange("(r c) -> r c", r=1)).then_inc(loaded, 16)
            sp.wait_ge(pairT_ready, 2)
            sp.dma_start(t["SORTED"][LIST:LIST + EP, :].rearrange("(a r c) k -> r a (c k)", a=2, c=P).rearrange(
                "r a (c k) -> r a c k", k=2), pairT[:, :, :, :]).then_inc(rows_stored, 16)
            sp.wait_ge(floats, 2)
            for kind in range(2):
                for l in range(2):
                    sp.dma_start(t["DIGROW"][kind, l].rearrange("(a r c) -> r a c", a=2, c=P),
                                 keyTF[:, kind, l, :, :]).then_inc(rows_stored, 16)
            for l in range(2):
                sp.dma_start(t["SORTED"][l * LIST + EP:l * LIST + EP + 2, :], sentinel[:, :]).then_inc(rows_stored, 16)
            sp.wait_ge(rows_stored, 112)

            def step(b, m, l):
                pace(sp, sp_passed, dup_ready, b - 1)
                pace(sp, sp_passed, ohT_ready, b - 1)
                off = (b - l * EG) * (ET * P)
                for tile, kind in ((krow, 0), (hrow, 1)):
                    sp.dma_start(tile[:, m % 2, :], t["DIGROW"][kind, l, bass.ds(off, ET * P)].partition_broadcast(P)
                                 ).then_inc(krow_loaded[m % 2], 16)

            step(0, 0, 0)
            step(1, 1, 0)

            def rest(l):
                lo = l * EG + 2
                with sp.Fori(lo, (l + 1) * EG - 2, 2) as i:
                    for u in range(2):
                        step(i + u, lo + u, l)
                step((l + 1) * EG - 1, (l + 1) * EG - 1, l)

            rest(0)
            with if_unsorted(sp):
                step(EG, EG, 1)
                step(EG + 1, EG + 1, 1)
                rest(1)
            sp.wait_ge(aux_ready, 2)
            for k in range(2):
                sp.dma_start(t["AUX"][k].rearrange("(h p l) -> p h l", h=2, l=DIG), aux[:, k, :, :]).then_inc(aux_stored, 16)
            sp.wait_ge(aux_stored, 32)

        @block.gpsimd
        def _(pool):
            pool.iota(iota[:, :], [[1, DIG]], base=0, channel_multiplier=0, allow_small_or_imprecise_dtypes=True)
            for h in range(2):
                pool.iota(pcol[:, h:h + 1], [[0, 1]], base=h * P, channel_multiplier=1,
                          allow_small_or_imprecise_dtypes=True)
            pool.memset(onesw[:, :], 1.0)
            pool.memset(earlier[:, 0:(ET - 1) * P], 1.0)
            pool.affine_select(out=below[:, :], in_=c["ones"][:, :], compare_op=ALU.is_gt, fill=0.0,
                               base=0, pattern=[[1, P]], channel_multiplier=-1)
            pool.affine_select(out=earlier[:, (ET - 1) * P:], in_=c["ones"][:, :], compare_op=ALU.is_gt, fill=0.0,
                               base=0, pattern=[[-1, P]], channel_multiplier=1).then_inc(consts, 1)
            pace(pool, pool_passed, pairs_ready, 2)
            pace(pool, pool_passed, rows_stored, 112)

            def step(b, m, l):
                slot = m % 2
                if not isinstance(b, int) or b >= 2:
                    pool.wait_ge(pair_stored[slot], dma_count(b - 2, slot, 2, 16 * ET))
                    pool.sem_inc(pool_passed, 1)
                pace(pool, pool_passed, pos_ready, b + 1)
                pool.tensor_copy(idx[:, slot, :], pos[:, bass.ds(b * ET, ET)])
                pool.tensor_copy(pay[:, slot, :, :], pairs[:, bass.ds((b - l * EG) * ET, ET), :]).then_inc(idx_ready, 1)
                pace(pool, pool_passed, idx_ready, b + 1)
                for j in range(ET):
                    pool.indirect_dma_start(t["SORTED"][:, :], bass.IndirectOffsetOnAxis(idx[:, slot, j:j + 1], 0),
                                            pay[:, slot, j, :], None).then_inc(pair_stored[slot], 16)

            rank_steps(pool, step, 0)
            for i in range(2):
                pool.wait_ge(pair_stored[i], 16 * ET * len(range(i, EG, 2)))
            with if_unsorted(pool):
                rank_steps(pool, step, 1)
                for i in range(2):
                    pool.wait_ge(pair_stored[i], 16 * ET * EG)

        @block.vector
        def _(dve):
            dve.memset(sentinel[:, :], 2 * N)
            dve.memset(keyT[:, :, :, :], N).then_inc(padded, 1)
            dve.memset(nextT[:, :, :], N).then_inc(padded, 1)
            dve.wait_ge(loaded, 144)
            dve.tensor_scalar(digT[:, 0, :, :, :], keyT[:, :, :, :], 8, None, ALU.logical_shift_right)
            dve.tensor_scalar(digT[:, 1, :, :, :], keyT[:, :, :, :], 255, None, ALU.bitwise_and).then_inc(digits, 1)
            dve.tensor_copy(keyTF[:, 0, :, :, :], keyT[:, :, :, :]).then_inc(floats, 1)
            for l in range(2):
                dve.tensor_copy(pairT[:, :, :, l], keyT[:, l, :, :]).then_inc(pairT_ready, 1)
            dve.tensor_copy(nextTF[:, :, :], nextT[:, :, :]).then_inc(next_ready, 1)
            dve.wait_ge(digits, 1)
            dve.tensor_copy(keyTF[:, 1, :, :, :], digT[:, 0, :, :, :]).then_inc(floats, 1)
            dve.tensor_copy(keyTF[:, 2, :, :, :], digT[:, 1, :, :, :]).then_inc(floats, 1)
            dve.wait_ge(ke_ready, 3)
            for l in range(2):
                dve.tensor_copy(pairs[:, :, l], ke[:, 0, l, :]).then_inc(pairs_ready, 1)
            dve.wait_ge(next_ready, 1)
            dve.tensor_tensor(falls[:, :, :], keyTF[:, 0, 1, :, :], nextTF[:, :, :], ALU.is_gt).then_inc(falls_ready, 1)
            dve.wait_ge(falls_ready, 1)
            dve.tensor_reduce(fallen[:, :], falls[:, :, :].rearrange("r a c -> r (a c)"), AX_X, ALU.add).then_inc(fallen_ready, 1)
            dve.wait_ge(fallen_mm, 1)
            dve.tensor_copy(unsorted[:, :], runs[0][:, 0:1]).then_inc(unsorted_ready, 1)
            dve.wait_ge(consts, 1)
            dve.tensor_scalar(npcol[:, :], pcol[:, :], -1.0, None, ALU.mult).then_inc(npcol_ready, 1)

            def onehots(tile, j, l, ready):
                for d in range(2):
                    o = dve.tensor_scalar(oh[:, j, d, :], iota[:, :], ke[:, 1 + d, l, bass.ds(tile, 1)], None, ALU.is_equal)
                o.then_inc(ready, 1)

            def count_tiles(base_tile, l, first):
                for j in range(ET):
                    n = base_tile + j + l * NT
                    if not first:
                        need(dve, oh_used, n + 1 - ET)
                    onehots(base_tile + j, j, l, oh_ready)

            for l in range(2):
                count_tiles(0, l, l == 0)
                with dve.Fori(ET, NT - 2 * ET + 1, ET) as i:
                    count_tiles(i, l, False)
                count_tiles(NT - ET, l, False)

            dve.wait_ge(oh_used, 2 * NT)
            for l in range(2):
                for h in range(2):
                    o = dve.tensor_copy(cnt[:, l, h, :], hist[2 * l + h][:, 0:DIG])
            o.then_inc(cnt_ready, 1)
            dve.wait_ge(cnt_ready, 1)
            dve.tensor_scalar(aux[:, 0, :, :], cnt[:, 0, :, :], 0.0, None, ALU.is_equal).then_inc(aux_ready, 1)
            dve.tensor_scalar(aux[:, 1, :, :], cnt[:, 1, :, :], 1.0, 1e-30, ALU.add, ALU.max).then_inc(aux_root, 1)
            for l in range(2):
                for h in range(2):
                    o = dve.tensor_tensor_scan(inc[:, l, h, :], onesw[:, :], cnt[:, l, h, :], 0.0, ALU.mult, ALU.add)
            o.then_inc(scanned, 1)
            dve.wait_ge(aux_root, 2)
            dve.reciprocal(aux[:, 1, :, :], aux[:, 1, :, :]).then_inc(aux_ready, 1)
            dve.wait_ge(base_mm, 1)
            dve.tensor_copy(base[:, 0:2], rows[:, 0, 0:2]).then_inc(base_ready, 1)
            dve.tensor_scalar(base[:, 2:4], rows[:, 0, 2:4], float(LIST), None, ALU.add).then_inc(base_ready, 1)
            dve.wait_ge(base_ready, 2)
            dve.wait_ge(scanned, 1)
            for l in range(2):
                for h in range(2):
                    o = dve.scalar_tensor_tensor(out=start[:, l, h, :], in0=inc[:, l, h, :],
                                                 scalar=base[:, 2 * l + h:2 * l + h + 1], in1=cnt[:, l, h, :],
                                                 op0=ALU.add, op1=ALU.subtract)
            o.then_inc(start_ready, 1)

            def place(b, m):
                slot = m % 2
                need(dve, rows_ready, b + 1)
                need(dve, oh2_ready, (b + 1) * ET)
                need(dve, pos_ready, b)
                for j in range(ET):
                    o = dve.tensor_tensor_reduce(out=selj[:, j, :], in0=chosen(slot, j), in1=oh[:, slot * ET + j, 1, :],
                                                 scale=1.0, scalar=0.0, op0=ALU.mult, op1=ALU.add,
                                                 accum_out=sel[:, j:j + 1])
                o.then_inc(sel_ready, 1)
                need(dve, sel_ready, b + 1)
                need(dve, dup_ready, b + 1)
                dve.tensor_tensor(pos[:, bass.ds(b * ET, ET)], sel[:, :], dup[:, slot, :], ALU.add).then_inc(pos_ready, 1)

            def step(b, m, l):
                slot = m % 2
                tile = (b - l * EG) * ET
                need(dve, run_ready, b - 1)
                for j in range(ET):
                    onehots(tile + j, slot * ET + j, l, oh2_ready)
                dve.wait_ge(krow_loaded[slot], dma_count(b, slot, 2, 32))
                need(dve, pos_ready, b - 1)
                need(dve, dup_ready, b)
                for j in range(ET):
                    w = (j + 1) * P
                    o = dve.scalar_tensor_tensor(out=dupj[:, j, 0:w], in0=krow[:, slot, 0:w],
                                                 scalar=ke[:, 0, l, bass.ds(tile + j, 1)],
                                                 in1=earlier[:, (ET - 1 - j) * P:], op0=ALU.is_equal,
                                                 op1=ALU.mult, accum_out=dup[:, slot, j:j + 1])
                o.then_inc(dup_ready, 1)
                if m != l * EG:
                    place(b - 1, m - 1)

            dve.wait_ge(start_ready, 1)
            rank_steps(dve, step, 0)
            place(EG - 1, EG - 1)
            with if_unsorted(dve):
                rank_steps(dve, step, 1)
                place(2 * EG - 1, 2 * EG - 1)

        @block.scalar
        def _(act):
            for kind in range(3):
                act.wait_ge(turned, kind + 1)
                nc.scalar.copy(ke[:, kind, :, :].rearrange("p l t -> p (l t)"), hist[kind][:, 0:2 * NT]).then_inc(ke_ready, 1)
            act.wait_ge(aux_root, 1)
            nc.scalar.activation(aux[:, 1, :, :], aux[:, 1, :, :], ACT.Sqrt).then_inc(aux_root, 1)

            act.wait_ge(npcol_ready, 1)

            def step(b, m, l):
                slot = m % 2
                if not isinstance(b, int) or b >= 1:
                    need(act, run_ready, b)
                    need(act, rows_ready, b - 1)
                    for h in range(2):
                        o = nc.scalar.copy(seen[:, slot, h, :], runs[h][:, 0:DIG])
                    o.then_inc(seen_ready, 1)
                act.wait_ge(krow_loaded[slot], dma_count(b, slot, 2, 32))
                need(act, ohT_ready, b)
                need(act, rows_ready, b - 1)
                for h in range(2):
                    o = nc.scalar.activation(off[:, h, :], hrow[:, slot, :], ACT.Square, bias=npcol[:, h:h + 1])
                o.then_inc(off_ready, 1)
                need(act, off_ready, b + 1)
                nc.scalar.activation(ohT[:, slot, :, :], off[:, :, :], ACT.Relu, bias=c["ones"][:, 0:1],
                                     scale=-1.0).then_inc(ohT_ready, 1)

            rank_steps(act, step, 0)
            with if_unsorted(act):
                rank_steps(act, step, 1)

        @block.tensor
        def _(pe):
            for kind in range(3):
                pe.wait_ge(floats, kind + 1)
                for l in range(2):
                    for a in range(2):
                        at = (l * 2 + a) * HT
                        o = pe.transpose(hist[kind][:, at:at + HT], keyTF[:, kind, l, a, :], c["ident"][0:HT, 0:HT])
                o.then_inc(turned, 1)
            pe.wait_ge(fallen_ready, 1)
            pe.matmul(runs[0][:, 0:1], c["ones"][0:HT, :], fallen[:, :], start=True, stop=True).then_inc(fallen_mm, 1)
            pe.wait_ge(ke_ready, 3)

            def count(base_tile, l, first, last):
                for j in range(ET):
                    n = base_tile + j + l * NT
                    need(pe, oh_ready, n + 1)
                    for h in range(2):
                        o = pe.matmul(hist[2 * l + h][:, 0:DIG], oh[:, j, 0, h * P:(h + 1) * P], oh[:, j, 1, :],
                                      start=first and j == 0, stop=last and j == ET - 1)
                    o.then_inc(oh_used, 1)

            for l in range(2):
                count(0, l, True, False)
                with pe.Fori(ET, NT - 2 * ET + 1, ET) as i:
                    count(i, l, False, False)
                count(NT - ET, l, False, True)
            pe.wait_ge(scanned, 1)
            pe.wait_ge(consts, 1)
            for l in range(2):
                pe.matmul(rows[:, 0, 2 * l:2 * l + 1], below[:, :], inc[:, l, 0, DIG - 1:DIG], start=True, stop=True)
                pe.matmul(rows[:, 0, 2 * l + 1:2 * l + 2], below[:, :], inc[:, l, 1, DIG - 1:DIG], start=True, stop=False)
                o = pe.matmul(rows[:, 0, 2 * l + 1:2 * l + 2], c["ones"][:, :], inc[:, l, 0, DIG - 1:DIG],
                              start=False, stop=True)
            o.then_inc(base_mm, 1)
            pe.wait_ge(start_ready, 1)

            def step(b, m, l):
                slot = m % 2
                first = m == l * EG
                need(pe, oh2_ready, (b + 1) * ET)
                need(pe, seen_ready, b)
                for h in range(2):
                    if first:
                        pe.matmul(runs[h][:, 0:DIG], c["ident"][:, :], start[:, l, h, :], start=True, stop=False,
                                  skip_group_check=True)
                    for j in range(ET):
                        o = pe.matmul(runs[h][:, 0:DIG], oh[:, slot * ET + j, 0, h * P:(h + 1) * P],
                                      oh[:, slot * ET + j, 1, :], start=False, stop=j == ET - 1, skip_group_check=True)
                o.then_inc(run_ready, 1)
                need(pe, ohT_ready, b + 1)
                need(pe, sel_ready, b - 1)
                table = start[:, l, :, :] if first else seen[:, slot, :, :]
                for j in range(ET):
                    for h in range(2):
                        o = pe.matmul(chosen(slot, j), ohT[:, slot, h, j * P:(j + 1) * P], table[:, h, :],
                                      start=(h == 0 and j % 2 == 0), stop=(h == 1), skip_group_check=True)
                o.then_inc(rows_ready, 1)

            rank_steps(pe, step, 0)
            with if_unsorted(pe):
                rank_steps(pe, step, 1)


def spread(row, p, n, w):
    return row[0:p, :].unsqueeze(1).to_broadcast([p, n, w])


def dense_embed(nc, c, t):
    UN = 8
    LO, HI = 16, 128
    A, B, Z, L, M, X, R, H, T = range(9)
    STEPS = NG + 1 + T
    with ExitStack() as ctx:
        def sb(name, shape, dt=F32):
            return ctx.enter_context(nc.sbuf_tensor(name, shape, dt))

        def ps(name, shape):
            return ctx.enter_context(nc.psum_tensor(name, shape, F32))

        sem = phase_sems(nc, ctx)
        xt = sb("xt", [P, UN, G, W])
        h0 = sb("h0", [P, 2, G, W])
        hT = sb("hT", [P, 2, G, 2, P])
        e0 = sb("e0", [P, 4, G, EW])
        n1 = sb("n1", [P, 2, G, D])
        e1 = sb("e1", [P, 4, G, EW])
        e1T = sb("e1T", [P, 2, G, P])
        x2 = sb("x2", [P, 4, G, XW])
        r = sb("r", [P, 4, G, W])
        rsq = sb("rsq", [P, G, W])
        rw = sb("rw", [P, 2, G, W])
        SX, SX2, SE0, SE1 = range(4)
        st = sb("st", [P, 4, G, 6])
        mv = sb("mv", [P, 4, 4, G, 2])
        nmean = sb("nmean", [P, 4, 4, G])
        std = sb("std", [P, 4, 4, G])
        rstd = sb("rstd", [P, 4, 4, G])
        ss = sb("ss", [P, 2, G])
        root = sb("root", [P, 2, G])
        nrm = sb("nrm", [P, 2, 2, G])
        inv = sb("inv", [P, 2, G])
        k = sb("k", [P, 2, G])
        kn = sb("kn", [P, 2, G])
        w = sb("w", [P, 2, G])
        aux = sb("aux", [P, 2, (NG + 1) * G])
        ps_h = ps("ps_h", [P, 4, 2, P])
        ps_z = ps("ps_z", [P, 4, D])
        ps_e = ps("ps_e", [P, 4, D])
        ps_x = ps("ps_x", [P, 4, W])
        ps_hth = ps("ps_hth", [P, 2, W])

        x_loaded = [sem(f"x_loaded{i}") for i in range(UN)]
        e0_stored = [sem(f"e0_stored{i}") for i in range(4)]
        e1_stored = [sem(f"e1_stored{i}") for i in range(4)]
        x2_stored = [sem(f"x2_stored{i}") for i in range(4)]
        aux_loaded = sem("aux_loaded")
        sp_passed = sem("embed_sp_passed")
        pool_passed = sem("embed_pool_passed")
        dve_passed = sem("embed_dve_passed")
        cleared = sem("cleared")
        stat = [sem(f"stat{i}") for i in range(4)]
        mv_ready = sem("mv_ready")
        nmean_ready = sem("nmean_ready")
        std_ready = sem("std_ready")
        rstd_ready = sem("rstd_ready")
        h0_ready = sem("h0_ready")
        h0_turned = sem("h0_turned")
        hT_ready = sem("hT_ready")
        z_mm = sem("z_mm")
        e0_ready = sem("e0_ready")
        e0_aux = sem("e0_aux")
        n1_ready = sem("n1_ready")
        e1_scaled = sem("e1_scaled")
        e1_ready = sem("e1_ready")
        e1_turned = sem("e1_turned")
        e1T_ready = sem("e1T_ready")
        x2_mm = sem("x2_mm")
        xb_ready = sem("xb_ready")
        x2_ready = sem("x2_ready")
        r_ready = sem("r_ready")
        ss_ready = sem("ss_ready")
        root_ready = sem("root_ready")
        nrm_ready = sem("nrm_ready")
        nmax_ready = sem("nmax_ready")
        inv_ready = sem("inv_ready")
        k_ready = sem("k_ready")
        kn_ready = sem("kn_ready")
        w_ready = sem("w_ready")
        rw_ready = sem("rw_ready")
        hth_mm = sem("hth_mm")
        b_ready = sem("b_ready")
        row_ready = sem("row_ready")
        block = ctx.enter_context(nc.Block())

        def exists(g):
            return not isinstance(g, int) or 0 <= g <= NG

        def shape(g):
            return (TAIL, 1) if isinstance(g, int) and g == NG else (P, G)

        def nodes(ap, g):
            p, n = shape(g)
            return ap[bass.ds(g * (P * G), p * n), :].rearrange("(p k) c -> p k c", k=n)

        def stored(eng, sems, g, m, passed=None):
            if not isinstance(g, int) or g >= 4:
                eng.wait_ge(sems[m % 4], dma_count(g - 4, m % 4, 4))
                if passed is not None:
                    eng.sem_inc(passed, 1)

        def measured(s):
            return not isinstance(s, int) or 0 <= s <= NG + X

        @block.sync
        def _(sp):
            for i in range(2):
                sp.dma_start(aux[:, i, 0:NG * G].rearrange("p (g k) -> p g k", k=G),
                             t["AUX"][i, 0:NG * P * G].rearrange("(g p k) -> p g k", p=P, k=G)).then_inc(aux_loaded, 16)
                sp.dma_start(aux[0:TAIL, i, NG * G:NG * G + 1],
                             t["AUX"][i, NG * P * G:N].rearrange("(p k) -> p k", k=1)).then_inc(aux_loaded, 16)

            def load(g, m):
                if exists(g):
                    p, n = shape(g)
                    pace(sp, sp_passed, x2_ready, g - UN + 1)
                    sp.dma_start(xt[0:p, m % UN, 0:n, :], nodes(t["x"], g)).then_inc(x_loaded[m % UN], 16)

            def step(s, m):
                load(s + 2, m + 2)
                g, mg = s - L, m - L
                if exists(g):
                    p, n = shape(g)
                    pace(sp, sp_passed, e0_ready, g + 1)
                    pace(sp, sp_passed, e0_aux, g + 1)
                    sp.dma_start(nodes(t["E0"], g), e0[0:p, mg % 4, 0:n, :]).then_inc(e0_stored[mg % 4], 16)
                g, mg = s - M, m - M
                if exists(g):
                    p, n = shape(g)
                    pace(sp, sp_passed, e1_ready, g + 1)
                    sp.dma_start(nodes(t["E1"], g), e1[0:p, mg % 4, 0:n, :]).then_inc(e1_stored[mg % 4], 16)
                g, mg = s - T, m - T
                if exists(g):
                    p, n = shape(g)
                    pace(sp, sp_passed, row_ready, g + 1)
                    sp.dma_start(nodes(t["X2"], g), x2[0:p, mg % 4, 0:n, :]).then_inc(x2_stored[mg % 4], 16)

            load(0, 0)
            load(1, 1)
            run_steps(sp, step, STEPS, LO, HI - UN, UN)
            for stores in (e0_stored, e1_stored, x2_stored):
                for i in range(4):
                    sp.wait_ge(stores[i], 16 * len(range(i, NG + 1, 4)))

        @block.gpsimd
        def _(pool):
            pool.memset(e0[:, :, :, D:], 0.0)
            pool.memset(e1[:, :, :, D:], 0.0)
            pool.memset(x2[:, :, :, W:], 0.0)
            pool.memset(mv[:, :, :, :, :], 1.0).then_inc(cleared, 1)
            pool.wait_ge(cleared, 1)
            pool.wait_ge(aux_loaded, 64)

            def step(s, m):
                g, mg = s - Z, m - Z
                if exists(g):
                    p, n = shape(g)
                    xs = xt[0:p, mg % UN, 0:n, :]
                    pace(pool, pool_passed, h0_ready, g + 1)
                    pool.tensor_tensor(xs, xs, spread(c["bias2"], p, n, W), ALU.add).then_inc(xb_ready, 1)
                    stored(pool, e0_stored, g, mg, pool_passed)
                    pool.tensor_copy(e0[0:p, mg % 4, 0:n, D], aux[0:p, 1, bass.ds(g * G, n)]).then_inc(e0_aux, 1)
                g, mg = s - H, m - H
                if exists(g):
                    p, n = shape(g)
                    at = (m - 2) % 4
                    row = x2[0:p, mg % 4, 0:n, :]
                    pace(pool, pool_passed, k_ready, g + 1)
                    pool.tensor_copy(row[:, :, W], k[0:p, mg % 2, 0:n])
                    pool.tensor_copy(row[:, :, W + 4], aux[0:p, 1, bass.ds(g * G, n)])
                    pool.tensor_tensor(row[:, :, W + 1], nmean[0:p, at, SX2, 0:n], k[0:p, mg % 2, 0:n], ALU.mult).then_inc(b_ready, 1)
                    pace(pool, pool_passed, b_ready, g + 1)
                    pool.tensor_tensor(row[:, :, W + 2], row[:, :, W], row[:, :, W + 4], ALU.mult)
                    pool.tensor_tensor(row[:, :, W + 3], row[:, :, W + 1], row[:, :, W + 4], ALU.mult).then_inc(row_ready, 1)
                g, mg = s - L, m - L
                if exists(g):
                    p, n = shape(g)
                    es = e1[0:p, mg % 4, 0:n, 0:D]
                    stored(pool, e1_stored, g, mg, pool_passed)
                    pace(pool, pool_passed, stat[SE1], g - 3)
                    pace(pool, pool_passed, e1_turned, g - 3)
                    pool.tensor_copy(e1[0:p, mg % 4, 0:n, D], aux[0:p, 1, bass.ds(g * G, n)])
                    pace(pool, pool_passed, n1_ready, g + 1)
                    pool.tensor_tensor(es, n1[0:p, mg % 2, 0:n, :], spread(c["ln1s"], p, n, D), ALU.mult).then_inc(e1_scaled, 1)
                    pace(pool, pool_passed, e1_scaled, g + 1)
                    pool.tensor_tensor(es, es, spread(c["ln1b"], p, n, D), ALU.add).then_inc(e1_ready, 1)

            run_steps(pool, step, STEPS, LO, HI, UN)

        @block.vector
        def _(dve):
            def stats(tile, place, p, n):
                for j in range(n):
                    o = dve.bn_stats(st[0:p, place, j, :], tile[:, j, :])
                o.then_inc(stat[place], 1)

            def mean_var(place, m, p, n, g):
                need(dve, stat[place], g + 1)
                dve.sem_inc(dve_passed, 1)
                for j in range(n):
                    o = dve.bn_aggr(mv[0:p, m % 4, place, j, :], st[0:p, place, j, :])
                return o

            def step(s, m):
                par, before = m % 4, (m - 1) % 4
                gh, mh = s - H, m - H
                ph, nh = shape(gh)
                hs = mh % 2
                if exists(s):
                    p, n = shape(s)
                    dve.wait_ge(x_loaded[m % UN], dma_count(s, m % UN, UN))
                    stats(xt[0:p, m % UN, 0:n, :], SX, p, n)
                if exists(gh):
                    need(dve, root_ready, gh + 1)
                    dve.tensor_tensor(nrm[0:ph, hs, 0, 0:nh], root[0:ph, hs, 0:nh], rstd[0:ph, (m - 2) % 4, SX2, 0:nh],
                                      ALU.mult).then_inc(nrm_ready, 1)
                if exists(gh):
                    need(dve, nrm_ready, gh + 1)
                    dve.tensor_scalar(nrm[0:ph, hs, 1, 0:nh], nrm[0:ph, hs, 0, 0:nh], EPS_L2, None, ALU.max).then_inc(nmax_ready, 1)
                if measured(s - 1):
                    need(dve, std_ready, s)
                    dve.reciprocal(rstd[:, before, :, :], std[:, before, :, :]).then_inc(rstd_ready, 1)
                g, mg = s - M, m - M
                if exists(g):
                    p, n = shape(g)
                    need(dve, e1_ready, g + 1)
                    stats(e1[0:p, mg % 4, 0:n, 0:D], SE1, p, n)
                if exists(s):
                    p, n = shape(s)
                    last = mean_var(SX, m, p, n, s)
                if exists(gh):
                    need(dve, nmax_ready, gh + 1)
                    dve.reciprocal(inv[0:ph, hs, 0:nh], nrm[0:ph, hs, 1, 0:nh]).then_inc(inv_ready, 1)
                if measured(s - 1):
                    need(dve, rstd_ready, s)
                g, mg = s - L, m - L
                if exists(g):
                    p, n = shape(g)
                    need(dve, e1_scaled, g - 1)
                    for j in range(n):
                        o = dve.tensor_scalar(n1[0:p, mg % 2, j, :], e0[0:p, mg % 4, j, 0:D],
                                              nmean[0:p, before, SE0, j:j + 1], rstd[0:p, before, SE0, j:j + 1],
                                              ALU.add, ALU.mult)
                    o.then_inc(n1_ready, 1)
                if exists(gh):
                    need(dve, inv_ready, gh + 1)
                    need(dve, row_ready, gh - 1)
                    dve.tensor_tensor(k[0:ph, hs, 0:nh], inv[0:ph, hs, 0:nh], rstd[0:ph, (m - 2) % 4, SX2, 0:nh],
                                      ALU.mult).then_inc(k_ready, 1)
                g, mg = s - M, m - M
                if exists(g):
                    p, n = shape(g)
                    last = mean_var(SE1, m, p, n, g)
                g, mg = s - X, m - X
                if exists(g):
                    p, n = shape(g)
                    need(dve, x2_mm, g + 1)
                    need(dve, xb_ready, g + 1)
                    need(dve, r_ready, g - 3)
                    stored(dve, x2_stored, g, mg)
                    for j in range(n):
                        o = dve.scalar_tensor_tensor(out=x2[0:p, mg % 4, j, 0:W], in0=ps_x[0:p, j, :],
                                                     scalar=rstd[0:p, before, SE1, j:j + 1],
                                                     in1=xt[0:p, mg % UN, j, :], op0=ALU.mult, op1=ALU.add)
                    o.then_inc(x2_ready, 1)
                if exists(gh):
                    need(dve, k_ready, gh + 1)
                    dve.tensor_tensor(kn[0:ph, hs, 0:nh], k[0:ph, hs, 0:nh], aux[0:ph, 0, bass.ds(gh * G, nh)],
                                      ALU.mult).then_inc(kn_ready, 1)
                g, mg = s - Z, m - Z
                if exists(g):
                    p, n = shape(g)
                    need(dve, z_mm, g + 1)
                    stored(dve, e0_stored, g, mg)
                    for j in range(n):
                        o = dve.scalar_tensor_tensor(out=e0[0:p, mg % 4, j, 0:D], in0=ps_z[0:p, j, :],
                                                     scalar=rstd[0:p, (m - 2) % 4, SX, j:j + 1],
                                                     in1=c["bias0"][0:p, :], op0=ALU.mult, op1=ALU.add)
                    o.then_inc(e0_ready, 1)
                if exists(gh):
                    need(dve, kn_ready, gh + 1)
                    need(dve, rw_ready, gh - 1)
                    dve.tensor_tensor(w[0:ph, hs, 0:nh], kn[0:ph, hs, 0:nh], k[0:ph, hs, 0:nh], ALU.mult).then_inc(w_ready, 1)
                g, mg = s - X, m - X
                if exists(g):
                    p, n = shape(g)
                    need(dve, x2_ready, g + 1)
                    stats(x2[0:p, mg % 4, 0:n, 0:W], SX2, p, n)
                g, mg = s - Z, m - Z
                if exists(g):
                    p, n = shape(g)
                    need(dve, e0_ready, g + 1)
                    stats(e0[0:p, mg % 4, 0:n, 0:D], SE0, p, n)
                for g, place in ((s - X, SX2), (s - Z, SE0)):
                    if exists(g):
                        p, n = shape(g)
                        last = mean_var(place, m, p, n, g)
                if measured(s):
                    last.then_inc(mv_ready, 1)
                    need(dve, mv_ready, s + 1)
                    need(dve, row_ready, s - 8)
                    dve.tensor_scalar(nmean[:, par, :, :], mv[:, par, :, :, 0], -1.0, None, ALU.mult).then_inc(nmean_ready, 1)

            dve.wait_ge(cleared, 1)
            dve.wait_ge(aux_loaded, 64)
            run_steps(dve, step, STEPS - 1, LO, HI, UN)
            need(dve, hth_mm, NG + 1)
            dve.tensor_copy(c["hth"][:, :, :], ps_hth[:, :, :])

        @block.scalar
        def _(act):
            def step(s, m):
                before = (m - 1) % 4
                g, mg = s - T, m - T
                if exists(g):
                    p, n = shape(g)
                    need(act, w_ready, g + 1)
                    need(act, hth_mm, g - 1)
                    for j in range(n):
                        o = nc.scalar.mul(rw[0:p, mg % 2, j, :], r[0:p, mg % 4, j, :], w[0:p, mg % 2, j:j + 1])
                    o.then_inc(rw_ready, 1)
                if measured(s - 1):
                    need(act, mv_ready, s)
                    nc.scalar.activation(std[:, before, 0:2, :], mv[:, before, 0:2, :, 1], ACT.Sqrt, bias=c["eps"][:, 0:1])
                    nc.scalar.activation(std[:, before, 2:4, :], mv[:, before, 2:4, :, 1], ACT.Sqrt,
                                         bias=c["eps"][:, 1:2]).then_inc(std_ready, 1)
                g, mg = s - H, m - H
                if exists(g):
                    p, n = shape(g)
                    need(act, ss_ready, g + 1)
                    need(act, nrm_ready, g - 1)
                    nc.scalar.activation(root[0:p, mg % 2, 0:n], ss[0:p, mg % 2, 0:n], ACT.Sqrt).then_inc(root_ready, 1)
                g, mg = s - B, m - B
                if exists(g):
                    p, n = shape(g)
                    need(act, nmean_ready, g + 1)
                    need(act, h0_turned, g - 1)
                    for j in range(n):
                        o = nc.scalar.activation(h0[0:p, mg % 2, j, :], xt[0:p, mg % UN, j, :], ACT.Relu,
                                                 bias=nmean[0:p, before, SX, j:j + 1])
                    o.then_inc(h0_ready, 1)
                g, mg = s - R, m - R
                if exists(g):
                    p, n = shape(g)
                    need(act, nmean_ready, s)
                    need(act, hth_mm, g - 3)
                    for j in range(n):
                        o = nc.scalar.activation(r[0:p, mg % 4, j, :], x2[0:p, mg % 4, j, 0:W], ACT.Relu,
                                                 bias=nmean[0:p, before, SX2, j:j + 1])
                    o.then_inc(r_ready, 1)
                g, mg = s - M, m - M
                if exists(g):
                    p, n = shape(g)
                    need(act, e1_turned, g + 1)
                    need(act, x2_mm, g - 1)
                    nc.scalar.copy(e1T[:, mg % 2, 0:n, 0:p], ps_e[:, 0:n, 0:p]).then_inc(e1T_ready, 1)
                g, mg = s - B, m - B
                if exists(g):
                    p, n = shape(g)
                    need(act, h0_turned, g + 1)
                    need(act, z_mm, g - 1)
                    nc.scalar.copy(hT[:, mg % 2, 0:n, :, 0:p], ps_h[:, 0:n, :, 0:p]).then_inc(hT_ready, 1)
                g, mg = s - R, m - R
                if exists(g):
                    p, n = shape(g)
                    need(act, r_ready, g + 1)
                    need(act, ss_ready, g)
                    for j in range(n):
                        o = nc.scalar.activation(rsq[0:p, j, :], r[0:p, mg % 4, j, :], ACT.Square,
                                                 accum_out=ss[0:p, mg % 2, j:j + 1])
                    o.then_inc(ss_ready, 1)

            run_steps(act, step, STEPS, LO, HI, UN)

        @block.tensor
        def _(pe):
            def step(s, m):
                g, mg = s - T - 1, m - T - 1
                if exists(g):
                    p, n = shape(g)
                    need(pe, rw_ready, g + 1)
                    for j in range(n):
                        for h in range(2):
                            o = pe.matmul(ps_hth[:, h, :], rw[0:p, mg % 2, j, h * P:(h + 1) * P], r[0:p, mg % 4, j, :],
                                          start=isinstance(g, int) and g == 0 and j == 0 and h == 0,
                                          stop=isinstance(g, int) and g == NG, skip_group_check=True)
                    o.then_inc(hth_mm, 1)
                g, mg = s - M, m - M
                if exists(g):
                    p, n = shape(g)
                    need(pe, e1_ready, g + 1)
                    need(pe, e1T_ready, g)
                    for j in range(n):
                        o = pe.transpose(ps_e[:, j, 0:p], e1[0:p, mg % 4, j, 0:D], c["ident"][0:p, 0:p])
                    o.then_inc(e1_turned, 1)
                g, mg = s - Z, m - Z
                if exists(g):
                    p, n = shape(g)
                    need(pe, hT_ready, g + 1)
                    need(pe, e0_ready, g)
                    for j in range(n):
                        for h in range(2):
                            o = pe.matmul(ps_z[0:p, j, :], hT[:, mg % 2, j, h, 0:p], c["wP"][:, h, :],
                                          start=h == 0, stop=h == 1)
                    o.then_inc(z_mm, 1)
                g, mg = s - B, m - B
                if exists(g):
                    p, n = shape(g)
                    need(pe, h0_ready, g + 1)
                    need(pe, hT_ready, g)
                    for j in range(n):
                        for h in range(2):
                            o = pe.transpose(ps_h[:, j, h, 0:p], h0[0:p, mg % 2, j, h * P:(h + 1) * P], c["ident"][0:p, 0:p])
                    o.then_inc(h0_turned, 1)
                g, mg = s - M, m - M
                if exists(g):
                    p, n = shape(g)
                    need(pe, e1T_ready, g + 1)
                    need(pe, x2_ready, g)
                    for j in range(n):
                        o = pe.matmul(ps_x[0:p, j, :], e1T[:, mg % 2, j, 0:p], c["w2c"][:, :], start=True, stop=True)
                    o.then_inc(x2_mm, 1)

            run_steps(pe, step, STEPS + 1, LO, HI, UN)


def unpack_lists(nc, c, t):
    with ExitStack() as ctx:
        def sb(name, shape, dt=F32):
            return ctx.enter_context(nc.sbuf_tensor(name, shape, dt))

        sem = phase_sems(nc, ctx)

        pairT = sb("pairT", [HT, 2, 2, P, 2], I32)
        nextT = sb("nextT", [HT, 2, 2, P, 2], I32)
        listT = sb("listT", [HT, 3, 2, 2, P])
        ends = sb("ends", [P, 2, NT])
        skip = sb("skip", [P, 2, NT])
        turn = [ctx.enter_context(nc.psum_tensor(f"turn{i}", [P, 512], F32)) for i in range(3)]
        loaded = sem("lists_loaded")
        floats = sem("list_floats")
        stored = sem("list_rows_stored")
        turned = sem("list_turned")
        ready = sem("list_ready")
        ends_ready = sem("ends_ready")
        fin_ready = sem("fin_ready")
        skip_ready = sem("skip_ready")
        block = ctx.enter_context(nc.Block())

        @block.sync
        def _(sp):
            for l in range(2):
                for off, tile in ((0, pairT), (1, nextT)):
                    at = l * LIST + off
                    sp.dma_start(tile[:, l, :, :, :], t["SORTED"][at:at + EP, :].rearrange(
                        "(a r c) k -> r a (c k)", a=2, c=P).rearrange("r a (c k) -> r a c k", k=2)).then_inc(loaded, 16)
            sp.wait_ge(floats, 2)
            for l in range(2):
                sp.dma_start(t["KEYROW"][l].rearrange("(a r c) -> r a c", a=2, c=P), listT[:, 0, l, :, :]).then_inc(stored, 16)
            sp.wait_ge(stored, 32)

        @block.vector
        def _(dve):
            dve.wait_ge(loaded, 64)
            for kind, tile, who in ((0, pairT, (0, 1)), (1, pairT, (1, 0)), (2, nextT, (0, 1))):
                for l in range(2):
                    dve.tensor_copy(listT[:, kind, l, :, :], tile[:, l, :, :, who[l]]).then_inc(floats, 1)
            dve.wait_ge(ready, 3)
            ek = c["ek"]
            dve.tensor_tensor(ends[:, :, :], ek[:, 0, :, :], ek[:, 2, :, :], ALU.not_equal).then_inc(ends_ready, 1)
            dve.tensor_scalar(c["keyI"][:, :, :], ek[:, 0, :, :], float(N - 1), None, ALU.min)
            dve.tensor_scalar(c["otherI"][:, :, :], ek[:, 1, :, :], float(N - 1), None, ALU.min)
            dve.wait_ge(ends_ready, 1)
            dve.scalar_tensor_tensor(out=c["fin"][:, :, :], in0=ek[:, 0, :, :], scalar=float(N), in1=ends[:, :, :],
                                     op0=ALU.is_lt, op1=ALU.mult).then_inc(fin_ready, 1)
            dve.wait_ge(fin_ready, 1)
            dve.tensor_scalar(skip[:, :, :], c["fin"][:, :, :], -SKIP, SKIP, ALU.mult, ALU.add).then_inc(skip_ready, 1)
            dve.wait_ge(skip_ready, 1)
            dve.tensor_tensor(c["finI"][:, :, :], skip[:, :, :], ek[:, 0, :, :], ALU.add)

        @block.scalar
        def _(act):
            for kind in range(3):
                act.wait_ge(turned, kind + 1)
                nc.scalar.copy(c["ek"][:, kind, :, :].rearrange("p l t -> p (l t)"), turn[kind][:, 0:2 * NT]).then_inc(ready, 1)

        @block.tensor
        def _(pe):
            for kind in range(3):
                pe.wait_ge(floats, 2 * kind + 2)
                for l in range(2):
                    for a in range(2):
                        at = (l * 2 + a) * HT
                        o = pe.transpose(turn[kind][:, at:at + HT], listT[:, kind, l, a, :], c["ident"][0:HT, 0:HT])
                o.then_inc(turned, 1)


def edge_attention(nc, c, t, layer):
    last = layer == 2
    UN, LO, HI = 8, 13, 45
    B, A, C, D_, E, F, H, K, T = 1, 2, 3, 4, 5, 6, 7, 8, 9
    SC = 9 if last else 7
    XG = 4
    END = EG + (K if last else F)
    STEPS = EG + SC
    VW = D + HEADS
    table = t["E1"] if last else t["E0"]
    wt = c["qkv2"] if last else c["qkv1"]
    L = f"_{layer}"
    with ExitStack() as ctx:
        def sb(name, shape, dt=F32):
            return ctx.enter_context(nc.sbuf_tensor(name + L, shape, dt))

        def ps(name, shape):
            return ctx.enter_context(nc.psum_tensor(name + L, shape, F32))

        sem = phase_sems(nc, ctx, L)

        idx = sb("gather_idx", [P, 8, 2, ET], I32)
        fidx = sb("final_idx", [P, 4, ET], I32)
        rrow = sb("src_rows", [P, 8, ET, EW])
        crow = sb("dst_rows", [P, 2, ET, EW])
        keys = sb("keys", [P, 2, ET * P])
        kc = sb("key_cols", [P, 2, ET + 1])
        dv = sb("dinv", [P, 8, ET])
        S = sb("same_src", [P, 2, ET, P])
        cm = sb("carry_to", [P, 2, ET, P])
        rT = sb("rT", [P, ET, P])
        cT = sb("cT", [P, ET, P])
        qs = sb("qs", [P, ET, D])
        qk = sb("qk", [P, ET, D])
        att = sb("att", [P, 2, ET * HEADS])
        vals = sb("vals", [P, 2, ET, VW])
        carry = sb("carry", [P, ET, VW])
        den = sb("den", [P, 2, ET, HEADS])
        avg = sb("avg", [P, ET, D])
        emb = sb("emb", [P, 2, ET, D])
        nrmd = sb("normalised", [P, 2, ET, D])
        st = sb("st", [P, 2, ET, 6])
        mv = sb("mv", [P, 2, 2, ET, 2])
        std = sb("std", [P, 2, 2, ET])
        rstd = sb("rstd", [P, 2, 2, ET])
        nb = sb("nb", [P, 2, 2, ET])
        ps_r = ps("ps_r", [P, ET, P])
        ps_c = ps("ps_c", [P, ET, P])
        ps_q = ps("ps_q", [P, ET, D])
        ps_kv = ps("ps_kv", [P, ET, 2, D])
        ps_a = ps("ps_a", [P, ET, 2 * D])
        if last:
            xr = sb("x_rows", [P, 4, ET, W])
            x2 = sb("x2_new", [P, 4, ET, XW])
            n2T = sb("n2T", [P, ET, P])
            r = sb("r", [P, 2, ET, W])
            rsq = sb("rsq", [P, ET, W])
            rw = sb("rw", [P, 2, ET, W])
            ss = sb("ss", [P, 2, ET])
            nrm = sb("nrm", [P, 2, ET])
            inv = sb("inv", [P, 2, ET])
            w1 = sb("w1", [P, 2, ET])
            ps_hth = ps("ps_hth", [P, 2, W])
        else:
            e1s = sb("e1_scaled", [P, 2, ET, D])
            e1 = sb("e1_new", [P, 4, ET, EW])

        r_loaded = [sem(f"r_loaded{i}") for i in range(8)]
        c_loaded = [sem(f"c_loaded{i}") for i in range(2)]
        x_loaded = [sem(f"xr_loaded{i}") for i in range(4)] if last else None
        keys_loaded = [sem(f"keys_loaded{i}") for i in range(2)]
        new_stored = [sem(f"new_stored{i}") for i in range(4)]
        names = ("sp_passed", "pool_passed", "dve_passed", "cleared", "idx_ready", "fidx_ready", "kc_ready",
                 "S_ready", "dv_ready", "r_turned", "c_turned", "rT_ready", "cT_ready", "q_mm", "kv_mm", "q_ready",
                 "qk_ready", "att_ready", "clip_ready", "exp_ready", "vals_ready", "agg_mm", "carry_ready",
                 "den_ready", "rec_ready", "avg_ready", "emb_ready", "stat", "mv_ready", "std_ready", "rstd_ready",
                 "nb_ready", "n_ready", "scaled", "new_ready")
        if last:
            names += ("n2_turned", "n2T_ready", "x2_mm", "x2_ready", "x2_stat", "r_ready", "ss_ready", "nrm_ready",
                      "nmax_ready", "inv_ready", "k_ready", "rw_ready", "hth_mm")
        sems = {name: sem(name) for name in names}
        (sp_passed, pool_passed, dve_passed, cleared, idx_ready, fidx_ready, kc_ready, S_ready, dv_ready, r_turned,
         c_turned, rT_ready, cT_ready, q_mm, kv_mm, q_ready, qk_ready, att_ready, clip_ready, exp_ready, vals_ready,
         agg_mm, carry_ready, den_ready, rec_ready, avg_ready, emb_ready, stat, mv_ready, std_ready, rstd_ready,
         nb_ready, n_ready, scaled, new_ready) = (sems[name] for name in names[:35])
        if last:
            (n2_turned, n2T_ready, x2_mm, x2_ready, x2_stat, r_ready, ss_ready, nrm_ready, nmax_ready, inv_ready,
             k_ready, rw_ready, hth_mm) = (sems[name] for name in names[35:])
        block = ctx.enter_context(nc.Block())

        def exists(g):
            return not isinstance(g, int) or 0 <= g < EG

        @block.sync
        def _(sp):
            def step(s, m):
                if exists(s):
                    pace(sp, sp_passed, S_ready, s - 1)
                    sp.dma_start(keys[:, m % 2, :], t["KEYROW"][0, bass.ds(s * (ET * P), ET * P)].partition_broadcast(P)
                                 ).then_inc(keys_loaded[m % 2], 16)

            run_steps(sp, step, EG, LO, HI, UN)

        @block.gpsimd
        def _(pool):
            bound = pool.to_reg(N - 1)

            def gather(tile, slot, source, kind, islot, loaded):
                for j in range(ET):
                    pool.indirect_dma_start(tile[:, slot, j, :], None, source[:, :],
                                            bass.IndirectOffsetOnAxis(idx[:, islot, kind, j:j + 1], 0)
                                            ).then_inc(loaded[slot], 16)

            def step(s, m):
                if exists(s):
                    if not isinstance(s, int) or s >= 8:
                        if last:
                            pool.wait_ge(x_loaded[m % 4], dma_count(s - 8, m % 4, 4, 16 * ET))
                            pool.sem_inc(pool_passed, 1)
                        pool.wait_ge(r_loaded[m % 8], dma_count(s - 8, m % 8, 8, 16 * ET))
                        pool.sem_inc(pool_passed, 1)
                    if not isinstance(s, int) or s >= 2:
                        pool.wait_ge(c_loaded[m % 2], dma_count(s - 2, m % 2, 2, 16 * ET))
                        pool.sem_inc(pool_passed, 1)
                    pool.tensor_copy(idx[:, m % 8, 0, :], c["keyI"][:, 0, bass.ds(s * ET, ET)])
                    pool.tensor_copy(idx[:, m % 8, 1, :], c["otherI"][:, 0, bass.ds(s * ET, ET)]).then_inc(idx_ready, 1)
                    pace(pool, pool_passed, idx_ready, s + 1)
                    pace(pool, pool_passed, emb_ready, s - 7)
                    gather(rrow, m % 8, table, 0, m % 8, r_loaded)
                    pace(pool, pool_passed, c_turned, s - 1)
                    gather(crow, m % 2, table, 1, m % 8, c_loaded)
                g, mg = s - XG, m - XG
                if last and exists(g):
                    pace(pool, pool_passed, x2_ready, g - 3)
                    if not isinstance(g, int) or g >= 4:
                        pool.wait_ge(x_loaded[mg % 4], dma_count(g - 4, mg % 4, 4, 16 * ET))
                        pool.sem_inc(pool_passed, 1)
                    gather(xr, mg % 4, t["x"], 0, mg % 8, x_loaded)
                g, mg = s - SC, m - SC
                if exists(g):
                    if not isinstance(g, int) or g >= 4:
                        pool.wait_ge(new_stored[mg % 4], dma_count(g - 4, mg % 4, 4, 16 * ET))
                        pool.sem_inc(pool_passed, 1)
                    pool.tensor_copy(fidx[:, mg % 4, :], c["finI"][:, 0, bass.ds(g * ET, ET)]).then_inc(fidx_ready, 1)
                    pace(pool, pool_passed, fidx_ready, g + 1)
                    pace(pool, pool_passed, new_ready, g + 1)
                    for j in range(ET):
                        new = x2[:, mg % 4, j, :] if last else e1[:, mg % 4, j, :]
                        pool.indirect_dma_start(t["X2" if last else "E1"][:, :],
                                                bass.IndirectOffsetOnAxis(fidx[:, mg % 4, j:j + 1], 0), new, None,
                                                bounds_check=bound, oob_is_err=False).then_inc(new_stored[mg % 4], 16)

            run_steps(pool, step, STEPS, LO, HI, UN)
            for k in range(4):
                pool.wait_ge(new_stored[k], 16 * ET * len(range(k, EG, 4)))

        @block.vector
        def _(dve):
            def stats(tile, place, m, done, g):
                for j in range(ET):
                    o = dve.bn_stats(st[:, place, j, :], tile[:, j, :])
                o.then_inc(done, 1)
                need(dve, done, g + 1)
                dve.sem_inc(dve_passed, 1)
                for j in range(ET):
                    o = dve.bn_aggr(mv[:, m % 2, place, j, :], st[:, place, j, :])
                return o

            def step(s, m):
                par, before = m % 2, (m - 1) % 2
                if not isinstance(s, int) or E <= s < EG + (H if last else E):
                    n = s - E
                    need(dve, std_ready, n + 1)
                    need(dve, n_ready, s - F)
                    if last:
                        need(dve, r_ready, s - K)
                    dve.reciprocal(rstd[:, before, :, :], std[:, before, :, :]).then_inc(rstd_ready, 1)
                    need(dve, rstd_ready, n + 1)
                    dve.scalar_tensor_tensor(out=nb[:, before, :, :], in0=mv[:, before, :, :, 0], scalar=-1.0,
                                             in1=rstd[:, before, :, :], op0=ALU.mult, op1=ALU.mult).then_inc(nb_ready, 1)
                gd, md = s - D_, m - D_
                d2 = md % 2
                if exists(gd):
                    need(dve, carry_ready, (gd + 1) * ET)
                    dve.tensor_scalar(den[:, 0, :, :], ps_a[:, :, D:VW], EPS_ATT, None, ALU.add).then_inc(den_ready, 1)
                    need(dve, den_ready, gd + 1)
                    dve.reciprocal(den[:, 1, :, :], den[:, 0, :, :]).then_inc(rec_ready, 1)
                    need(dve, rec_ready, gd + 1)
                    dve.tensor_tensor(
                        avg[:, :, :].rearrange("p j (h d) -> p j h d", h=HEADS),
                        ps_a[:, :, 0:D].rearrange("p j (h d) -> p j h d", h=HEADS),
                        den[:, 1, :, :].unsqueeze(3).to_broadcast([P, ET, HEADS, HD]), ALU.mult).then_inc(avg_ready, 1)
                ga, ma = s - A, m - A
                a2 = ma % 2
                if exists(ga):
                    need(dve, q_ready, ga + 1)
                    need(dve, kv_mm, ga + 1)
                    dve.tensor_tensor(qk[:, :, :], qs[:, :, :], ps_kv[:, :, 0, :], ALU.mult).then_inc(qk_ready, 1)
                g, mg = s - B, m - B
                if exists(g):
                    need(dve, c_turned, g + 1)
                    need(dve, kv_mm, g)
                    dve.tensor_copy(cT[:, :, :], ps_c[:, :, :]).then_inc(cT_ready, 1)
                    dve.wait_ge(r_loaded[mg % 8], dma_count(g, mg % 8, 8, 16 * ET))
                    dve.tensor_copy(dv[:, mg % 8, :], rrow[:, mg % 8, :, D]).then_inc(dv_ready, 1)
                if exists(ga):
                    need(dve, qk_ready, ga + 1)
                    need(dve, exp_ready, ga - 1)
                    dve.tensor_reduce(att[:, a2, :], qk[:, :, :].rearrange("p j (h d) -> p (j h) d", h=HEADS),
                                      AX_X, ALU.add).then_inc(att_ready, 1)
                    need(dve, att_ready, ga + 1)
                    dve.tensor_scalar(att[:, a2, :], att[:, a2, :], -10.0, 10.0, ALU.max, ALU.min).then_inc(clip_ready, 1)
                    lo = 1 if isinstance(ga, int) and ga == 0 else 0
                    if lo:
                        dve.memset(kc[:, a2, 0:1], -1.0)
                    dve.tensor_copy(kc[:, a2, lo:], c["ek"][:, 0, 0, bass.ds(ga * ET - 1 + lo, ET + 1 - lo)]).then_inc(kc_ready, 1)
                    need(dve, kc_ready, ga + 1)
                    dve.wait_ge(keys_loaded[a2], dma_count(ga, a2, 2))
                    need(dve, agg_mm, (ga - 1) * ET)
                    for j in range(ET):
                        kj = keys[:, a2, j * P:(j + 1) * P]
                        dve.tensor_scalar(S[:, a2, j, :], kj, kc[:, a2, j + 1:j + 2], None, ALU.is_equal)
                        o = dve.tensor_scalar(cm[QUAD:, a2, j, :], kj[QUAD:, :], kc[QUAD:, a2, j:j + 1],
                                              c["e127"][QUAD:, :], ALU.is_equal, ALU.mult)
                    o.then_inc(S_ready, 1)
                    need(dve, exp_ready, ga + 1)
                    dve.tensor_tensor(
                        vals[:, a2, :, 0:D].rearrange("p j (h d) -> p j h d", h=HEADS),
                        ps_kv[:, :, 1, :].rearrange("p j (h d) -> p j h d", h=HEADS),
                        vals[:, a2, :, D:VW].unsqueeze(3).to_broadcast([P, ET, HEADS, HD]), ALU.mult).then_inc(vals_ready, 1)
                if last:
                    g, mg = s - F, m - F
                    if exists(g):
                        need(dve, n2_turned, g + 1)
                        need(dve, x2_mm, g)
                        dve.tensor_copy(n2T[:, :, :], ps_r[:, :, :]).then_inc(n2T_ready, 1)
                if exists(gd):
                    need(dve, avg_ready, gd + 1)
                    need(dve, n_ready, gd - 1)
                    dve.tensor_tensor(emb[:, d2, :, :], avg[:, :, :], rrow[:, md % 8, :, 0:D], ALU.add).then_inc(emb_ready, 1)
                    need(dve, emb_ready, gd + 1)
                    tail = stats(emb[:, d2, :, :], 0, m, stat, gd)
                if not last:
                    g, mg = s - F, m - F
                    if exists(g):
                        if not isinstance(s, int) or s < EG + D_:
                            tail.then_inc(mv_ready, 1)
                        p2 = mg % 2
                        need(dve, n_ready, g + 1)
                        if not isinstance(g, int) or g >= 4:
                            dve.wait_ge(new_stored[mg % 4], dma_count(g - 4, mg % 4, 4, 16 * ET))
                        dve.tensor_tensor(e1s[:, p2, :, :], nrmd[:, p2, :, :], spread(c["ln1s"], P, ET, D), ALU.mult)
                        dve.tensor_copy(e1[:, mg % 4, :, D], dv[:, mg % 8, :]).then_inc(scaled, 1)
                        need(dve, scaled, g + 1)
                        dve.tensor_tensor(e1[:, mg % 4, :, 0:D], e1s[:, p2, :, :], spread(c["ln1b"], P, ET, D),
                                          ALU.add).then_inc(new_ready, 1)
                    elif exists(gd):
                        tail.then_inc(mv_ready, 1)
                else:
                    g, mg = s - K, m - K
                    if exists(g):
                        p2, sl = mg % 2, m % 2
                        row = x2[:, mg % 4, :, :]
                        need(dve, nrm_ready, g + 1)
                        dve.tensor_scalar(nrm[:, p2, :], nrm[:, p2, :], EPS_L2, None, ALU.max).then_inc(nmax_ready, 1)
                        need(dve, nmax_ready, g + 1)
                        dve.reciprocal(inv[:, p2, :], nrm[:, p2, :]).then_inc(inv_ready, 1)
                        need(dve, inv_ready, g + 1)
                        dve.tensor_tensor(w1[:, p2, :], inv[:, p2, :], c["fin"][:, 0, bass.ds(g * ET, ET)], ALU.mult)
                        dve.tensor_tensor(row[:, :, W], rstd[:, sl, 1, :], inv[:, p2, :], ALU.mult)
                        dve.tensor_copy(row[:, :, W + 4], dv[:, mg % 8, :])
                        dve.tensor_tensor(row[:, :, W + 1], nb[:, sl, 1, :], inv[:, p2, :], ALU.mult).then_inc(k_ready, 1)
                        need(dve, k_ready, g + 1)
                        dve.tensor_tensor(row[:, :, W + 2], row[:, :, W], row[:, :, W + 4], ALU.mult)
                        dve.tensor_tensor(row[:, :, W + 3], row[:, :, W + 1], row[:, :, W + 4], ALU.mult).then_inc(new_ready, 1)
                        need(dve, hth_mm, g - 1)
                        for j in range(ET):
                            o = dve.tensor_scalar(rw[:, p2, j, :], r[:, p2, j, :], inv[:, p2, j:j + 1],
                                                  w1[:, p2, j:j + 1], ALU.mult, ALU.mult)
                        o.then_inc(rw_ready, 1)
                    g, mg = s - F, m - F
                    if exists(g):
                        need(dve, x2_mm, g + 1)
                        dve.wait_ge(x_loaded[mg % 4], dma_count(g, mg % 4, 4, 16 * ET))
                        need(dve, r_ready, g - 3)
                        if not isinstance(g, int) or g >= 4:
                            dve.wait_ge(new_stored[mg % 4], dma_count(g - 4, mg % 4, 4, 16 * ET))
                        dve.tensor_tensor(x2[:, mg % 4, :, 0:W], ps_kv[:, :, :, :].rearrange("p j k d -> p j (k d)"),
                                          xr[:, mg % 4, :, :], ALU.add).then_inc(x2_ready, 1)
                        need(dve, x2_ready, g + 1)
                        tail = stats(x2[:, mg % 4, :, 0:W], 1, m, x2_stat, g)
                    if exists(gd) or exists(g):
                        tail.then_inc(mv_ready, 1)

            dve.memset(mv[:, :, :, :, :], 1.0).then_inc(cleared, 1)
            if last:
                dve.memset(x2[:, :, :, W:], 0.0).then_inc(cleared, 1)
            else:
                dve.memset(e1[:, :, :, D:], 0.0).then_inc(cleared, 1)
            dve.wait_ge(cleared, 2)
            run_steps(dve, step, END, LO, HI, UN)
            if last:
                need(dve, hth_mm, EG)
                dve.tensor_tensor(c["hth"][:, :, :], c["hth"][:, :, :], ps_hth[:, :, :], ALU.add)

        @block.scalar
        def _(act):
            def step(s, m):
                par, before = m % 2, (m - 1) % 2

                def hand_on(j):
                    g = s - C
                    if exists(g):
                        need(act, agg_mm, g * ET + j + 1)
                        nc.scalar.copy(carry[QUAD:, j, :], ps_a[QUAD:, j, 0:VW]).then_inc(carry_ready, 1)

                g, mg = s - A, m - A
                if exists(g):
                    need(act, q_mm, g + 1)
                    need(act, qk_ready, g)
                    nc.scalar.copy(qs[:, :, :], ps_q[:, :, :]).then_inc(q_ready, 1)
                g, mg = s - B, m - B
                if exists(g):
                    need(act, r_turned, g + 1)
                    need(act, q_mm, g)
                    nc.scalar.copy(rT[:, :, :], ps_r[:, :, :]).then_inc(rT_ready, 1)
                hand_on(0)
                hand_on(1)
                g, mg = s - A, m - A
                if exists(g):
                    p2 = mg % 2
                    need(act, clip_ready, g + 1)
                    need(act, agg_mm, (g - 1) * ET)
                    nc.scalar.activation(vals[:, p2, :, D:VW], att[:, p2, :].rearrange("p (j h) -> p j h", h=HEADS),
                                         ACT.Exp).then_inc(exp_ready, 1)
                hand_on(2)
                hand_on(3)
                g, mg = s - E, m - E
                if exists(g):
                    p2 = mg % 2
                    need(act, nb_ready, g + 1)
                    need(act, n2_turned if last else new_ready, g - 1)
                    for j in range(ET):
                        o = nc.scalar.activation(nrmd[:, p2, j, :], emb[:, p2, j, :], ACT.Identity,
                                                 bias=nb[:, before, 0, j:j + 1], scale=rstd[:, before, 0, j:j + 1])
                    o.then_inc(n_ready, 1)
                if last:
                    g, mg = s - H, m - H
                    if exists(g):
                        p2 = mg % 2
                        need(act, nb_ready, s - E + 1)
                        need(act, hth_mm, g - 1)
                        need(act, rw_ready, g - 1)
                        for j in range(ET):
                            o = nc.scalar.activation(r[:, p2, j, :], x2[:, mg % 4, j, 0:W], ACT.Relu,
                                                     bias=nb[:, before, 1, j:j + 1], scale=rstd[:, before, 1, j:j + 1])
                        o.then_inc(r_ready, 1)
                        need(act, r_ready, g + 1)
                        need(act, ss_ready, g)
                        for j in range(ET):
                            o = nc.scalar.activation(rsq[:, j, :], r[:, p2, j, :], ACT.Square, accum_out=ss[:, p2, j:j + 1])
                        o.then_inc(ss_ready, 1)
                        need(act, ss_ready, g + 1)
                        need(act, inv_ready, g - 1)
                        nc.scalar.activation(nrm[:, p2, :], ss[:, p2, :], ACT.Sqrt).then_inc(nrm_ready, 1)
                n = s - D_
                if not isinstance(s, int) or D_ <= s < EG + (F if last else D_):
                    need(act, mv_ready, n + 1)
                    need(act, rstd_ready, n - 1)
                    nc.scalar.activation(std[:, par, 0, :], mv[:, par, 0, :, 1], ACT.Sqrt, bias=c["eps"][:, 1:2])
                    nc.scalar.activation(std[:, par, 1, :], mv[:, par, 1, :, 1], ACT.Sqrt,
                                         bias=c["eps"][:, 0:1]).then_inc(std_ready, 1)

            run_steps(act, step, EG + (H if last else E), LO, HI, UN)

        @block.tensor
        def _(pe):
            def step(s, m):
                g, mg = s - B, m - B
                if exists(g):
                    pe.wait_ge(r_loaded[mg % 8], dma_count(g, mg % 8, 8, 16 * ET))
                    need(pe, rT_ready, g)
                    if last:
                        need(pe, n2T_ready, g - F + B)
                    for j in range(ET):
                        o = pe.transpose(ps_r[:, j, :], rrow[:, mg % 8, j, 0:D], c["ident"][:, :])
                    o.then_inc(r_turned, 1)
                    pe.wait_ge(c_loaded[mg % 2], dma_count(g, mg % 2, 2, 16 * ET))
                    need(pe, cT_ready, g)
                    for j in range(ET):
                        o = pe.transpose(ps_c[:, j, :], crow[:, mg % 2, j, 0:D], c["ident"][:, :])
                    o.then_inc(c_turned, 1)
                for j in range(ET):
                    g, mg = s - C, m - C
                    if exists(g):
                        p2 = mg % 2
                        if j == 0:
                            need(pe, S_ready, g + 1)
                            need(pe, vals_ready, g + 1)
                            need(pe, avg_ready, g)
                        first = isinstance(g, int) and g == 0 and j == 0
                        need(pe, carry_ready, g * ET + j)
                        o = pe.matmul(ps_a[:, j, 0:VW], S[:, p2, j, :], vals[:, p2, j, :], start=True, stop=first)
                        if not first:
                            o = pe.matmul(ps_a[:, j, 0:VW], cm[QUAD:, p2, j, :], carry[QUAD:, (j - 1) % ET, :],
                                          start=False, stop=True)
                        o.then_inc(agg_mm, 1)
                    g, mg = s - T, m - T
                    if last and exists(g):
                        need(pe, rw_ready, g + 1)
                        for h in range(2):
                            o = pe.matmul(ps_hth[:, h, :], rw[:, mg % 2, j, h * P:(h + 1) * P], r[:, mg % 2, j, :],
                                          start=isinstance(g, int) and g == 0 and j == 0 and h == 0,
                                          stop=isinstance(g, int) and g == EG - 1 and j == ET - 1,
                                          skip_group_check=True)
                        if j == ET - 1:
                            o.then_inc(hth_mm, 1)
                g, mg = s - F, m - F
                if last and exists(g):
                    need(pe, n_ready, g + 1)
                    need(pe, rT_ready, s if not isinstance(s, int) else min(s, EG))
                    for j in range(ET):
                        o = pe.transpose(ps_r[:, j, :], nrmd[:, mg % 2, j, :], c["ident"][:, :])
                    o.then_inc(n2_turned, 1)
                    need(pe, n2T_ready, g + 1)
                    need(pe, vals_ready, s - A + 1 if not isinstance(s, int) else min(s - A + 1, EG))
                    need(pe, x2_ready, g)
                    for j in range(ET):
                        x2_out = ps_kv[:, j, :, :].rearrange("p k d -> p (k d)")
                        pe.matmul(x2_out, c["ones"][0:1, :], c["bias2"][0:1, :], start=True, stop=False)
                        o = pe.matmul(x2_out, n2T[:, j, :], c["w2"][:, :], start=False, stop=True)
                    o.then_inc(x2_mm, 1)
                g, mg = s - B, m - B
                if exists(g):
                    need(pe, rT_ready, g + 1)
                    need(pe, q_ready, g)
                    for j in range(ET):
                        o = pe.matmul(ps_q[:, j, :], rT[:, j, :], wt[:, 0, :], start=True, stop=True)
                    o.then_inc(q_mm, 1)
                    need(pe, cT_ready, g + 1)
                    need(pe, vals_ready, g)
                    if last:
                        need(pe, x2_ready, g - F + B + 1)
                    for j in range(ET):
                        o = pe.matmul(ps_kv[:, j, :, :], cT[:, j, :], wt[:, 1:3, :], start=True, stop=True)
                    o.then_inc(kv_mm, 1)

            run_steps(pe, step, EG + (T if last else C), LO, HI, UN)


def dense_gcn(nc, c, t):
    UN, LO, HI = 8, 8, 128
    B, V, M, Z, Q, O = 0, 1, 2, 3, 4, 5
    AHEAD = 2
    with ExitStack() as ctx:
        def sb(name, shape, dt=F32):
            return ctx.enter_context(nc.sbuf_tensor("n_" + name, shape, dt))

        def ps(name, shape):
            return ctx.enter_context(nc.psum_tensor("n_" + name, shape, F32))

        sem = phase_sems(nc, ctx)
        wsum = sb("wsum", [P, 2, W])
        x2 = sb("x2_in", [P, 8, G, XW])
        h = sb("h", [P, 2, G, W])
        hT = sb("hT", [P, 2, G, 2, P])
        zb = sb("zb", [P, 2, G, W])
        z = sb("z", [P, 4, G, W])
        zsq = sb("zsq", [P, G, W])
        ss = sb("ss", [P, 2, G])
        nrm = sb("nrm", [P, 2, G])
        inv = sb("inv", [P, 2, G])
        o_sb = sb("o_sb", [P, 4, G, W])
        ps_h = ps("ps_h", [P, 2, 4, 2, P])
        ps_z = ps("ps_z", [P, 2, 4, W])

        x_loaded = [sem(f"x2_loaded{i}") for i in range(8)]
        o_stored = [sem(f"out_stored{i}") for i in range(4)]
        (sp_passed, m_mm, wv_ready, wsum_ready, h_ready, h_turned, hT_ready, z_mm, zb_ready,
         z_ready, ss_ready, nrm_ready, nmax_ready, inv_ready, o_ready) = (sem("gcn_" + s) for s in (
            "sp_passed", "m_mm", "wv_ready", "wsum_ready", "h_ready", "h_turned",
            "hT_ready", "z_mm", "zb_ready", "z_ready", "ss_ready", "nrm_ready", "nmax_ready", "inv_ready", "o_ready"))
        block = ctx.enter_context(nc.Block())

        def exists(g):
            return not isinstance(g, int) or 0 <= g <= NG

        def shape(g):
            return (TAIL, 1) if isinstance(g, int) and g == NG else (P, G)

        def nodes(ap, g):
            p, n = shape(g)
            return ap[bass.ds(g * (P * G), p * n), :].rearrange("(p k) c -> p k c", k=n)

        @block.sync
        def _(sp):
            def load(g, m):
                if exists(g):
                    p, n = shape(g)
                    pace(sp, sp_passed, o_ready, g - 7)
                    sp.dma_start(x2[0:p, m % 8, 0:n, :], nodes(t["X2"], g)).then_inc(x_loaded[m % 8], 16)

            def step(s, m):
                load(s + AHEAD, m + AHEAD)
                g, mg = s - O, m - O
                if exists(g):
                    p, n = shape(g)
                    pace(sp, sp_passed, o_ready, g + 1)
                    sp.dma_start(nodes(t["out"], g), o_sb[0:p, mg % 4, 0:n, :]).then_inc(o_stored[mg % 4], 16)

            for g in range(AHEAD):
                load(g, g)
            run_steps(sp, step, NG + 1 + O, LO, HI, UN)
            for k in range(4):
                sp.wait_ge(o_stored[k], 16 * len(range(k, NG + 1, 4)))

        @block.vector
        def _(dve):
            dve.wait_ge(m_mm, 1)
            dve.tensor_scalar(c["wv"][:, :, :], ps_z[:, 0, 0:2, :], BETA / N, None, ALU.mult).then_inc(wv_ready, 1)
            dve.wait_ge(wv_ready, 1)
            dve.tensor_tensor(wsum[:, :, :], c["wv"][:, :, :], c["wg"][:, :, :], ALU.add).then_inc(wsum_ready, 1)

            def step(s, m):
                g, mg = s - V, m - V
                if exists(g):
                    p, n = shape(g)
                    need(dve, h_turned, g + 1)
                    need(dve, z_mm, g - 1)
                    dve.tensor_copy(hT[:, mg % 2, 0:n, :, 0:p], ps_h[:, mg % 2, 0:n, :, 0:p]).then_inc(hT_ready, 1)
                g, mg = s - Z, m - Z
                if exists(g):
                    p, n = shape(g)
                    need(dve, z_mm, g + 1)
                    need(dve, z_ready, g - 1)
                    dve.tensor_tensor(zb[0:p, mg % 2, 0:n, :], ps_z[0:p, mg % 2, 0:n, :], spread(c["bg"], p, n, W),
                                      ALU.add).then_inc(zb_ready, 1)
                g, mg = s - O, m - O
                if exists(g):
                    p, n = shape(g)
                    p2 = mg % 2
                    need(dve, nrm_ready, g + 1)
                    dve.tensor_scalar(nrm[0:p, p2, 0:n], nrm[0:p, p2, 0:n], EPS_L2, None, ALU.max).then_inc(nmax_ready, 1)
                    need(dve, nmax_ready, g + 1)
                    dve.reciprocal(inv[0:p, p2, 0:n], nrm[0:p, p2, 0:n]).then_inc(inv_ready, 1)
                    need(dve, inv_ready, g + 1)
                    if not isinstance(g, int) or g >= 4:
                        dve.wait_ge(o_stored[mg % 4], dma_count(g - 4, mg % 4, 4))
                    for k in range(n):
                        o = dve.scalar_tensor_tensor(out=o_sb[0:p, mg % 4, k, :], in0=z[0:p, mg % 4, k, :],
                                                     scalar=inv[0:p, p2, k:k + 1], in1=x2[0:p, mg % 8, k, 0:W],
                                                     op0=ALU.mult, op1=ALU.add)
                    o.then_inc(o_ready, 1)

            run_steps(dve, step, NG + 1 + O, LO, HI, UN)

        @block.scalar
        def _(act):
            def step(s, m):
                gq, mq = s - Q, m - Q
                q2 = mq % 2
                if exists(gq):
                    p, n = shape(gq)
                    need(act, zb_ready, gq + 1)
                    need(act, o_ready, gq - 3)
                    nc.scalar.activation(z[0:p, mq % 4, 0:n, :], zb[0:p, q2, 0:n, :], ACT.Relu).then_inc(z_ready, 1)
                g, mg = s - B, m - B
                if exists(g):
                    p, n = shape(g)
                    act.wait_ge(x_loaded[mg % 8], dma_count(g, mg % 8, 8))
                    need(act, h_turned, g - 1)
                    for k in range(n):
                        row = x2[0:p, mg % 8, k, :]
                        o = nc.scalar.activation(h[0:p, mg % 2, k, :], row[:, 0:W], ACT.Relu,
                                                 bias=row[:, W + 1:W + 2], scale=row[:, W:W + 1])
                    o.then_inc(h_ready, 1)
                if exists(gq):
                    p, n = shape(gq)
                    need(act, z_ready, gq + 1)
                    need(act, ss_ready, gq)
                    for k in range(n):
                        o = nc.scalar.activation(zsq[0:p, k, :], z[0:p, mq % 4, k, :], ACT.Square,
                                                 accum_out=ss[0:p, q2, k:k + 1])
                    o.then_inc(ss_ready, 1)
                    need(act, ss_ready, gq + 1)
                    need(act, inv_ready, gq - 1)
                    nc.scalar.activation(nrm[0:p, q2, 0:n], ss[0:p, q2, 0:n], ACT.Sqrt).then_inc(nrm_ready, 1)

            run_steps(act, step, NG + 1 + Q, LO, HI, UN)

        @block.tensor
        def _(pe):
            for i in range(2):
                for k in range(2):
                    o = pe.matmul(ps_z[:, 0, i, :], c["hth"][:, k, i * P:(i + 1) * P], c["wv"][:, k, :],
                                  start=i == 0 and k == 0, stop=i == 1 and k == 1, skip_group_check=True)
            o.then_inc(m_mm, 1)
            pe.wait_ge(wsum_ready, 1)

            def step(s, m):
                g, mg = s - M, m - M
                if exists(g):
                    p, n = shape(g)
                    need(pe, hT_ready, g + 1)
                    need(pe, zb_ready, g - 1)
                    for k in range(n):
                        for i in range(2):
                            o = pe.matmul(ps_z[0:p, mg % 2, k, :], hT[:, mg % 2, k, i, 0:p], wsum[:, i, :],
                                          start=i == 0, stop=i == 1)
                    o.then_inc(z_mm, 1)
                g, mg = s - B, m - B
                if exists(g):
                    p, n = shape(g)
                    need(pe, h_ready, g + 1)
                    need(pe, hT_ready, g - 1)
                    for k in range(n):
                        for i in range(2):
                            o = pe.transpose(ps_h[:, mg % 2, k, i, 0:p], h[0:p, mg % 2, k, i * P:(i + 1) * P],
                                             c["ident"][0:p, 0:p])
                    o.then_inc(h_turned, 1)

            run_steps(pe, step, NG + 1 + M, LO, HI, UN)


def edge_gcn(nc, c, t):
    UN, LO, HI = 8, 12, 44
    B, A, C, V, M, Q, O, SC = 1, 2, 3, 4, 5, 6, 7, 8
    STEPS = EG + SC
    with ExitStack() as ctx:
        def sb(name, shape, dt=F32):
            return ctx.enter_context(nc.sbuf_tensor("g_" + name, shape, dt))

        def ps(name, shape):
            return ctx.enter_context(nc.psum_tensor("g_" + name, shape, F32))

        sem = phase_sems(nc, ctx, "_g")
        idx = sb("gather_idx", [P, 4, 2, ET], I32)
        fidx = sb("final_idx", [P, 4, ET], I32)
        srow = sb("src_rows", [P, 2, ET, XW])
        drow = sb("dst_rows", [P, 8, ET, XW])
        keys = sb("keys", [P, 2, ET * P])
        kc = sb("key_cols", [P, 2, ET + 1])
        S = sb("same_dst", [P, 2, ET, P])
        cm = sb("carry_to", [P, 2, ET, P])
        hs = sb("hs", [P, 2, ET, W])
        carry = sb("carry", [P, ET, W])
        hd = sb("hd", [P, 2, ET, W])
        sums = sb("sums", [P, 2, ET, W])
        both = sb("both", [P, 2, 2, ET, 2, P])
        zb = sb("zb", [P, 2, ET, W])
        z = sb("z", [P, 2, ET, W])
        zsq = sb("zsq", [P, ET, W])
        ss = sb("ss", [P, 2, ET])
        nrm = sb("nrm", [P, 2, ET])
        inv = sb("inv", [P, 2, ET])
        o_sb = sb("o_sb", [P, 4, ET, W])
        ps_a = ps("ps_a", [P, ET, W])
        ps_t = ps("ps_t", [P, 2, ET, 2, P])
        ps_z = ps("ps_z", [P, ET, W])

        s_loaded = [sem(f"s_loaded{i}") for i in range(2)]
        d_loaded = [sem(f"d_loaded{i}") for i in range(8)]
        keys_loaded = [sem(f"keys_loaded{i}") for i in range(2)]
        new_stored = [sem(f"new_stored{i}") for i in range(4)]
        (sp_passed, pool_passed, idx_ready, fidx_ready, kc_ready, S_ready, hs_ready, agg_mm, carry_ready, hd_ready,
         sums_ready, own_ready, hd_turned, sums_turned, both_ready, z_mm, zb_ready, z_ready, ss_ready, nrm_ready,
         nmax_ready, inv_ready, o_ready) = (sem(s) for s in (
            "sp_passed", "pool_passed", "idx_ready", "fidx_ready", "kc_ready", "S_ready", "hs_ready", "agg_mm",
            "carry_ready", "hd_ready", "sums_ready", "own_ready", "hd_turned", "sums_turned", "both_ready", "z_mm",
            "zb_ready", "z_ready", "ss_ready", "nrm_ready", "nmax_ready", "inv_ready", "o_ready"))
        block = ctx.enter_context(nc.Block())

        def exists(g):
            return not isinstance(g, int) or 0 <= g < EG

        @block.sync
        def _(sp):
            def step(s, m):
                pace(sp, sp_passed, S_ready, s - 1)
                sp.dma_start(keys[:, m % 2, :], t["KEYROW"][1, bass.ds(s * (ET * P), ET * P)].partition_broadcast(P)
                             ).then_inc(keys_loaded[m % 2], 16)

            run_steps(sp, step, EG, LO, HI, UN)

        @block.gpsimd
        def _(pool):
            bound = pool.to_reg(N - 1)

            def gather(tile, slot, kind, islot, loaded):
                for j in range(ET):
                    pool.indirect_dma_start(tile[:, slot, j, :], None, t["X2"][:, :],
                                            bass.IndirectOffsetOnAxis(idx[:, islot, kind, j:j + 1], 0)
                                            ).then_inc(loaded[slot], 16)

            def step(s, m):
                if exists(s):
                    if not isinstance(s, int) or s >= 4:
                        pool.wait_ge(d_loaded[(m - 4) % 8], dma_count(s - 4, (m - 4) % 8, 8, 16 * ET))
                        pool.sem_inc(pool_passed, 1)
                    if not isinstance(s, int) or s >= 2:
                        pool.wait_ge(s_loaded[m % 2], dma_count(s - 2, m % 2, 2, 16 * ET))
                        pool.sem_inc(pool_passed, 1)
                    pool.tensor_copy(idx[:, m % 4, 0, :], c["keyI"][:, 1, bass.ds(s * ET, ET)])
                    pool.tensor_copy(idx[:, m % 4, 1, :], c["otherI"][:, 1, bass.ds(s * ET, ET)]).then_inc(idx_ready, 1)
                    pace(pool, pool_passed, idx_ready, s + 1)
                    pace(pool, pool_passed, hs_ready, s - 1)
                    gather(srow, m % 2, 1, m % 4, s_loaded)
                    pace(pool, pool_passed, o_ready, s - 7)
                    gather(drow, m % 8, 0, m % 4, d_loaded)
                g, mg = s - SC, m - SC
                if exists(g):
                    if not isinstance(g, int) or g >= 4:
                        pool.wait_ge(new_stored[mg % 4], dma_count(g - 4, mg % 4, 4, 16 * ET))
                        pool.sem_inc(pool_passed, 1)
                    pool.tensor_copy(fidx[:, mg % 4, :], c["finI"][:, 1, bass.ds(g * ET, ET)]).then_inc(fidx_ready, 1)
                    pace(pool, pool_passed, fidx_ready, g + 1)
                    pace(pool, pool_passed, o_ready, g + 1)
                    for j in range(ET):
                        pool.indirect_dma_start(t["out"][:, :], bass.IndirectOffsetOnAxis(fidx[:, mg % 4, j:j + 1], 0),
                                                o_sb[:, mg % 4, j, :], None,
                                                bounds_check=bound, oob_is_err=False).then_inc(new_stored[mg % 4], 16)

            run_steps(pool, step, STEPS, LO, HI, UN)
            for k in range(4):
                pool.wait_ge(new_stored[k], 16 * ET * len(range(k, EG, 4)))

        @block.vector
        def _(dve):
            def step(s, m):
                g, mg = s - C, m - C
                if exists(g):
                    p2 = mg % 2
                    need(dve, carry_ready, (g + 1) * ET)
                    need(dve, hd_ready, g + 1)
                    need(dve, sums_turned, g - 1)
                    for j in range(ET):
                        dinv = drow[:, mg % 8, j, W + 4:W + 5]
                        o = dve.scalar_tensor_tensor(out=sums[:, p2, j, :], in0=hd[:, p2, j, :], scalar=dinv,
                                                     in1=ps_a[:, j, :], op0=ALU.mult, op1=ALU.add)
                    o.then_inc(sums_ready, 1)
                    need(dve, sums_ready, g + 1)
                    for j in range(ET):
                        dinv = drow[:, mg % 8, j, W + 4:W + 5]
                        o = dve.tensor_scalar(sums[:, p2, j, :], sums[:, p2, j, :], dinv, None, ALU.mult)
                    o.then_inc(own_ready, 1)
                g, mg = s - V, m - V
                if exists(g):
                    need(dve, hd_turned, g + 1)
                    need(dve, sums_turned, g + 1)
                    need(dve, z_mm, g - 1)
                    for kind in range(2):
                        o = dve.tensor_copy(both[:, mg % 2, kind, :, :, :], ps_t[:, kind, :, :, :])
                    o.then_inc(both_ready, 1)
                g, mg = s - O, m - O
                if exists(g):
                    p2 = mg % 2
                    need(dve, nrm_ready, g + 1)
                    dve.tensor_scalar(nrm[:, p2, :], nrm[:, p2, :], EPS_L2, None, ALU.max).then_inc(nmax_ready, 1)
                    need(dve, nmax_ready, g + 1)
                    dve.reciprocal(inv[:, p2, :], nrm[:, p2, :]).then_inc(inv_ready, 1)
                    need(dve, inv_ready, g + 1)
                    if not isinstance(g, int) or g >= 4:
                        dve.wait_ge(new_stored[mg % 4], dma_count(g - 4, mg % 4, 4, 16 * ET))
                    for j in range(ET):
                        o = dve.scalar_tensor_tensor(out=o_sb[:, mg % 4, j, :], in0=z[:, p2, j, :],
                                                     scalar=inv[:, p2, j:j + 1], in1=drow[:, mg % 8, j, 0:W],
                                                     op0=ALU.mult, op1=ALU.add)
                    o.then_inc(o_ready, 1)
                g, mg = s - B, m - B
                if exists(g):
                    p2 = mg % 2
                    lo = 1 if isinstance(g, int) and g == 0 else 0
                    if lo:
                        dve.memset(kc[:, p2, 0:1], -1.0)
                    dve.tensor_copy(kc[:, p2, lo:], c["ek"][:, 0, 1, bass.ds(g * ET - 1 + lo, ET + 1 - lo)]).then_inc(kc_ready, 1)
                    need(dve, kc_ready, g + 1)
                    dve.wait_ge(keys_loaded[p2], dma_count(g, p2, 2))
                    need(dve, agg_mm, (g - 1) * ET)
                    for j in range(ET):
                        kj = keys[:, p2, j * P:(j + 1) * P]
                        dve.tensor_scalar(S[:, p2, j, :], kj, kc[:, p2, j + 1:j + 2], None, ALU.is_equal)
                        o = dve.tensor_scalar(cm[QUAD:, p2, j, :], kj[QUAD:, :], kc[QUAD:, p2, j:j + 1],
                                              c["e127"][QUAD:, :], ALU.is_equal, ALU.mult)
                    o.then_inc(S_ready, 1)
                g, mg = s - M, m - M
                if exists(g):
                    need(dve, z_mm, g + 1)
                    need(dve, z_ready, g - 1)
                    dve.tensor_tensor(zb[:, mg % 2, :, :], ps_z[:, :, :], spread(c["bg"], P, ET, W), ALU.add).then_inc(zb_ready, 1)

            run_steps(dve, step, EG + O, LO, HI, UN)

        @block.scalar
        def _(act):
            def step(s, m):
                def hand_on(j):
                    g = s - A
                    if exists(g):
                        need(act, agg_mm, g * ET + j + 1)
                        nc.scalar.copy(carry[QUAD:, j, :], ps_a[QUAD:, j, :]).then_inc(carry_ready, 1)

                g, mg = s - B, m - B
                if exists(g):
                    act.wait_ge(s_loaded[mg % 2], dma_count(g, mg % 2, 2, 16 * ET))
                    need(act, agg_mm, (g - 1) * ET)
                    for j in range(ET):
                        row = srow[:, mg % 2, j, :]
                        o = nc.scalar.activation(hs[:, mg % 2, j, :], row[:, 0:W], ACT.Relu,
                                                 bias=row[:, W + 3:W + 4], scale=row[:, W + 2:W + 3])
                    o.then_inc(hs_ready, 1)
                hand_on(0)
                g, mg = s - A, m - A
                if exists(g):
                    act.wait_ge(d_loaded[mg % 8], dma_count(g, mg % 8, 8, 16 * ET))
                    need(act, hd_turned, g - 1)
                    need(act, sums_ready, g - 1)
                    for j in range(ET):
                        row = drow[:, mg % 8, j, :]
                        o = nc.scalar.activation(hd[:, mg % 2, j, :], row[:, 0:W], ACT.Relu,
                                                 bias=row[:, W + 1:W + 2], scale=row[:, W:W + 1])
                    o.then_inc(hd_ready, 1)
                hand_on(1)
                g, p2 = s - Q, (m - Q) % 2
                if exists(g):
                    need(act, zb_ready, g + 1)
                    need(act, o_ready, g - 1)
                    nc.scalar.activation(z[:, p2, :, :], zb[:, p2, :, :], ACT.Relu).then_inc(z_ready, 1)
                hand_on(2)
                if exists(g):
                    need(act, z_ready, g + 1)
                    need(act, ss_ready, g)
                    for j in range(ET):
                        o = nc.scalar.activation(zsq[:, j, :], z[:, p2, j, :], ACT.Square, accum_out=ss[:, p2, j:j + 1])
                    o.then_inc(ss_ready, 1)
                hand_on(3)
                if exists(g):
                    need(act, ss_ready, g + 1)
                    need(act, inv_ready, g - 1)
                    nc.scalar.activation(nrm[:, p2, :], ss[:, p2, :], ACT.Sqrt).then_inc(nrm_ready, 1)

            run_steps(act, step, EG + Q, LO, HI, UN)

        @block.tensor
        def _(pe):
            def step(s, m):
                for j in range(ET):
                    g, mg = s - M, m - M
                    if exists(g):
                        if j == 0:
                            need(pe, both_ready, g + 1)
                            need(pe, zb_ready, g)
                        for kind, w in ((0, c["wg"]), (1, c["wv"])):
                            for i in range(2):
                                o = pe.matmul(ps_z[:, j, :], both[:, mg % 2, kind, j, i, :], w[:, i, :],
                                              start=kind == 0 and i == 0, stop=kind == 1 and i == 1)
                        if j == ET - 1:
                            o.then_inc(z_mm, 1)
                    g, mg = s - A, m - A
                    if exists(g):
                        p2 = mg % 2
                        if j == 0:
                            need(pe, S_ready, g + 1)
                            need(pe, hs_ready, g + 1)
                            need(pe, sums_ready, g)
                        first = isinstance(g, int) and g == 0 and j == 0
                        need(pe, carry_ready, g * ET + j)
                        o = pe.matmul(ps_a[:, j, :], S[:, p2, j, :], hs[:, p2, j, :], start=True, stop=first)
                        if not first:
                            o = pe.matmul(ps_a[:, j, :], cm[QUAD:, p2, j, :], carry[QUAD:, (j - 1) % ET, :],
                                          start=False, stop=True)
                        o.then_inc(agg_mm, 1)
                g, mg = s - C, m - C
                if exists(g):
                    for kind, tile, ready, turned in ((1, hd, hd_ready, hd_turned), (0, sums, own_ready, sums_turned)):
                        need(pe, ready, g + 1)
                        need(pe, both_ready, g)
                        for j in range(ET):
                            for i in range(2):
                                o = pe.transpose(ps_t[:, kind, j, i, :], tile[:, mg % 2, j, i * P:(i + 1) * P],
                                                 c["ident"][:, :])
                        o.then_inc(turned, 1)

            run_steps(pe, step, EG + M, LO, HI, UN)


_INS = ['x', 'src', 'dst', 'L0_gnn_W_P_w', 'L0_gnn_W_P_b', 'L0_gnn_W_pos', 'L0_gnn_q1', 'L0_gnn_k1', 'L0_gnn_v1',
        'L0_gnn_ln1_s', 'L0_gnn_ln1_b', 'L0_gnn_q2', 'L0_gnn_k2', 'L0_gnn_v2', 'L0_gnn_ln2_s', 'L0_gnn_ln2_b',
        'L0_gnn_inv_w', 'L0_gnn_inv_b', 'L1_gnn_W_gcn', 'L1_gnn_b_gcn', 'L1_gnn_W_V']
_OUTS = [((50000, 256), 'float32')]


def kernel(**inputs):
    import numpy as _np
    import concourse.bacc as _bacc
    from concourse import mybir as _mybir
    from concourse.bass_utils import run_bass_kernel_spmd as _run

    nc = _bacc.Bacc("TRN2", target_bir_lowering=False, num_devices=1)
    arrays, args = {}, []
    for name in _INS:
        a = _np.ascontiguousarray(inputs[name])
        arrays[f"in_{name}_dram"] = a
        args.append(nc.dram_tensor(f"in_{name}_dram", a.shape, _mybir.dt.from_np(a.dtype), kind="ExternalInput").ap())
    for i, (shape, dtype) in enumerate(_OUTS):
        dt = _mybir.dt.from_np(_np.dtype(dtype))
        args.append(nc.dram_tensor(f"out_{i}_dram", shape, dt, kind="ExternalOutput").ap())
    program(nc, *args)
    r = _run(nc, [arrays], core_ids=[0])
    got = tuple(r.results[0][f"out_{i}_dram"] for i in range(len(_OUTS)))
    return got[0]
```
